# Optimizing a Trainium2 kernel written in Bass

```python
import numpy as np
import jax
import jax.numpy as jnp

def _softmax(x, axis=-1):
    return jax.nn.softmax(x, axis=axis)

def _gelu(x):
    return jax.nn.gelu(x, approximate=True)

def _silu(x):
    return jax.nn.silu(x)

def _sigmoid(x):
    return jax.nn.sigmoid(x)

def _layernorm(x, axis=-1, eps=1e-05):
    m = jnp.mean(x, axis=axis, keepdims=True)
    v = jnp.var(x, axis=axis, keepdims=True)
    return (x - m) / jnp.sqrt(v + eps)

def _scatter_add(tgt, idx, src, axis=0):
    return tgt.at[idx].add(src)

def _segment_sum(src, seg, n):
    return jax.ops.segment_sum(src, seg, n)
kernel_name = 'mk_gnn_ffn_d1_gnn_r8_d9da6f'

def setup_inputs(seed: int=0):
    np.random.seed(seed)
    _w = jnp.asarray

    def _rec_inputs():
        import jax
        import jax.numpy as jnp
        _gk = jax.random.key(seed)
        x = -0.0003713 + 1 * jax.random.normal(jax.random.fold_in(_gk, 1), (6250, 256), jnp.float32)
        src = jax.random.randint(jax.random.fold_in(_gk, 2), (200000,), 0, 6250, jnp.int32)
        dst = jnp.minimum((6250 * jax.random.uniform(jax.random.fold_in(_gk, 3), (200000,)) ** 2.0).astype(jnp.int32), 49999)
        _o = jnp.argsort(dst, stable=True)
        src = src[_o]
        dst = dst[_o]
        return (x, src, dst)
    x, src, dst = _rec_inputs()

    def _L0_gnn_setup():
        import jax, jax.numpy as jnp
        import numpy as np
        N = 6250
        M = 100000
        H = 8
        DK = 32
        DV = 32
        DE = 256
        INV_SQRT_DK = float(1.0 / np.sqrt(DK))
        key = jax.random.key(seed)
        k0, k1, k2, k3 = jax.random.split(key, 4)
        x = jax.random.normal(k0, (N, DE), dtype=jnp.float32)
        edge_index = jax.random.randint(k1, (2, M), 0, N, dtype=jnp.int64)
        qkv_out = (2 * DK + DV) * H
        W_qkv = jax.random.normal(k2, (qkv_out, DE), dtype=jnp.float32) / np.sqrt(DE).astype(np.float32)
        b_qkv = jnp.zeros((qkv_out,), dtype=jnp.float32)
        W_ff = jax.random.normal(k3, (DE, DV * H), dtype=jnp.float32) / np.sqrt(DV * H).astype(np.float32)
        b_ff = jnp.zeros((DE,), dtype=jnp.float32)
        return {'x': x, 'edge_index': edge_index, 'W_qkv': W_qkv, 'b_qkv': b_qkv, 'W_ff': W_ff, 'b_ff': b_ff}
    _L0_gnn_all = _L0_gnn_setup()
    _L0_gnn_in = {k: v for k, v in _L0_gnn_all.items() if k in ('W_qkv', 'b_qkv', 'W_ff', 'b_ff')}
    del _L0_gnn_all

    def _L0_ffn_setup():
        import jax, jax.numpy as jnp
        import numpy as np
        E = 8
        K = 2
        D = 256
        H = 512
        DOUT = 256
        EPS = 1e-05
        key = jax.random.key(seed)
        ks = jax.random.split(key, 9)
        s = 0.02
        return {'x': jax.random.normal(ks[0], (4, 1024, D), jnp.float32), 'gamma': 1.0 + 0.05 * jax.random.normal(ks[1], (D,), jnp.float32), 'beta': 0.05 * jax.random.normal(ks[2], (D,), jnp.float32), 'Wr': 0.01 * jax.random.normal(ks[3], (D, E), jnp.float32), 'br': jnp.zeros((E,), jnp.float32), 'W1': s * jax.random.normal(ks[4], (E, D, H), jnp.float32), 'b1': s * jax.random.normal(ks[5], (E, H), jnp.float32), 'W2': s * jax.random.normal(ks[6], (E, H, DOUT), jnp.float32), 'b2': s * jax.random.normal(ks[7], (E, DOUT), jnp.float32)}
    _L0_ffn_all = _L0_ffn_setup()
    _L0_ffn_in = {k: v for k, v in _L0_ffn_all.items() if k in ('gamma', 'beta', 'Wr', 'br', 'W1', 'b1', 'W2', 'b2')}
    del _L0_ffn_all
    return {'x': x, 'src': src, 'dst': dst, 'L0_gnn_W_qkv': _L0_gnn_in['W_qkv'], 'L0_gnn_b_qkv': _L0_gnn_in['b_qkv'], 'L0_gnn_W_ff': _L0_gnn_in['W_ff'], 'L0_gnn_b_ff': _L0_gnn_in['b_ff'], 'L0_ffn_gamma': _L0_ffn_in['gamma'], 'L0_ffn_beta': _L0_ffn_in['beta'], 'L0_ffn_Wr': _L0_ffn_in['Wr'], 'L0_ffn_br': _L0_ffn_in['br'], 'L0_ffn_W1': _L0_ffn_in['W1'], 'L0_ffn_b1': _L0_ffn_in['b1'], 'L0_ffn_W2': _L0_ffn_in['W2'], 'L0_ffn_b2': _L0_ffn_in['b2']}

def reference(x, src, dst, L0_gnn_W_qkv, L0_gnn_b_qkv, L0_gnn_W_ff, L0_gnn_b_ff, L0_ffn_gamma, L0_ffn_beta, L0_ffn_Wr, L0_ffn_br, L0_ffn_W1, L0_ffn_b1, L0_ffn_W2, L0_ffn_b2):
    import jax
    import jax.numpy as jnp

    def _L0_gnn_ref(x, edge_index, W_qkv, b_qkv, W_ff, b_ff):
        import jax, jax.numpy as jnp
        import numpy as np
        N = 6250
        M = 100000
        H = 8
        DK = 32
        DV = 32
        DE = 256
        INV_SQRT_DK = float(1.0 / np.sqrt(DK))
        senders, receivers = (edge_index[0], edge_index[1])
        qkv = x @ W_qkv.T + b_qkv
        Q = qkv[:, :DK * H].reshape(N, H, DK)
        K = qkv[:, DK * H:2 * DK * H].reshape(N, H, DK)
        V = qkv[:, 2 * DK * H:].reshape(N, H, DV)
        att = jnp.einsum('mhd,mhd->mh', Q[receivers], K[senders]) * INV_SQRT_DK
        seg_max = jax.ops.segment_max(att, receivers, num_segments=N)
        e = jnp.exp(att - jax.lax.stop_gradient(seg_max)[receivers])
        denom = jax.ops.segment_sum(e, receivers, num_segments=N)[receivers]
        attention = jnp.where(denom > 0, e / denom, jnp.zeros_like(e))
        out = jax.ops.segment_sum(attention[:, :, None] * V[senders], receivers, num_segments=N)
        return out.reshape(N, H * DV) @ W_ff.T + b_ff

    def _L0_ffn_ref(x, gamma, beta, Wr, br, W1, b1, W2, b2):
        import jax, jax.numpy as jnp
        import numpy as np
        E = 8
        K = 2
        D = 256
        H = 512
        DOUT = 256
        EPS = 1e-05
        mu = jnp.mean(x, axis=-1, keepdims=True)
        var = jnp.mean(jnp.square(x - mu), axis=-1, keepdims=True)
        xn = (x - mu) * jax.lax.rsqrt(var + EPS) * gamma + beta
        logits = jnp.einsum('bsd,de->bse', xn, Wr) + br
        top_vals, top_idx = jax.lax.top_k(logits, K)
        w = jax.nn.softmax(top_vals, axis=-1)
        w_full = jnp.einsum('bsk,bske->bse', w, jax.nn.one_hot(top_idx, E, dtype=w.dtype))
        y = jnp.zeros(x.shape[:-1] + (DOUT,), x.dtype)
        for e in range(E):
            h = jax.nn.gelu(jnp.einsum('bsd,dh->bsh', xn, W1[e]) + b1[e], approximate=False)
            y_e = jnp.einsum('bsh,hd->bsd', h, W2[e]) + b2[e]
            y = y + y_e * w_full[..., e, None]
        return y
    edge_index = jnp.stack([src, dst])
    x = x + _L0_gnn_ref(_layernorm(x, axis=-1), edge_index, L0_gnn_W_qkv, L0_gnn_b_qkv, L0_gnn_W_ff, L0_gnn_b_ff)
    x = x + _L0_ffn_ref(_layernorm(x, axis=-1)[None], L0_ffn_gamma, L0_ffn_beta, L0_ffn_Wr, L0_ffn_br, L0_ffn_W1, L0_ffn_b1, L0_ffn_W2, L0_ffn_b2)[0]
    return x

_drawn_inputs = setup_inputs


def setup_inputs(seed=0):
    import zlib

    import numpy as np

    out = dict(_drawn_inputs(seed))
    spreads = {'L0_gnn_b_qkv': (0.0, 0.1), 'L0_gnn_b_ff': (0.0, 0.1), 'L0_ffn_br': (0.0, 0.1)}
    factors = {'L0_ffn_gamma': 6.267, 'L0_ffn_beta': 5.122, 'L0_ffn_b1': 8.0, 'L0_ffn_b2': 4.454}
    for name, (base, spread) in spreads.items():
        noise = np.random.default_rng([zlib.crc32(name.encode()), seed]).standard_normal(out[name].shape)
        drawn = base * np.exp(spread * noise) if base else spread * noise
        out[name] = jnp.asarray(drawn.astype(out[name].dtype))
    for name, factor in factors.items():
        out[name] = (out[name] * factor).astype(out[name].dtype)
    return out
```

```python
from contextlib import ExitStack

import concourse.bass as bass
from concourse import mybir

ALU = mybir.AluOpType
ACT = mybir.ActivationFunctionType
F32 = mybir.dt.float32
BF16 = mybir.dt.bfloat16
I32 = mybir.dt.int32
X = mybir.AxisListType.X

P = 128
NODES = 6250
EDGES = 200000
D = 256
HEADS = 8
DH = D // HEADS
KC = D // P
BLOCKS = -(-NODES // P)
ROWS = BLOCKS * P
TILES = -(-EDGES // P)
PAD_TILE = TILES
GV = 4
GROUPS = -(-((TILES + BLOCKS - 1 + BLOCKS * (GV - 1)) // GV) // 4) * 4
VISITS = GROUPS * GV
VC = -(-(VISITS + 8) // P)
VPAD = VC * P
UNROLL = 4
BIG = 1.0e30
SB = 7
ST = BLOCKS // SB
EXPERTS = 8
HID = 512
HC = HID // P
EPS = 1e-5
SCALE = float(DH) ** -0.5
assert GROUPS % UNROLL == 0 and ST * SB == BLOCKS


class Core:

    def __init__(self, nc, stack):
        self.nc = nc
        self.stack = stack

    def sem(self, name):
        return self.stack.enter_context(self.nc.semaphore(name))


def wait_here(eng, core):
    eng.sem_inc(core.waited, 1)


def tensors(nc, stack):
    def sb(name, shape, dt):
        return stack.enter_context(nc.sbuf_tensor(name, shape, dt))

    def ps(name, shape, dt):
        return stack.enter_context(nc.psum_tensor(name, shape, dt))
    return sb, ps


def phase_constants(nc, core, d):
    with ExitStack() as st:
        sb, ps = tensors(nc, st)
        diag = sb("diag", [P, P], I32)
        iota_i = sb("iota_i", [P, P], I32)
        wq_rows = sb("wq_rows", [P, 3 * KC, D], F32)
        wf_rows = sb("wf_rows", [P, KC, D], F32)
        tp = ps("tp_w", [P, 4, 512], F32)
        iota_done, ident_done = core.sem("c_iota"), core.sem("c_ident")
        w_in, tp_done, tp_used, small_in = (core.sem(n) for n in ("c_w_in", "c_tp", "c_tp_used", "c_small"))
        with nc.Block() as block:
            @block.gpsimd
            def _(pool):
                pool.iota(diag[:, :], pattern=[[1, P]], base=0, channel_multiplier=-1).then_inc(iota_done, 1)
                pool.iota(iota_i[:, :], pattern=[[1, P]], base=0, channel_multiplier=0).then_inc(iota_done, 1)

            @block.sync
            def _(sp):
                sp.dma_start(wq_rows[:, :, :], d["W_qkv"].rearrange("(c p) k -> p c k", p=P)).then_inc(w_in, 16)
                sp.dma_start(wf_rows[:, :, :], d["W_ff"].rearrange("(c p) k -> p c k", p=P)).then_inc(w_in, 16)
                sp.dma_start(core.b_qkv[:, :], d["b_qkv"].partition_broadcast(P)).then_inc(small_in, 16)
                sp.wait_ge(small_in, 16)

            @block.vector
            def _(dve):
                dve.wait_ge(iota_done, 2)
                dve.tensor_scalar(core.ident[:, :], diag[:, :], 0.0, None, ALU.is_equal)
                dve.tensor_scalar(core.ident_bf[:, :], diag[:, :], 0.0, None, ALU.is_equal)
                dve.tensor_copy(core.iota_bf[:, :], iota_i[:, :])
                dve.memset(core.ones[:, :], 1.0)
                dve.memset(core.eps[:, :], EPS)
                dve.memset(core.zero_bf[:, :], 0.0).then_inc(ident_done, 1)

            def weight_chunks():
                for c in range(3 * KC):
                    for k in range(KC):
                        yield wq_rows[:, c, k * P:(k + 1) * P], core.wqkvT[:, k, c * P:(c + 1) * P]
                for c in range(KC):
                    for k in range(KC):
                        yield wf_rows[:, c, k * P:(k + 1) * P], core.wffT[:, k, c * P:(c + 1) * P]

            @block.tensor
            def _(pe):
                pe.wait_ge(ident_done, 1)
                pe.wait_ge(w_in, 32)
                for n, (src, _) in enumerate(weight_chunks()):
                    if n >= 4:
                        pe.wait_ge(tp_used, n - 3)
                    pe.transpose(tp[:, n % 4, 0:P], src, core.ident[:, :]).then_inc(tp_done, 1)

            @block.scalar
            def _(act):
                for n, (_, dst) in enumerate(weight_chunks()):
                    act.wait_ge(tp_done, n + 1)
                    act.copy(dst, tp[:, n % 4, 0:P]).then_inc(tp_used, 1)


def phase_project(nc, core, d):
    with ExitStack() as st:
        sb, ps = tensors(nc, st)
        taken = [0]

        def carve(shape):
            size = shape[0] * shape[1] * (shape[2] if len(shape) == 3 else 1)
            flat = core.att[:, taken[0]:taken[0] + size]
            taken[0] += size
            if len(shape) == 3:
                return flat.rearrange("p (a b c) -> p a b c", a=shape[0], b=shape[1])
            return flat.rearrange("p (a b) -> p a b", a=shape[0])

        x_t = carve([SB, D])
        stats = sb("p_stats", [P, SB, 6], F32)
        mv = sb("p_mv", [P, SB, 2], F32)
        std = sb("p_std", [P, SB], F32)
        rstd = sb("p_rstd", [P, SB], F32)
        xh = carve([SB, D])
        xhT = carve([SB, KC, P])
        qkv = carve([SB, 3 * D])
        rest1 = carve([SB, D])
        rest2 = carve([SB, D])
        tp = [ps(f"p_tp{i}", [P, KC, 256], F32) for i in range(2)]
        qp = [ps(f"p_qp{i}", [P, 1024], F32) for i in range(3)]
        x_in = [core.sem(f"p_x_in{j}") for j in range(SB)]
        k_out = [core.sem(f"p_k_out{j}") for j in range(SB)]
        v_out = [core.sem(f"p_v_out{j}") for j in range(SB)]
        names = ("stats", "mv", "std", "rstd", "xh", "tp", "xhT", "qkvp", "qkv", "q1", "r1", "q2", "r2", "q3")
        s = {n: core.sem("p_s_" + n) for n in names}

        with nc.Block() as block:
            @block.sync
            def _(sp):
                with sp.Fori(0, ST) as t:
                    for j in range(SB):
                        n = t * SB + j
                        sp.wait_ge(s["xh"], t * SB)
                        sp.dma_start(x_t[:, j, :], d["x"][bass.ds(n * P, P), :]).then_inc(x_in[j], 16)
                    for j in range(SB):
                        n = t * SB + j
                        sp.wait_ge(s["qkv"], n + 1)
                        sp.dma_start(d["k_table"][bass.ds(n * P, P), :], qkv[:, j, D:2 * D]).then_inc(k_out[j], 16)
                        sp.dma_start(d["v_table"][bass.ds(n * P, P), :], qkv[:, j, 2 * D:3 * D]).then_inc(v_out[j], 16)
                for j in range(SB):
                    sp.wait_ge(k_out[j], 16 * ST)
                    sp.wait_ge(v_out[j], 16 * ST)

            @block.vector
            def _(dve):
                with dve.Fori(0, ST) as t:
                    for j in range(SB):
                        dve.wait_ge(x_in[j], 16 * (t + 1))
                        dve.bn_stats(stats[:, j, :], x_t[:, j, :]).then_inc(s["stats"], 1)
                    for j in range(SB):
                        dve.wait_ge(s["stats"], t * SB + j + 1)
                        dve.wait_ge(s["std"], t * SB)
                        wait_here(dve, core)
                        dve.bn_aggr(mv[:, j, :], stats[:, j, :]).then_inc(s["mv"], 1)
                    for j in range(SB):
                        dve.wait_ge(s["std"], t * SB + j + 1)
                        dve.reciprocal(rstd[:, j:j + 1], std[:, j:j + 1]).then_inc(s["rstd"], 1)
                    for j in range(SB):
                        dve.wait_ge(s["rstd"], t * SB + j + 1)
                        dve.wait_ge(s["tp"], t * SB)
                        dve.tensor_scalar(xh[:, j, :], x_t[:, j, :], mv[:, j, 0:1], rstd[:, j:j + 1],
                                          ALU.subtract, ALU.mult).then_inc(s["xh"], 1)
                    for j in range(SB):
                        n = t * SB + j
                        dve.wait_ge(s["qkvp"], n + 1)
                        dve.wait_ge(s["r1"], t * SB)
                        dve.wait_ge(s["q1"], t * SB)
                        dve.wait_ge(k_out[j], 16 * t)
                        dve.wait_ge(v_out[j], 16 * t)
                        dve.tensor_tensor(qkv[:, j, :], qp[j % 3][:, 0:3 * D], core.b_qkv[:, :],
                                          ALU.add).then_inc(s["qkv"], 1)

            @block.scalar
            def _(act):
                with act.Fori(0, ST) as t:
                    for j in range(SB):
                        act.wait_ge(s["mv"], t * SB + j + 1)
                        act.wait_ge(s["rstd"], t * SB)
                        act.activation(std[:, j:j + 1], mv[:, j, 1:2], ACT.Sqrt,
                                       bias=core.eps[:, :]).then_inc(s["std"], 1)
                    for j in range(SB):
                        act.wait_ge(s["tp"], t * SB + j + 1)
                        act.wait_ge(s["qkvp"], t * SB)
                        act.copy(xhT[:, j, :, :], tp[j % 2][:, :, 0:P]).then_inc(s["xhT"], 1)
                    for part, src, need in ((0, None, "qkv"), (1, rest1, "r1"), (2, rest2, "r2")):
                        for j in range(SB):
                            n = t * SB + j
                            act.wait_ge(s[need], n + 1)
                            source = qkv[:, j, 0:D] if src is None else src[:, j, :]
                            wait_here(act, core)
                            act.copy(core.q_parts[:, bass.ds((n * 3 + part) * D, D)],
                                     source).then_inc(s[("q1", "q2", "q3")[part]], 1)

            @block.gpsimd
            def _(pool):
                with pool.Fori(0, ST) as t:
                    for part in range(2):
                        for j in range(SB):
                            n = t * SB + j
                            pool.wait_ge(s[("q1", "q2")[part]], n + 1)
                            if part:
                                pool.wait_ge(s["r1"], n + 1)
                            pool.wait_ge(s[("q2", "q3")[part]], t * SB)
                            src = rest1[:, j, :] if part else qkv[:, j, 0:D]
                            dst = rest2 if part else rest1
                            pool.tensor_tensor(dst[:, j, :], src, core.q_parts[:, bass.ds((n * 3 + part) * D, D)],
                                               ALU.subtract).then_inc(s[("r1", "r2")[part]], 1)

            @block.tensor
            def _(pe):
                with pe.Fori(0, ST) as t:
                    for j in range(SB):
                        n = t * SB + j
                        pe.wait_ge(s["xh"], n + 1)
                        pe.wait_ge(s["xhT"], n if j == 0 else n - 1)
                        for k in range(KC):
                            mm = pe.transpose(tp[j % 2][:, k, 0:P], xh[:, j, k * P:(k + 1) * P], core.ident[:, :])
                        mm.then_inc(s["tp"], 1)
                    for j in range(SB):
                        n = t * SB + j
                        pe.wait_ge(s["xhT"], n + 1)
                        pe.wait_ge(s["qkv"], n if j == 0 else (n - 1 if j == 1 else n - 2))
                        for lo, hi in ((0, 512), (512, 768)):
                            for k in range(KC):
                                mm = pe.matmul(qp[j % 3][:, lo:hi], xhT[:, j, k, :], core.wqkvT[:, k, lo:hi],
                                               start=(k == 0), stop=(k == KC - 1))
                        mm.then_inc(s["qkvp"], 1)


def phase_route(nc, core, d):
    NB1 = BLOCKS + 1
    full = TILES // P * P // P
    left = TILES - full * P
    with ExitStack() as st:
        sb, ps = tensors(nc, st)
        first = sb("r_first", [P, full + 1], I32)
        firstf = sb("r_firstf", [P, full + 1], F32)
        bound_i = sb("r_bound_i", [P, NB1], I32)
        bound = sb("r_bound", [P, NB1], F32)
        visit_i = sb("r_visit_i", [P, VC], I32)
        visit = sb("r_visit", [P, VC], F32)
        below = sb("r_below", [P, NB1, full + 1], F32)
        cnt = sb("r_cnt", [P, NB1], F32)
        T = sb("r_T", [P, NB1], F32)
        size = sb("r_size", [P, BLOCKS], F32)
        size_i = sb("r_size_i", [P, BLOCKS], I32)
        size_q = sb("r_size_q", [P, BLOCKS], I32)
        one = sb("r_one", [P, BLOCKS], F32)
        gend = sb("r_gend", [P, BLOCKS], F32)
        v0 = sb("r_v0", [P, BLOCKS], F32)
        rel = sb("r_rel", [P, BLOCKS], F32)
        steps = sb("r_steps", [P, 3, BLOCKS], F32)
        ge = sb("r_ge", [P, VC, BLOCKS], F32)
        tmp = sb("r_tmp", [P, VC, BLOCKS], F32)
        vb = sb("r_vb", [P, VC], F32)
        vt = sb("r_vt", [P, VC], F32)
        vend = sb("r_vend", [P, VC], F32)
        ok = sb("r_ok", [P, VC], F32)
        tile_i = sb("r_tile_i", [P, VC], I32)
        rows = sb("r_rows", [P, VC, 2 * P], I32)
        src_f = sb("r_src_f", [P, VC, P], F32)
        loc_f = sb("r_loc_f", [P, VC, P], F32)
        psum_cnt = ps("r_cnt_ps", [P, 512], F32)
        tp = [ps(f"r_tp{i}", [P, 4, P], F32) for i in range(2)]
        iotas, first_in, step, cnt_ps, tile_ready = (core.sem("r_" + n) for n in
                                                     ("iotas", "first_in", "step", "cnt_ps", "tile_ready"))
        rows_in, tp_done, tp_used, split = (core.sem("r_" + n) for n in ("rows_in", "tp_done", "tp_used", "split"))
        padded = core.sem("r_padded")
        with nc.Block() as block:
            @block.gpsimd
            def _(pool):
                pool.memset(first[:, :], 1 << 20).then_inc(padded, 1)
                pool.iota(bound_i[:, :], pattern=[[P, NB1]], base=0, channel_multiplier=0).then_inc(iotas, 1)
                pool.iota(visit_i[:, :], pattern=[[P, VC]], base=0, channel_multiplier=1).then_inc(iotas, 1)
                last_row = pool.to_reg(PAD_TILE)
                pool.wait_ge(tile_ready, 1)
                for c in range(VC):
                    pool.indirect_dma_start(rows[:, c, :], None, d["edges"],
                                            bass.IndirectOffsetOnAxis(ap=tile_i[:, c:c + 1], axis=0),
                                            bounds_check=last_row, oob_is_err=False).then_inc(rows_in, 16)

            @block.sync
            def _(sp):
                dst_first = d["edges"][:, P:P + 1]
                sp.wait_ge(padded, 1)
                sp.dma_start(first[:, 0:full].unsqueeze(2),
                             dst_first[0:full * P, :].rearrange("(p c) o -> p c o", c=full),
                             allow_slow_non_contiguous=True).then_inc(first_in, 16)
                sp.dma_start(first[0:left, full:full + 1], dst_first[full * P:TILES, :],
                             allow_slow_non_contiguous=True).then_inc(first_in, 16)
                sp.wait_ge(first_in, 32)

            @block.tensor
            def _(pe):
                pe.wait_ge(step, 1)
                pe.matmul(psum_cnt[:, 0:NB1], core.ones[:, :], cnt[:, :], start=True, stop=True).then_inc(cnt_ps, 1)
                for c in range(VC):
                    pe.wait_ge(split, c + 1)
                    if c >= 2:
                        pe.wait_ge(tp_used, 2 * (c - 1))
                    pe.transpose(tp[c % 2][:, 0, :], src_f[:, c, :], core.ident[:, :])
                    pe.transpose(tp[c % 2][:, 1, :], loc_f[:, c, :], core.ident[:, :]).then_inc(tp_done, 1)

            @block.scalar
            def _(act):
                for c in range(VC):
                    act.wait_ge(tp_done, c + 1)
                    act.copy(core.srcT[:, c * P:(c + 1) * P], tp[c % 2][:, 0, :]).then_inc(tp_used, 1)
                    act.copy(core.dstT[:, c * P:(c + 1) * P], tp[c % 2][:, 1, :]).then_inc(tp_used, 1)

            @block.vector
            def _(dve):
                done = [0]
                chain = core.sem("r_chain")

                def then(ins):
                    done[0] += 1
                    ins.then_inc(chain, 1)
                    dve.wait_ge(chain, done[0])

                dve.wait_ge(iotas, 2)
                dve.wait_ge(first_in, 32)
                dve.tensor_copy(bound[:, :], bound_i[:, :])
                dve.tensor_copy(visit[:, :], visit_i[:, :])
                dve.memset(one[:, :], 1.0)
                then(dve.tensor_copy(firstf[:, :], first[:, :]))
                then(dve.tensor_tensor(below[:, :, :], firstf[:, :].unsqueeze(1).to_broadcast([P, NB1, full + 1]),
                                       bound[:, :].unsqueeze(2).to_broadcast([P, NB1, full + 1]), ALU.is_lt))
                dve.tensor_reduce(cnt[:, :], below[:, :, :], X, ALU.add).then_inc(step, 1)
                dve.wait_ge(cnt_ps, 1)
                then(dve.tensor_scalar(T[:, :], psum_cnt[:, 0:NB1], -1.0, 0.0, ALU.add, ALU.max))
                then(dve.tensor_tensor(size[:, :], T[:, 1:NB1], T[:, 0:BLOCKS], ALU.subtract))
                then(dve.tensor_scalar(size_i[:, :], size[:, :], float(GV), None, ALU.add))
                then(dve.tensor_scalar(size_q[:, :], size_i[:, :], 2, None, ALU.arith_shift_right))
                then(dve.tensor_copy(size[:, :], size_q[:, :]))
                then(dve.tensor_tensor_scan(gend[:, :], one[:, :], size[:, :], 0.0, ALU.mult, ALU.add))
                dve.memset(core.bounds[:, 0:1], 0)
                dve.memset(core.bounds[:, BLOCKS:NB1], GROUPS)
                dve.tensor_copy(core.bounds[:, 1:BLOCKS], gend[:, 0:BLOCKS - 1])
                then(dve.tensor_tensor(v0[:, :], gend[:, :], size[:, :], ALU.subtract))
                then(dve.tensor_scalar(v0[:, :], v0[:, :], float(GV), None, ALU.mult))
                then(dve.tensor_tensor(rel[:, :], T[:, 0:BLOCKS], v0[:, :], ALU.subtract))
                dve.memset(steps[:, 0, 0:1], 0.0)
                dve.memset(steps[:, 0, 1:BLOCKS], 1.0)
                dve.tensor_copy(steps[:, 1, 0:1], rel[:, 0:1])
                dve.tensor_tensor(steps[:, 1, 1:BLOCKS], rel[:, 1:BLOCKS], rel[:, 0:BLOCKS - 1], ALU.subtract)
                dve.tensor_copy(steps[:, 2, 0:1], T[:, 1:2])
                dve.tensor_tensor(steps[:, 2, 1:BLOCKS], T[:, 2:NB1], T[:, 1:BLOCKS], ALU.subtract)
                then(dve.tensor_tensor(ge[:, :, :], visit[:, :].unsqueeze(2).to_broadcast([P, VC, BLOCKS]),
                                       v0[:, :].unsqueeze(1).to_broadcast([P, VC, BLOCKS]), ALU.is_ge))
                for n, out in enumerate((vb, vt, vend)):
                    then(dve.tensor_tensor(tmp[:, :, :], ge[:, :, :],
                                           steps[:, n, :].unsqueeze(1).to_broadcast([P, VC, BLOCKS]), ALU.mult))
                    then(dve.tensor_reduce(out[:, :], tmp[:, :, :], X, ALU.add))
                then(dve.tensor_tensor(vt[:, :], vt[:, :], visit[:, :], ALU.add))
                then(dve.tensor_tensor(ok[:, :], vt[:, :], vend[:, :], ALU.is_le))
                then(dve.tensor_scalar(vt[:, :], vt[:, :], -float(PAD_TILE), None, ALU.add))
                then(dve.tensor_tensor(vt[:, :], vt[:, :], ok[:, :], ALU.mult))
                dve.tensor_scalar(vb[:, :], vb[:, :], float(P), None, ALU.mult)
                dve.tensor_scalar(tile_i[:, :], vt[:, :], float(PAD_TILE), None, ALU.add).then_inc(tile_ready, 1)
                dve.wait_ge(tile_ready, 1)
                dve.wait_ge(rows_in, 16 * VC)
                dve.tensor_copy(src_f[:, :, :], rows[:, :, 0:P])
                then(dve.tensor_copy(core.dstV[:, :, :], rows[:, :, P:2 * P]))
                for c in range(VC):
                    dve.tensor_scalar(loc_f[:, c, :], core.dstV[:, c, :], vb[:, c:c + 1], None,
                                      ALU.subtract).then_inc(split, 1)


def issue_gathers(pool, core, table, stage, ring, ring_in, ring_used, staged):
    last_row = pool.to_reg(ROWS - 1)
    with pool.Fori(0, GROUPS // UNROLL) as i:
        for q in range(UNROLL):
            g = i * UNROLL + q
            for u in range(q * GV, (q + 1) * GV):
                pool.wait_ge(ring_in[u], 16 * i)
            pool.tensor_copy(stage[:, q, :], core.srcT[:, bass.ds(g * GV, GV)]).then_inc(staged, 1)
            pool.wait_ge(ring_used, 2 * g + 2)
            pool.wait_ge(staged, g + 1)
            wait_here(pool, core)
            for u in range(GV):
                slot = q * GV + u
                pool.indirect_dma_start(ring[:, slot, :], None, table,
                                        bass.IndirectOffsetOnAxis(ap=stage[:, q, u:u + 1], axis=0),
                                        bounds_check=last_row, oob_is_err=False).then_inc(ring_in[slot], 16)


def phase_scores(nc, core, d):
    with ExitStack() as st:
        sb, ps = tensors(nc, st)
        stage = sb("s_stage", [P, UNROLL, GV], I32)
        k_ring = sb("s_k_ring", [P, UNROLL * GV, D], F32)
        onehot = sb("s_onehot", [P, 2, 2, P], BF16)
        onehotT = sb("s_onehotT", [P, 2, 2, P], BF16)
        prod = sb("s_prod", [P, 2, 2 * D], F32)
        tp = [ps(f"s_tp{i}", [P, 8, P], BF16) for i in range(2)]
        q_edge = [ps(f"s_q_edge{i}", [P, 2 * D], F32) for i in range(2)]
        k_in = [core.sem(f"s_k_in{i}") for i in range(UNROLL * GV)]
        staged, onehot_done, tp_done, onehotT_done, q_edge_done, prod_done, att_done = (
            core.sem("s_" + n) for n in ("staged", "onehot", "tp", "onehotT", "q_edge", "prod", "att"))
        RING, PAIR = 2 * UNROLL, 2

        with nc.Block() as block:
            @block.gpsimd
            def _(pool):
                issue_gathers(pool, core, d["k_table"], stage, k_ring, k_in, prod_done, staged)

            @block.vector
            def _(dve):
                dve.sem_inc(prod_done, RING)
                dve.memset(core.att[:, VISITS * HEADS:], 0.0)

                def one_hot(v, h):
                    for u in range(2):
                        ins = dve.tensor_scalar(onehot[:, h, u, :], core.iota_bf[:, :],
                                                core.dstT[:, bass.ds(v + u, 1)], None, ALU.is_equal)
                    ins.then_inc(onehot_done, 1)

                def reduce(s, h):
                    dve.wait_ge(prod_done, s + RING)
                    dve.tensor_reduce(core.att[:, bass.ds((s - 1) * 2 * HEADS, 2 * HEADS)],
                                      prod[:, 1 - h, :].rearrange("p (g k) -> p g k", k=DH), X,
                                      ALU.add).then_inc(att_done, 1)

                def product(i, s, h, slot, first=False):
                    if not first:
                        dve.wait_ge(att_done, s - 1)
                    dve.wait_ge(k_in[slot], 16 * (i + 1))
                    dve.wait_ge(k_in[slot + 1], 16 * (i + 1))
                    dve.wait_ge(q_edge_done, s + 1 + PAIR)
                    dve.tensor_tensor(prod[:, h, :], q_edge[h][:, :],
                                      k_ring[:, slot:slot + 2, :].rearrange("p s k -> p (s k)"),
                                      ALU.mult).then_inc(prod_done, 1)

                one_hot(0, 0)
                one_hot(2, 1)
                product(0, 0, 0, 0, first=True)
                dve.wait_ge(tp_done, 1)
                one_hot(4, 0)
                product(0, 1, 1, 2, first=True)
                reduce(1, 1)
                dve.wait_ge(tp_done, 2)
                one_hot(6, 1)
                with dve.Fori(0, GROUPS // UNROLL - 1) as i:
                    for k in range(2 * UNROLL):
                        s = i * 2 * UNROLL + k + 2
                        late = k + 2 >= 2 * UNROLL
                        product(i + 1 if late else i, s, k % 2, (k + 2) % (2 * UNROLL) * 2)
                        reduce(s, k % 2)
                        dve.wait_ge(tp_done, s + 1)
                        one_hot((s + 2) * 2, k % 2)
                last = GROUPS // UNROLL - 1
                for k in range(2 * UNROLL - 2):
                    s = last * 2 * UNROLL + k + 2
                    product(last, s, k % 2, (k + 2) * 2)
                    reduce(s, k % 2)
                    if s + 2 < 2 * GROUPS:
                        dve.wait_ge(tp_done, s + 1)
                        one_hot((s + 2) * 2, k % 2)
                reduce(2 * GROUPS, 0)

            @block.tensor
            def _(pe):
                with pe.Fori(0, BLOCKS) as b:
                    lo = pe.value_load(core.bounds[0:1, bass.ds(b, 1)], min_val=0, max_val=GROUPS - 1)
                    hi = pe.value_load(core.bounds[0:1, bass.ds(b + 1, 1)], min_val=1, max_val=GROUPS)
                    with pe.Fori(lo, hi) as g:
                        for h in range(2):
                            s = g * 2 + h
                            pe.wait_ge(onehot_done, s + 1)
                            pe.wait_ge(onehotT_done, s + 1)
                            for u in range(2):
                                mm = pe.transpose(tp[h][:, u, :], onehot[:, h, u, :], core.ident_bf[:, :])
                            mm.then_inc(tp_done, 1)
                        for h in range(2):
                            s = g * 2 + h
                            pe.wait_ge(onehotT_done, s + 1 + PAIR)
                            pe.wait_ge(prod_done, s + 1 + RING - 2)
                            for u in range(2):
                                for part in range(3):
                                    mm = pe.matmul(q_edge[h][:, u * D:(u + 1) * D], onehotT[:, h, u, :],
                                                   core.q_parts[:, bass.ds((b * 3 + part) * D, D)],
                                                   start=(part == 0), stop=(part == 2))
                            mm.then_inc(q_edge_done, 1)

            @block.scalar
            def _(act):
                act.sem_inc(onehotT_done, PAIR)
                act.sem_inc(q_edge_done, PAIR)
                with act.Fori(0, GROUPS) as g:
                    for h in range(2):
                        s = g * 2 + h
                        act.wait_ge(tp_done, s + 1)
                        act.wait_ge(q_edge_done, s + 1)
                        act.copy(onehotT[:, h, :, :], tp[h][:, 0:2, :]).then_inc(onehotT_done, 1)


def phase_softmax(nc, core, d):
    HH = HEADS // 2
    items = [(hh, c) for hh in range(2) for c in range(VC)]
    with ExitStack() as st:
        sb, _ = tensors(nc, st)
        attT = core.attT
        pen = sb("m_pen", [P, VPAD + 1], F32)
        fwd = core.fwd
        ends = sb("m_ends", [P, VC, 4, HEADS], F32)
        row = sb("m_row", [HEADS, 4, VPAD], F32)
        cont = sb("m_cont", [HEADS, VPAD + 1], F32)
        segmax = core.att[:, :].rearrange("p (h c e) -> p h c e", h=HEADS, c=VC)
        p_out = core.att[:, :].rearrange("p (v h) -> p v h", h=HEADS)
        scan_done = core.sem("m_scan")
        scans = [0]

        def in_visit_scans(dve, h, source):
            dve.tensor_tensor_scan(fwd[:, h % 2, :], pen[:, 0:VPAD], source, -BIG, ALU.add,
                                   ALU.max).then_inc(scan_done, 1)
            dve.wait_ge(scan_done, scans[0] + 1)
            scans[0] += 2
            return dve.tensor_tensor_scan(
                segmax[:, h, :, :].rearrange("p c e -> p (c e)")[:, ::-1], pen[:, 1:VPAD + 1][:, ::-1],
                fwd[:, h % 2, :][:, ::-1], -BIG, ALU.add, ALU.max).then_inc(scan_done, 1)

        def chained(dve, sem):
            done = [0]

            def then(ins):
                done[0] += 1
                ins.then_inc(sem, 1)
                dve.wait_ge(sem, done[0])
            return then

        with ExitStack() as pst:
            _, ps = tensors(nc, pst)
            tp = [ps(f"m_tp{i}", [P, HH, P], F32) for i in range(4)]
            tp_done, tp_used, chain = (core.sem("m1_" + n) for n in ("tp", "tp_used", "chain"))
            with nc.Block() as block:
                @block.tensor
                def _(pe):
                    for n, (hh, c) in enumerate(items):
                        if n >= 4:
                            pe.wait_ge(tp_used, n - 3)
                        for h in range(HH):
                            mm = pe.transpose(tp[n % 4][:, h, :],
                                              p_out[:, c * P:(c + 1) * P, hh * HH + h], core.ident[:, :])
                        mm.then_inc(tp_done, 1)

                @block.scalar
                def _(act):
                    for n, (hh, c) in enumerate(items):
                        act.wait_ge(tp_done, n + 1)
                        act.copy(attT[:, hh * HH:(hh + 1) * HH, c, :], tp[n % 4][:, :, :]).then_inc(tp_used, 1)

                @block.vector
                def _(dve):
                    then = chained(dve, chain)
                    begins = pen[:, 0:VPAD].rearrange("p (c e) -> p c e", c=VC)
                    dve.memset(begins[:, :, 0:1], -BIG)
                    dve.memset(pen[:, VPAD:], -BIG)
                    then(dve.tensor_tensor(begins[:, :, 1:P], core.dstV[:, :, 1:P], core.dstV[:, :, 0:P - 1],
                                           ALU.not_equal))
                    then(dve.tensor_scalar(begins[:, :, 1:P], begins[:, :, 1:P], -BIG, None, ALU.mult))
                    dve.wait_ge(tp_used, len(items))
                    for h in range(HEADS):
                        in_visit_scans(dve, h, attT[:, h, :, :].rearrange("p c e -> p (c e)"))
                    dve.wait_ge(scan_done, scans[0])
                    dve.tensor_copy(ends[:, :, 0, :], segmax[:, :, :, P - 1].rearrange("p h c -> p c h"))
                    dve.tensor_copy(ends[:, :, 1, :], segmax[:, :, :, 0].rearrange("p h c -> p c h"))
                    dve.tensor_copy(ends[:, :, 2, :], core.dstV[:, :, 0:1].to_broadcast([P, VC, HEADS]))
                    dve.tensor_copy(ends[:, :, 3, :], core.dstV[:, :, P - 1:P].to_broadcast([P, VC, HEADS]))

        with ExitStack() as pst:
            _, ps = tensors(nc, pst)
            row_ps = [ps(f"m_row_ps{i}", [P, 4 * 512], F32) for i in range(2)]
            row_done, row_used, chain = (core.sem("m2_" + n) for n in ("row", "row_used", "chain"))
            with nc.Block() as block:
                @block.tensor
                def _(pe):
                    for kind in range(4):
                        if kind >= 2:
                            pe.wait_ge(row_used, kind - 1)
                        for c in range(VC):
                            mm = pe.transpose(row_ps[kind % 2][0:HEADS, c * P:(c + 1) * P], ends[:, c, kind, :],
                                              core.ident[:, :])
                        mm.then_inc(row_done, 1)

                @block.scalar
                def _(act):
                    for kind in range(4):
                        act.wait_ge(row_done, kind + 1)
                        act.copy(row[:, kind, :], row_ps[kind % 2][0:HEADS, 0:VPAD]).then_inc(row_used, 1)

                @block.vector
                def _(dve):
                    then = chained(dve, chain)
                    last_max, first_max, first_dst, last_dst = (row[:, k, :] for k in range(4))
                    pen_fwd, pen_bwd = fwd[0:HEADS, 0, :], fwd[0:HEADS, 1, :]
                    dve.wait_ge(row_used, 4)
                    dve.memset(cont[:, 0:1], 1.0)
                    dve.memset(cont[:, VPAD:VPAD + 1], 1.0)
                    dve.tensor_tensor(cont[:, 1:VPAD], first_dst[:, 1:VPAD], last_dst[:, 0:VPAD - 1], ALU.not_equal)
                    then(dve.tensor_tensor(pen_bwd, first_dst, last_dst, ALU.not_equal))
                    then(dve.tensor_scalar(cont[:, :], cont[:, :], -BIG, None, ALU.mult))
                    then(dve.tensor_scalar(pen_bwd, pen_bwd, -BIG, None, ALU.mult))
                    then(dve.tensor_tensor(pen_fwd, pen_bwd, cont[:, 0:VPAD], ALU.min))
                    then(dve.tensor_tensor(pen_bwd, pen_bwd, cont[:, 1:VPAD + 1], ALU.min))
                    then(dve.tensor_tensor_scan(last_max, pen_fwd, last_max, -BIG, ALU.add, ALU.max))
                    then(dve.tensor_tensor_scan(first_max[:, ::-1], pen_bwd[:, ::-1], first_max[:, ::-1], -BIG,
                                                ALU.add, ALU.max))
                    dve.memset(row[:, 2, 0:1], -BIG)
                    dve.memset(row[:, 3, VPAD - 1:VPAD], -BIG)
                    dve.tensor_tensor(row[:, 2, 1:VPAD], last_max[:, 0:VPAD - 1], cont[:, 1:VPAD], ALU.add)
                    dve.tensor_tensor(row[:, 3, 0:VPAD - 1], first_max[:, 1:VPAD], cont[:, 1:VPAD], ALU.add)

        with ExitStack() as pst:
            _, ps = tensors(nc, pst)
            carry = ps("m_carry", [P, 2, 16, 16], F32)
            tp = [ps(f"m3_tp{i}", [P, HH, P], F32) for i in range(4)]
            carry_done, inject, diff, tp_done, tp_used = (core.sem("m3_" + n) for n in
                                                          ("carry", "inject", "diff", "tp", "tp_used"))
            with nc.Block() as block:
                @block.tensor
                def _(pe):
                    for way in range(2):
                        for c in range(VC):
                            mm = pe.transpose(carry[:, way, c, 0:HEADS], row[:, 2 + way, c * P:(c + 1) * P],
                                              core.ident[0:HEADS, 0:HEADS])
                    mm.then_inc(carry_done, 1)
                    for n, (hh, c) in enumerate(items):
                        pe.wait_ge(diff, (hh + 1) * HH)
                        if n >= 4:
                            pe.wait_ge(tp_used, n - 3)
                        for h in range(HH):
                            mm = pe.transpose(tp[n % 4][:, h, :], attT[:, hh * HH + h, c, :], core.ident[:, :])
                        mm.then_inc(tp_done, 1)

                @block.vector
                def _(dve):
                    dve.wait_ge(carry_done, 1)
                    for way, e in ((0, 0), (1, P - 1)):
                        at = segmax[:, :, :, e].rearrange("p h c -> p c h")
                        dve.tensor_tensor(at, carry[:, way, 0:VC, 0:HEADS], at, ALU.max).then_inc(inject, 1)
                    dve.wait_ge(inject, 2)
                    for h in range(HEADS):
                        in_visit_scans(dve, h, segmax[:, h, :, :].rearrange("p c e -> p (c e)"))

                before = scans[0] - 2 * HEADS

                @block.gpsimd
                def _(pool):
                    for h in range(HEADS):
                        pool.wait_ge(scan_done, before + 2 * (h + 1))
                        pool.tensor_tensor(attT[:, h, :, :], attT[:, h, :, :], segmax[:, h, :, :],
                                           ALU.subtract).then_inc(diff, 1)

                @block.scalar
                def _(act):
                    act.wait_ge(diff, HEADS)
                    for n, (hh, c) in enumerate(items):
                        act.wait_ge(tp_done, n + 1)
                        act.activation(p_out[:, c * P:(c + 1) * P, hh * HH:(hh + 1) * HH].rearrange("p v h -> p h v"),
                                       tp[n % 4][:, :, :], ACT.Exp, scale=SCALE).then_inc(tp_used, 1)


def phase_gather_values(nc, core, d):
    W = D + HEADS
    with ExitStack() as st:
        sb, ps = tensors(nc, st)
        stage = sb("v_stage", [P, UNROLL, GV], I32)
        v_ring = sb("v_ring", [P, UNROLL * GV, D], F32)
        onehot = sb("v_onehot", [P, 2, 2, P], F32)
        pv = sb("v_pv", [P, 2, 2, W], F32)
        p_ps = [ps(f"v_p{i}", [P, 512], F32) for i in range(2)]
        acc_ps = ps("v_acc", [P, 512], F32)
        v_in = [core.sem(f"v_in{i}") for i in range(UNROLL * GV)]
        staged, p_ready, p_col, pv_done, mm_done, acc_done, acc_used = (
            core.sem("v_" + n) for n in ("staged", "p_ready", "p_col", "pv", "mm", "acc", "acc_used"))
        RING, PAIR = 2 * UNROLL, 2
        with nc.Block() as block:
            @block.gpsimd
            def _(pool):
                issue_gathers(pool, core, d["v_table"], stage, v_ring, v_in, pv_done, staged)

            @block.vector
            def _(dve):
                dve.sem_inc(pv_done, RING)
                with dve.Fori(0, GROUPS // UNROLL) as i:
                    for k in range(2 * UNROLL):
                        s, h, slot = i * 2 * UNROLL + k, k % 2, 2 * k
                        dve.wait_ge(mm_done, s + 1)
                        for u in range(2):
                            dve.tensor_scalar(onehot[:, h, u, :], core.iota_bf[:, :],
                                              core.dstT[:, bass.ds(2 * s + u, 1)], None, ALU.is_equal)
                        dve.wait_ge(v_in[slot], 16 * (i + 1))
                        dve.wait_ge(v_in[slot + 1], 16 * (i + 1))
                        dve.wait_ge(p_ready, s + 1)
                        dve.tensor_tensor(
                            pv[:, h, :, 0:D].rearrange("p u (g k) -> p u g k", k=DH),
                            p_ps[h][:, 0:2 * HEADS].rearrange("p (u g) -> p u g", u=2).unsqueeze(3)
                            .to_broadcast([P, 2, HEADS, DH]),
                            v_ring[:, slot:slot + 2, :].rearrange("p u (g k) -> p u g k", k=DH),
                            ALU.mult).then_inc(pv_done, 1)

            @block.tensor
            def _(pe):
                pe.sem_inc(mm_done, PAIR)
                with pe.Fori(0, BLOCKS) as b:
                    lo = pe.value_load(core.bounds[0:1, bass.ds(b, 1)], min_val=0, max_val=GROUPS - 1)
                    hi = pe.value_load(core.bounds[0:1, bass.ds(b + 1, 1)], min_val=1, max_val=GROUPS)
                    pe.wait_ge(acc_used, b)
                    pe.matmul(acc_ps[:, 0:W], core.zero_bf[:, 0:P], core.zero_bf[:, 0:W], start=True, stop=False,
                              skip_group_check=True)
                    with pe.Fori(lo, hi) as g:
                        for h in range(2):
                            s = g * 2 + h
                            pe.wait_ge(pv_done, s + 1 + RING)
                            pe.wait_ge(p_col, s + 1)
                            for u in range(2):
                                mm = pe.matmul(acc_ps[:, 0:W], onehot[:, h, u, :], pv[:, h, u, :], start=False,
                                               stop=False, skip_group_check=True)
                            mm.then_inc(mm_done, 1)
                    pe.matmul(acc_ps[:, 0:W], core.zero_bf[:, 0:P], core.zero_bf[:, 0:W], start=False, stop=True,
                              skip_group_check=True).then_inc(acc_done, 1)

            @block.scalar
            def _(act):
                with act.Fori(0, BLOCKS) as b:
                    lo = act.value_load(core.bounds[0:1, bass.ds(b, 1)], min_val=0, max_val=GROUPS - 1)
                    hi = act.value_load(core.bounds[0:1, bass.ds(b + 1, 1)], min_val=1, max_val=GROUPS)
                    with act.Fori(lo, hi) as g:
                        for h in range(2):
                            s = g * 2 + h
                            p_now = core.att[:, bass.ds(s * 2 * HEADS, 2 * HEADS)]
                            act.wait_ge(pv_done, s + 1 + RING - PAIR)
                            wait_here(act, core)
                            act.copy(p_ps[h][:, 0:2 * HEADS], p_now).then_inc(p_ready, 1)
                            act.wait_ge(mm_done, s + 1)
                            wait_here(act, core)
                            act.copy(pv[:, h, :, D:W], p_now.rearrange("p (u g) -> p u g", u=2)).then_inc(p_col, 1)
                    act.wait_ge(acc_done, b + 1)
                    wait_here(act, core)
                    act.copy(core.acc[:, bass.ds(b * W, W)], acc_ps[:, 0:W]).then_inc(acc_used, 1)


def phase_node(nc, core, d):
    W = D + HEADS
    with ExitStack() as st:
        sb, ps = tensors(nc, st)
        inv_l = sb("n_inv_l", [P, 2, SB, HEADS], F32)
        x_t = core.tail[:, 0:SB * D].rearrange("p (j k) -> p j k", j=SB)
        ln = core.tail[:, SB * D:3 * SB * D].rearrange("p (r j k) -> p r j k", r=2, j=SB)
        o = ln[:, 1, :, :]
        oT = sb("n_oT", [P, SB, KC, P], F32)
        xnT = oT
        stats = sb("n_stats", [P, 2, SB, 6], F32)
        mv = sb("n_mv", [P, 2, SB, 2], F32)
        std = sb("n_std", [P, 2, SB], F32)
        rstd = sb("n_rstd", [P, 2, SB], F32)
        b_ff = sb("n_b_ff", [P, D], F32)
        wr = sb("n_wr", [P, KC, EXPERTS], F32)
        br = sb("n_br", [P, EXPERTS], F32)
        gamma = sb("n_gamma", [P, KC], F32)
        beta = sb("n_beta", [P, KC], F32)
        o_tp = [ps(f"n_o_tp{i}", [P, KC, 256], F32) for i in range(2)]
        yp = [ps(f"n_yp{i}", [P, 512], F32) for i in range(2)]
        z_tp = [ps(f"n_z_tp{i}", [P, KC, 256], F32) for i in range(2)]
        lp = [ps(f"n_lp{i}", [P, 512], F32) for i in range(2)]
        x_in = [core.sem(f"n_x_in{j}") for j in range(SB)]
        par_in = core.sem("n_par_in")
        names = ("lmax", "inv_l", "xb", "o", "o_tp", "oT", "yp", "y1", "stats", "mv", "std", "rstd", "ln",
                 "z_tp", "xnT", "keep", "lp", "logits")
        s = {n: core.sem("n_s_" + n) for n in names}

        def free_slot(eng, sem, n, j):
            eng.wait_ge(sem, n if j == 0 else n - 1)

        def y1_at(n):
            return core.acc[:, bass.ds(n * W, D)]

        with nc.Block() as block:
            @block.sync
            def _(sp):
                sp.dma_start(b_ff[:, :], d["b_ff"].partition_broadcast(P)).then_inc(par_in, 16)
                sp.dma_start(br[:, :], d["br"].partition_broadcast(P)).then_inc(par_in, 16)
                sp.dma_start(wr[:, :, :], d["Wr"].rearrange("(k p) e -> p k e", p=P)).then_inc(par_in, 16)
                for k in range(KC):
                    for tile, name in ((gamma, "gamma"), (beta, "beta")):
                        sp.dma_start(tile[:, k:k + 1], d[name][k * P:(k + 1) * P].rearrange("(p a) -> p a", a=1)
                                     ).then_inc(par_in, 16)
                with sp.Fori(0, ST) as t:
                    for j in range(SB):
                        sp.wait_ge(s["y1"], t * SB)
                        sp.dma_start(x_t[:, j, :], d["x"][bass.ds((t * SB + j) * P, P), :]).then_inc(x_in[j], 16)
                sp.dma_start(core.w1[:, :, :, :], d["W1"].rearrange("e (k p) h -> p e k h", p=P)
                             ).then_inc(core.w_in, 16)
                sp.dma_start(core.w2[:, :, :, :], d["W2"].rearrange("e (c p) o -> p e c o", p=P)
                             ).then_inc(core.w_in, 16)
                sp.dma_start(core.b2[:, :], d["b2"]).then_inc(core.w_in, 16)
                sp.dma_start(core.b1_rows[:, :], d["b1"].rearrange("e (c p) -> (e c) p", p=P)).then_inc(core.w_in, 16)
                sp.wait_ge(core.w_in, 64)

            @block.gpsimd
            def _(pool):
                pool.wait_ge(par_in, 16 * (3 + 2 * KC))
                with pool.Fori(0, ST) as t:
                    for j in range(SB):
                        n = t * SB + j
                        pool.wait_ge(s["inv_l"], t + 1)
                        pool.wait_ge(s["z_tp"], t * SB)
                        pool.tensor_tensor(
                            o[:, j, :].rearrange("p (h k) -> p h k", k=DH),
                            y1_at(n).rearrange("p (h k) -> p h k", k=DH),
                            inv_l[:, 1, j, :].unsqueeze(2).to_broadcast([P, HEADS, DH]), ALU.mult).then_inc(s["o"], 1)
                    for j in range(SB):
                        pool.wait_ge(x_in[j], 16 * (t + 1))
                        pool.tensor_tensor(x_t[:, j, :], x_t[:, j, :], b_ff[:, :], ALU.add).then_inc(s["xb"], 1)
                    for j in range(SB):
                        n = t * SB + j
                        pool.wait_ge(s["xnT"], n + 1)
                        pool.tensor_copy(core.xnT[:, :, bass.ds(n * P, P)], xnT[:, j, :, :]).then_inc(s["keep"], 1)

            @block.vector
            def _(dve):
                dve.wait_ge(par_in, 16 * (3 + 2 * KC))
                with dve.Fori(0, ST) as t:
                    sums = core.acc[:, bass.ds(t * SB * W, SB * W)].rearrange("p (j w) -> p j w", w=W)[:, :, D:W]
                    dve.wait_ge(s["o"], t * SB)
                    dve.tensor_scalar(inv_l[:, 0, :, :], sums, 1e-30, None, ALU.max).then_inc(s["lmax"], 1)
                    dve.wait_ge(s["lmax"], t + 1)
                    dve.reciprocal(inv_l[:, 1, :, :], inv_l[:, 0, :, :]).then_inc(s["inv_l"], 1)
                    for j in range(SB):
                        n = t * SB + j
                        dve.wait_ge(s["yp"], n + 1)
                        dve.wait_ge(s["xb"], n + 1)
                        dve.wait_ge(s["o"], n + 1)
                        dve.tensor_tensor(y1_at(n), yp[j % 2][:, 0:D], x_t[:, j, :], ALU.add).then_inc(s["y1"], 1)
                    for r in range(2):
                        for j in range(SB):
                            n = t * SB + j
                            if r == 0:
                                dve.wait_ge(s["y1"], n + 1)
                            else:
                                dve.wait_ge(s["ln"], 2 * t * SB + j + 1)
                            wait_here(dve, core)
                            dve.bn_stats(stats[:, r, j, :], ln[:, 0, j, :] if r else y1_at(n)).then_inc(s["stats"], 1)
                        for j in range(SB):
                            dve.wait_ge(s["stats"], (2 * t + r) * SB + j + 1)
                            wait_here(dve, core)
                            dve.bn_aggr(mv[:, r, j, :], stats[:, r, j, :]).then_inc(s["mv"], 1)
                        for j in range(SB):
                            dve.wait_ge(s["std"], (2 * t + r) * SB + j + 1)
                            dve.reciprocal(rstd[:, r, j:j + 1], std[:, r, j:j + 1]).then_inc(s["rstd"], 1)
                        for j in range(SB):
                            n = t * SB + j
                            dve.wait_ge(s["rstd"], (2 * t + r) * SB + j + 1)
                            if r == 1:
                                dve.wait_ge(s["z_tp"], t * SB)
                            dve.tensor_scalar(ln[:, r, j, :], ln[:, 0, j, :] if r else y1_at(n),
                                              mv[:, r, j, 0:1], rstd[:, r, j:j + 1], ALU.subtract,
                                              ALU.mult).then_inc(s["ln"], 1)
                    for j in range(SB):
                        n = t * SB + j
                        dve.wait_ge(s["lp"], n + 1)
                        dve.tensor_tensor(core.logits[:, bass.ds(n, 1), :].rearrange("p a e -> p (a e)"),
                                          lp[j % 2][:, 0:EXPERTS], br[:, :], ALU.add).then_inc(s["logits"], 1)

            @block.scalar
            def _(act):
                act.wait_ge(par_in, 16 * (3 + 2 * KC))
                with act.Fori(0, ST) as t:
                    for j in range(SB):
                        n = t * SB + j
                        act.wait_ge(s["o_tp"], n + 1)
                        act.wait_ge(s["keep"], t * SB)
                        act.wait_ge(s["lp"], t * SB)
                        act.copy(oT[:, j, :, :], o_tp[j % 2][:, :, 0:P]).then_inc(s["oT"], 1)
                    for r in range(2):
                        for j in range(SB):
                            act.wait_ge(s["mv"], (2 * t + r) * SB + j + 1)
                            act.activation(std[:, r, j:j + 1], mv[:, r, j, 1:2], ACT.Sqrt,
                                           bias=core.eps[:, :]).then_inc(s["std"], 1)
                    for j in range(SB):
                        n = t * SB + j
                        act.wait_ge(s["z_tp"], n + 1)
                        act.wait_ge(s["yp"], (t + 1) * SB)
                        for k in range(KC):
                            ins = act.activation(xnT[:, j, k, :], z_tp[j % 2][:, k, 0:P], ACT.Identity,
                                                 scale=gamma[:, k:k + 1], bias=beta[:, k:k + 1])
                        ins.then_inc(s["xnT"], 1)

            @block.tensor
            def _(pe):
                pe.wait_ge(par_in, 16 * (3 + 2 * KC))
                with pe.Fori(0, ST) as t:
                    for j in range(SB):
                        n = t * SB + j
                        pe.wait_ge(s["o"], n + 1)
                        free_slot(pe, s["oT"], n, j)
                        for k in range(KC):
                            mm = pe.transpose(o_tp[j % 2][:, k, 0:P], o[:, j, k * P:(k + 1) * P], core.ident[:, :])
                        mm.then_inc(s["o_tp"], 1)
                    for j in range(SB):
                        n = t * SB + j
                        pe.wait_ge(s["oT"], n + 1)
                        free_slot(pe, s["y1"], n, j)
                        for k in range(KC):
                            mm = pe.matmul(yp[j % 2][:, 0:D], oT[:, j, k, :], core.wffT[:, k, :], start=(k == 0),
                                           stop=(k == KC - 1))
                        mm.then_inc(s["yp"], 1)
                    for j in range(SB):
                        n = t * SB + j
                        pe.wait_ge(s["ln"], (2 * t + 1) * SB + j + 1)
                        free_slot(pe, s["xnT"], n, j)
                        for k in range(KC):
                            mm = pe.transpose(z_tp[j % 2][:, k, 0:P], ln[:, 1, j, k * P:(k + 1) * P],
                                              core.ident[:, :])
                        mm.then_inc(s["z_tp"], 1)
                    for j in range(SB):
                        n = t * SB + j
                        pe.wait_ge(s["xnT"], n + 1)
                        free_slot(pe, s["logits"], n, j)
                        for k in range(KC):
                            mm = pe.matmul(lp[j % 2][:, 0:EXPERTS], xnT[:, j, k, :], wr[:, k, :], start=(k == 0),
                                           stop=(k == KC - 1))
                        mm.then_inc(s["lp"], 1)


def phase_gate(nc, core, d):
    W = D + HEADS
    with ExitStack() as st:
        sb, ps = tensors(nc, st)
        iota = sb("g_iota", [P, EXPERTS], I32)
        rank = sb("g_rank", [P, EXPERTS], F32)
        key = sb("g_key", [P, BLOCKS, EXPERTS], F32)
        left = sb("g_left", [P, BLOCKS, EXPERTS], F32)
        mask = sb("g_mask", [P, 2, BLOCKS, EXPERTS], F32)
        top = sb("g_top", [P, 2, BLOCKS], F32)
        best = sb("g_best", [P, BLOCKS], F32)
        diff = sb("g_diff", [P, BLOCKS], F32)
        e2 = sb("g_e2", [P, BLOCKS], F32)
        part = sb("g_part", [P, 2, BLOCKS], F32)
        w_now = sb("g_w_now", [P, SB, EXPERTS], F32)
        wT = sb("g_wT", [EXPERTS, SB, P], F32)
        tp = [ps(f"g_tp{i}", [P, 512], F32) for i in range(2)]
        bp = [ps(f"g_bp{i}", [P, 512], F32) for i in range(2)]
        b1_tp = ps("g_b1_tp", [P, 512], F32)
        iota_done, chain, diff_done, e2_done, w_now_done, tp_done, wT_done, bp_done, y_done, b1_done = (
            core.sem("g_" + n) for n in ("iota", "chain", "diff", "e2", "w_now", "tp", "wT", "bp", "y", "b1"))

        def over_experts(a):
            return a.unsqueeze(2).to_broadcast([P, BLOCKS, EXPERTS])

        with nc.Block() as block:
            @block.gpsimd
            def _(pool):
                pool.iota(iota[:, :], pattern=[[-1, EXPERTS]], base=EXPERTS, channel_multiplier=0
                          ).then_inc(iota_done, 1)

            @block.scalar
            def _(act):
                act.wait_ge(b1_done, 1)
                act.copy(core.b1[:, :], b1_tp[:, 0:EXPERTS * HC])
                act.wait_ge(diff_done, 1)
                act.activation(e2[:, :], diff[:, :], ACT.Exp).then_inc(e2_done, 1)
                with act.Fori(0, ST) as t:
                    for j in range(SB):
                        n = t * SB + j
                        act.wait_ge(tp_done, n + 1)
                        act.wait_ge(bp_done, t * SB)
                        act.copy(wT[:, j, :], tp[j % 2][0:EXPERTS, 0:P]).then_inc(wT_done, 1)

            @block.tensor
            def _(pe):
                pe.transpose(b1_tp[:, 0:EXPERTS * HC], core.b1_rows[:, :],
                             core.ident[0:EXPERTS * HC, 0:EXPERTS * HC]).then_inc(b1_done, 1)
                with pe.Fori(0, ST) as t:
                    for j in range(SB):
                        n = t * SB + j
                        pe.wait_ge(w_now_done, t + 1)
                        pe.wait_ge(wT_done, n if j == 0 else n - 1)
                        pe.transpose(tp[j % 2][0:EXPERTS, 0:P], w_now[:, j, :], core.ident[:, :]
                                     ).then_inc(tp_done, 1)
                    for j in range(SB):
                        n = t * SB + j
                        pe.wait_ge(wT_done, n + 1)
                        pe.wait_ge(y_done, n if j == 0 else n - 1)
                        pe.matmul(bp[j % 2][:, 0:D], wT[:, j, :], core.b2[:, :], start=True, stop=True
                                  ).then_inc(bp_done, 1)

            @block.vector
            def _(dve):
                done = [0]

                def then(ins):
                    done[0] += 1
                    ins.then_inc(chain, 1)
                    dve.wait_ge(chain, done[0])

                dve.wait_ge(iota_done, 1)
                then(dve.tensor_copy(rank[:, :], iota[:, :]))
                for r in range(2):
                    source = left if r else core.logits
                    then(dve.tensor_reduce(top[:, r, :], source[:, :, :], X, ALU.max))
                    then(dve.tensor_tensor(key[:, :, :], source[:, :, :], over_experts(top[:, r, :]), ALU.is_equal))
                    then(dve.tensor_tensor(key[:, :, :], key[:, :, :],
                                           rank[:, :].unsqueeze(1).to_broadcast([P, BLOCKS, EXPERTS]), ALU.mult))
                    then(dve.tensor_reduce(best[:, :], key[:, :, :], X, ALU.max))
                    then(dve.tensor_tensor(mask[:, r, :, :], key[:, :, :], over_experts(best[:, :]), ALU.is_equal))
                    if r == 0:
                        then(dve.scalar_tensor_tensor(out=left[:, :, :], in0=mask[:, 0, :, :], scalar=-BIG,
                                                      in1=core.logits[:, :, :], op0=ALU.mult, op1=ALU.add))
                dve.tensor_tensor(diff[:, :], top[:, 1, :], top[:, 0, :], ALU.subtract).then_inc(diff_done, 1)
                dve.wait_ge(e2_done, 1)
                then(dve.tensor_scalar(best[:, :], e2[:, :], 1.0, None, ALU.add))
                then(dve.reciprocal(part[:, 0, :], best[:, :]))
                then(dve.tensor_tensor(part[:, 1, :], e2[:, :], part[:, 0, :], ALU.mult))
                for r in range(2):
                    then(dve.tensor_tensor(mask[:, r, :, :], mask[:, r, :, :], over_experts(part[:, r, :]),
                                           ALU.mult))
                then(dve.tensor_tensor(core.gate[:, :, :], mask[:, 0, :, :], mask[:, 1, :, :], ALU.add))
                with dve.Fori(0, ST) as t:
                    dve.wait_ge(tp_done, t * SB)
                    dve.tensor_copy(w_now[:, :, :], core.gate[:, bass.ds(t * SB, SB), :]).then_inc(w_now_done, 1)
                    for j in range(SB):
                        n = t * SB + j
                        dve.wait_ge(bp_done, n + 1)
                        y = core.acc[:, bass.ds(n * W, D)]
                        dve.tensor_tensor(y, bp[j % 2][:, 0:D], y, ALU.add).then_inc(y_done, 1)


def phase_experts(nc, core, d):
    W = D + HEADS
    HALF = SB * P // 2
    assert HALF <= 512 and (EXPERTS * SB) % 4 == 0
    with ExitStack() as st:
        sb, ps = tensors(nc, st)
        hT = [sb("e_hT", [P, HC, SB * P], F32),
              core.tail[:, 0:HC * SB * P].rearrange("p (c n) -> p c n", c=HC)]
        hp = [ps(f"e_hp{i}", [P, 2, 512], F32) for i in range(2)]
        yp = [ps(f"e_yp{i}", [P, 512], F32) for i in range(4)]
        hp_done, gelu_done, yp_done, y_done, out_done = (core.sem("e_" + n) for n in
                                                         ("hp", "gelu", "yp", "y", "out"))
        with nc.Block() as block:
            @block.tensor
            def _(pe):
                pe.sem_inc(yp_done, 2 * SB)

                def up(t, e):
                    for c in range(HC):
                        m = (t * EXPERTS + e) * HC + c
                        pe.wait_ge(gelu_done, m + 1)
                        for half in range(2):
                            for k in range(KC):
                                mm = pe.matmul(hp[c % 2][:, half, 0:HALF], core.w1[:, e, k, c * P:(c + 1) * P],
                                               core.xnT[:, k, bass.ds(t * SB * P + half * HALF, HALF)],
                                               start=(k == 0), stop=(k == KC - 1))
                        mm.then_inc(hp_done, 1)

                def down(t, e):
                    pe.wait_ge(gelu_done, (t * EXPERTS + e + 1) * HC + 2)
                    for j in range(SB):
                        r = (t * EXPERTS + e) * SB + j
                        slot = (e * SB + j) % 4
                        pe.wait_ge(y_done, r + 1)
                        for c in range(HC):
                            mm = pe.matmul(yp[slot][:, 0:D], hT[e % 2][:, c, j * P:(j + 1) * P],
                                           core.w2[:, e, c, :], start=(c == 0), stop=(c == HC - 1))
                        mm.then_inc(yp_done, 1)

                with pe.Fori(0, ST) as t:
                    up(t, 0)
                    for e in range(EXPERTS):
                        if e + 1 < EXPERTS:
                            up(t, e + 1)
                        down(t, e)

            @block.scalar
            def _(act):
                act.sem_inc(gelu_done, 2)
                with act.Fori(0, ST) as t:
                    for e in range(EXPERTS):
                        for c in range(HC):
                            m = (t * EXPERTS + e) * HC + c
                            act.wait_ge(hp_done, m + 1)
                            if c == 0:
                                act.wait_ge(yp_done, (t * EXPERTS + e + 1) * SB)
                            act.activation(hT[e % 2][:, c, :].rearrange("p (a n) -> p a n", a=2),
                                           hp[c % 2][:, :, 0:HALF], ACT.Gelu,
                                           bias=core.b1[:, e * HC + c:e * HC + c + 1]).then_inc(gelu_done, 1)

            @block.vector
            def _(dve):
                dve.sem_inc(y_done, 4)
                with dve.Fori(0, ST) as t:
                    for e in range(EXPERTS):
                        for j in range(SB):
                            n, r = t * SB + j, (t * EXPERTS + e) * SB + j
                            dve.wait_ge(yp_done, r + 1 + 2 * SB)
                            if e:
                                dve.wait_ge(y_done, r - SB + 1 + 4)
                            y = core.acc[:, bass.ds(n * W, D)]
                            gate = core.gate[:, bass.ds(n, 1), e]
                            dve.scalar_tensor_tensor(out=y, in0=yp[(e * SB + j) % 4][:, 0:D], scalar=gate, in1=y,
                                                     op0=ALU.mult, op1=ALU.add).then_inc(y_done, 1)

            @block.sync
            def _(sp):
                with sp.Fori(0, ST) as t:
                    sp.wait_ge(y_done, (t + 1) * EXPERTS * SB + 4)
                    sp.dma_start(d["out"][bass.ds(t * SB * P, SB * P), :].rearrange("(j p) c -> p j c", p=P),
                                 core.acc[:, bass.ds(t * SB * W, SB * W)].rearrange("p (j w) -> p j w", w=W)[:, :, 0:D]
                                 ).then_inc(out_done, 16)
                sp.wait_ge(out_done, 16 * ST)


def build(nc, d):
    with ExitStack() as st:
        core = Core(nc, st)
        sb, ps = tensors(nc, st)
        core.ident = sb("ident", [P, P], F32)
        core.ident_bf = sb("ident_bf", [P, P], BF16)
        core.iota_bf = sb("iota_bf", [P, P], BF16)
        core.zero_bf = sb("zero_bf", [P, D + HEADS], BF16)
        core.ones = sb("ones", [P, P], F32)
        core.eps = sb("eps", [P, 1], F32)
        core.wffT = sb("wffT", [P, KC, D], F32)
        core.bounds = sb("bounds", [P, BLOCKS + 1], I32)
        core.w_in = core.sem("w_in")
        core.waited = core.sem("waited")
        arena = sb("arena", [P, BLOCKS * 3 * D // 2], F32)
        core.q_parts = arena[:, :].bitcast(BF16)
        core.attT = arena[:, 0:HEADS * VPAD].rearrange("p (h c e) -> p h c e", h=HEADS, c=VC)
        core.fwd = arena[:, HEADS * VPAD:(HEADS + 2) * VPAD].rearrange("p (a v) -> p a v", a=2)
        core.acc = arena[:, 0:BLOCKS * (D + HEADS)]
        core.tail = arena[:, BLOCKS * (D + HEADS):]
        with ExitStack() as edge_life:
            sbe, _ = tensors(nc, edge_life)
            core.srcT = sbe("srcT", [P, VPAD], I32)
            core.dstT = sbe("dstT", [P, VPAD], F32)
            core.dstV = sbe("dstV", [P, VC, P], F32)
            core.att = sbe("att", [P, VPAD * HEADS], F32)
            with ExitStack() as w_life:
                sbw, _ = tensors(nc, w_life)
                core.wqkvT = sbw("wqkvT", [P, KC, 3 * D], F32)
                core.b_qkv = sbw("b_qkv", [P, 3 * D], F32)
                phase_constants(nc, core, d)
                phase_project(nc, core, d)
            phase_route(nc, core, d)
            phase_scores(nc, core, d)
            phase_softmax(nc, core, d)
            phase_gather_values(nc, core, d)
        core.xnT = sb("xnT", [P, KC, ROWS], F32)
        core.gate = sb("gate", [P, BLOCKS, EXPERTS], F32)
        core.w1 = sb("w1", [P, EXPERTS, KC, HID], F32)
        core.w2 = sb("w2", [P, EXPERTS, HC, D], F32)
        core.b1 = sb("b1", [P, EXPERTS * HC], F32)
        with ExitStack() as gate_life:
            sbg, _ = tensors(nc, gate_life)
            core.logits = sbg("logits", [P, BLOCKS, EXPERTS], F32)
            core.b2 = sbg("b2", [EXPERTS, D], F32)
            core.b1_rows = sbg("b1_rows", [EXPERTS * HC, P], F32)
            phase_node(nc, core, d)
            phase_gate(nc, core, d)
        phase_experts(nc, core, d)


_WEIGHTS = {"W_qkv": "L0_gnn_W_qkv", "b_qkv": "L0_gnn_b_qkv", "W_ff": "L0_gnn_W_ff", "b_ff": "L0_gnn_b_ff",
            "gamma": "L0_ffn_gamma", "beta": "L0_ffn_beta", "Wr": "L0_ffn_Wr", "br": "L0_ffn_br",
            "W1": "L0_ffn_W1", "b1": "L0_ffn_b1", "W2": "L0_ffn_W2", "b2": "L0_ffn_b2"}


def kernel(**inputs):
    import numpy as np
    import concourse.bacc as bacc
    from concourse.bass_utils import run_bass_kernel_spmd

    x = np.zeros((ROWS, D), np.float32)
    x[:NODES] = inputs["x"]
    edges = np.zeros((2, (TILES + 1) * P), np.int32)
    edges[1] = -1
    edges[0, :EDGES] = inputs["src"]
    edges[1, :EDGES] = inputs["dst"]
    edges = np.ascontiguousarray(edges.reshape(2, TILES + 1, P).transpose(1, 0, 2)).reshape(TILES + 1, 2 * P)
    arrays = {"x": x, "edges": edges}
    for name, given in _WEIGHTS.items():
        arrays[name] = np.ascontiguousarray(inputs[given])

    nc = bacc.Bacc("TRN2", target_bir_lowering=False, num_devices=1)
    d = {name: nc.dram_tensor("in_" + name, a.shape, mybir.dt.from_np(a.dtype), kind="ExternalInput").ap()
         for name, a in arrays.items()}
    d["k_table"] = nc.dram_tensor("k_table", (ROWS, D), F32).ap()
    d["v_table"] = nc.dram_tensor("v_table", (ROWS, D), F32).ap()
    d["out"] = nc.dram_tensor("out", (ROWS, D), F32, kind="ExternalOutput").ap()
    build(nc, d)
    got = run_bass_kernel_spmd(nc, [{"in_" + name: a for name, a in arrays.items()}], core_ids=[0])
    return got.results[0]["out"][:NODES]
```

```python
from contextlib import ExitStack

import concourse.bass as bass
from concourse import mybir

ALU = mybir.AluOpType
ACT = mybir.ActivationFunctionType
F32 = mybir.dt.float32
BF16 = mybir.dt.bfloat16
I32 = mybir.dt.int32
X = mybir.AxisListType.X

P = 128
NODES = 6250
EDGES = 200000
D = 256
HEADS = 8
DH = D // HEADS
KC = D // P
BLOCKS = -(-NODES // P)
ROWS = BLOCKS * P
TILES = -(-EDGES // P)
PAD_TILE = TILES
GV = 4
GROUPS = -(-((TILES + BLOCKS - 1 + BLOCKS * (GV - 1)) // GV) // 4) * 4
VISITS = GROUPS * GV
VC = -(-(VISITS + 8) // P)
VPAD = VC * P
BATCH = 16
BATCHES = VISITS // BATCH
STEPS = BATCH // 2
RING_STEPS = 2 * STEPS
LAG = STEPS + STEPS // 2
W = HEADS + D
HOLD = -(-VISITS // BATCH // 8) * 8
ROWTAB = 2 * HEADS * (BATCH + 1) + 2 * BATCH + 2
BIG = 1.0e30
SB = 7
ST = BLOCKS // SB
EXPERTS = 8
HID = 512
HC = HID // P
EPS = 1e-5
SCALE = float(DH) ** -0.5
assert ST * SB == BLOCKS and VISITS % (2 * BATCH) == 0 and D == HEADS * DH


class Core:

    def __init__(self, nc, stack):
        self.nc = nc
        self.stack = stack

    def sem(self, name):
        return self.stack.enter_context(self.nc.semaphore(name))


def wait_here(eng, core):
    eng.sem_inc(core.waited, 1)


def tensors(nc, stack):
    def sb(name, shape, dt):
        return stack.enter_context(nc.sbuf_tensor(name, shape, dt))

    def ps(name, shape, dt):
        return stack.enter_context(nc.psum_tensor(name, shape, dt))
    return sb, ps


def phase_constants(nc, core, d):
    with ExitStack() as st:
        sb, ps = tensors(nc, st)
        diag = sb("diag", [P, P], I32)
        iota_i = sb("iota_i", [P, P], I32)
        wq_rows = sb("wq_rows", [P, 3 * KC, D], F32)
        wf_rows = sb("wf_rows", [P, KC, D], F32)
        wffT = sb("wffT_first", [P, KC, D], F32)
        tp = ps("tp_w", [P, 4, 512], F32)
        iota_done, ident_done = core.sem("c_iota"), core.sem("c_ident")
        w_in, tp_done, tp_used, small_in = (core.sem(n) for n in ("c_w_in", "c_tp", "c_tp_used", "c_small"))
        with nc.Block() as block:
            @block.gpsimd
            def _(pool):
                pool.iota(diag[:, :], pattern=[[1, P]], base=0, channel_multiplier=-1).then_inc(iota_done, 1)
                pool.iota(iota_i[:, :], pattern=[[1, P]], base=0, channel_multiplier=0).then_inc(iota_done, 1)
                pool.memset(core.acc[:, :], 0.0)

            @block.sync
            def _(sp):
                sp.dma_start(wq_rows[:, :, :], d["W_qkv"].rearrange("(c p) k -> p c k", p=P)).then_inc(w_in, 16)
                sp.dma_start(wf_rows[:, :, :], d["W_ff"].rearrange("(c p) k -> p c k", p=P)).then_inc(w_in, 16)
                sp.dma_start(core.b_qkv[:, :], d["b_qkv"].partition_broadcast(P)).then_inc(small_in, 16)
                sp.wait_ge(small_in, 16)
                sp.wait_ge(tp_used, (3 * KC + KC) * KC)
                sp.dma_start(d["wff_table"], wffT[:, :, :]).then_inc(small_in, 16)
                sp.wait_ge(small_in, 32)

            @block.vector
            def _(dve):
                dve.wait_ge(iota_done, 2)
                dve.tensor_scalar(core.ident[:, :], diag[:, :], 0.0, None, ALU.is_equal)
                dve.tensor_scalar(core.ident_bf[:, :], diag[:, :], 0.0, None, ALU.is_equal)
                dve.tensor_copy(core.iota_bf[:, :], iota_i[:, :])
                dve.memset(core.ones[:, :], 1.0)
                dve.memset(core.eps[:, :], EPS).then_inc(ident_done, 1)

            def weight_chunks():
                for c in range(3 * KC):
                    for k in range(KC):
                        yield wq_rows[:, c, k * P:(k + 1) * P], core.wqkvT[:, k, c * P:(c + 1) * P]
                for c in range(KC):
                    for k in range(KC):
                        yield wf_rows[:, c, k * P:(k + 1) * P], wffT[:, k, c * P:(c + 1) * P]

            @block.tensor
            def _(pe):
                pe.wait_ge(ident_done, 1)
                pe.wait_ge(w_in, 32)
                for n, (src, _) in enumerate(weight_chunks()):
                    if n >= 4:
                        pe.wait_ge(tp_used, n - 3)
                    pe.transpose(tp[:, n % 4, 0:P], src, core.ident[:, :]).then_inc(tp_done, 1)

            @block.scalar
            def _(act):
                for n, (_, dst) in enumerate(weight_chunks()):
                    act.wait_ge(tp_done, n + 1)
                    act.copy(dst, tp[:, n % 4, 0:P]).then_inc(tp_used, 1)


def phase_project(nc, core, d):
    with ExitStack() as st:
        sb, ps = tensors(nc, st)
        x_t = sb("p_x_t", [P, SB, D], F32)
        stats = sb("p_stats", [P, SB, 6], F32)
        mv = sb("p_mv", [P, SB, 2], F32)
        std = sb("p_std", [P, SB], F32)
        rstd = sb("p_rstd", [P, SB], F32)
        xh = sb("p_xh", [P, SB, D], F32)
        xhT = sb("p_xhT", [P, SB, KC, P], F32)
        qkv = sb("p_qkv", [P, SB, 3 * D], F32)
        rest1 = sb("p_rest1", [P, SB, D], F32)
        rest2 = sb("p_rest2", [P, SB, D], F32)
        tp = [ps(f"p_tp{i}", [P, KC, 256], F32) for i in range(2)]
        qp = [ps(f"p_qp{i}", [P, 1024], F32) for i in range(3)]
        x_in = [core.sem(f"p_x_in{j}") for j in range(SB)]
        kv_out = [core.sem(f"p_kv_out{j}") for j in range(SB)]
        names = ("stats", "mv", "std", "rstd", "xh", "tp", "xhT", "qkvp", "qkv", "q1", "r1", "q2", "r2", "q3")
        s = {n: core.sem("p_s_" + n) for n in names}

        with nc.Block() as block:
            @block.sync
            def _(sp):
                with sp.Fori(0, ST) as t:
                    for j in range(SB):
                        n = t * SB + j
                        sp.wait_ge(s["xh"], t * SB)
                        sp.dma_start(x_t[:, j, :], d["x"][bass.ds(n * P, P), :]).then_inc(x_in[j], 16)
                    for j in range(SB):
                        n = t * SB + j
                        sp.wait_ge(s["qkv"], n + 1)
                        sp.dma_start(d["kv_table"][bass.ds(n * P, P), :], qkv[:, j, D:3 * D]).then_inc(kv_out[j], 16)
                for j in range(SB):
                    sp.wait_ge(kv_out[j], 16 * ST)

            @block.vector
            def _(dve):
                with dve.Fori(0, ST) as t:
                    for j in range(SB):
                        dve.wait_ge(x_in[j], 16 * (t + 1))
                        dve.bn_stats(stats[:, j, :], x_t[:, j, :]).then_inc(s["stats"], 1)
                    for j in range(SB):
                        dve.wait_ge(s["stats"], t * SB + j + 1)
                        dve.wait_ge(s["std"], t * SB)
                        wait_here(dve, core)
                        dve.bn_aggr(mv[:, j, :], stats[:, j, :]).then_inc(s["mv"], 1)
                    for j in range(SB):
                        dve.wait_ge(s["std"], t * SB + j + 1)
                        dve.reciprocal(rstd[:, j:j + 1], std[:, j:j + 1]).then_inc(s["rstd"], 1)
                    for j in range(SB):
                        dve.wait_ge(s["rstd"], t * SB + j + 1)
                        dve.wait_ge(s["tp"], t * SB)
                        dve.tensor_scalar(xh[:, j, :], x_t[:, j, :], mv[:, j, 0:1], rstd[:, j:j + 1],
                                          ALU.subtract, ALU.mult).then_inc(s["xh"], 1)
                    for j in range(SB):
                        n = t * SB + j
                        dve.wait_ge(s["qkvp"], n + 1)
                        dve.wait_ge(s["r1"], t * SB)
                        dve.wait_ge(s["q1"], t * SB)
                        dve.wait_ge(kv_out[j], 16 * t)
                        dve.tensor_tensor(qkv[:, j, :], qp[j % 3][:, 0:3 * D], core.b_qkv[:, :],
                                          ALU.add).then_inc(s["qkv"], 1)

            @block.scalar
            def _(act):
                with act.Fori(0, ST) as t:
                    for j in range(SB):
                        act.wait_ge(s["mv"], t * SB + j + 1)
                        act.wait_ge(s["rstd"], t * SB)
                        act.activation(std[:, j:j + 1], mv[:, j, 1:2], ACT.Sqrt,
                                       bias=core.eps[:, :]).then_inc(s["std"], 1)
                    for j in range(SB):
                        act.wait_ge(s["tp"], t * SB + j + 1)
                        act.wait_ge(s["qkvp"], t * SB)
                        act.copy(xhT[:, j, :, :], tp[j % 2][:, :, 0:P]).then_inc(s["xhT"], 1)
                    for part, src, need in ((0, None, "qkv"), (1, rest1, "r1"), (2, rest2, "r2")):
                        for j in range(SB):
                            n = t * SB + j
                            act.wait_ge(s[need], n + 1)
                            source = qkv[:, j, 0:D] if src is None else src[:, j, :]
                            wait_here(act, core)
                            act.copy(core.q_parts[:, bass.ds((n * 3 + part) * D, D)],
                                     source).then_inc(s[("q1", "q2", "q3")[part]], 1)

            @block.gpsimd
            def _(pool):
                with pool.Fori(0, ST) as t:
                    for part in range(2):
                        for j in range(SB):
                            n = t * SB + j
                            pool.wait_ge(s[("q1", "q2")[part]], n + 1)
                            if part:
                                pool.wait_ge(s["r1"], n + 1)
                            pool.wait_ge(s[("q2", "q3")[part]], t * SB)
                            src = rest1[:, j, :] if part else qkv[:, j, 0:D]
                            dst = rest2 if part else rest1
                            pool.tensor_tensor(dst[:, j, :], src, core.q_parts[:, bass.ds((n * 3 + part) * D, D)],
                                               ALU.subtract).then_inc(s[("r1", "r2")[part]], 1)

            @block.tensor
            def _(pe):
                with pe.Fori(0, ST) as t:
                    for j in range(SB):
                        n = t * SB + j
                        pe.wait_ge(s["xh"], n + 1)
                        pe.wait_ge(s["xhT"], n if j == 0 else n - 1)
                        for k in range(KC):
                            mm = pe.transpose(tp[j % 2][:, k, 0:P], xh[:, j, k * P:(k + 1) * P], core.ident[:, :])
                        mm.then_inc(s["tp"], 1)
                    for j in range(SB):
                        n = t * SB + j
                        pe.wait_ge(s["xhT"], n + 1)
                        pe.wait_ge(s["qkv"], n if j == 0 else (n - 1 if j == 1 else n - 2))
                        for lo, hi in ((0, 512), (512, 768)):
                            for k in range(KC):
                                mm = pe.matmul(qp[j % 3][:, lo:hi], xhT[:, j, k, :], core.wqkvT[:, k, lo:hi],
                                               start=(k == 0), stop=(k == KC - 1))
                        mm.then_inc(s["qkvp"], 1)


def phase_route(nc, core, d):
    NB1 = BLOCKS + 1
    full = TILES // P * P // P
    left = TILES - full * P
    with ExitStack() as st:
        sb, ps = tensors(nc, st)
        first = sb("r_first", [P, full + 1], I32)
        firstf = sb("r_firstf", [P, full + 1], F32)
        bound_i = sb("r_bound_i", [P, NB1], I32)
        bound = sb("r_bound", [P, NB1], F32)
        visit_i = sb("r_visit_i", [P, VC], I32)
        visit = sb("r_visit", [P, VC], F32)
        below = sb("r_below", [P, NB1, full + 1], F32)
        cnt = sb("r_cnt", [P, NB1], F32)
        T = sb("r_T", [P, NB1], F32)
        size = sb("r_size", [P, BLOCKS], F32)
        size_i = sb("r_size_i", [P, BLOCKS], I32)
        size_q = sb("r_size_q", [P, BLOCKS], I32)
        one = sb("r_one", [P, BLOCKS], F32)
        gend = sb("r_gend", [P, BLOCKS], F32)
        v0 = sb("r_v0", [P, BLOCKS], F32)
        rel = sb("r_rel", [P, BLOCKS], F32)
        steps = sb("r_steps", [P, 3, BLOCKS], F32)
        ge = sb("r_ge", [P, VC, BLOCKS], F32)
        tmp = sb("r_tmp", [P, VC, BLOCKS], F32)
        vb = sb("r_vb", [P, VC], F32)
        vt = sb("r_vt", [P, VC], F32)
        vend = sb("r_vend", [P, VC], F32)
        ok = sb("r_ok", [P, VC], F32)
        tile_i = sb("r_tile_i", [P, VC], I32)
        rows = sb("r_rows", [P, VC, 2 * P], I32)
        src_f = sb("r_src_f", [P, VC, P], F32)
        loc_f = sb("r_loc_f", [P, VC, P], F32)
        dst_f = sb("r_dst_f", [P, VC, P], F32)
        inside, below_end = rows[:, :, 0:P].bitcast(F32), rows[:, :, P:2 * P].bitcast(F32)
        begins = sb("r_begins", [P, VC, P + 1], F32)
        ends = sb("r_ends", [P, VC, 3], F32)
        before = sb("r_before", [1, 3], F32)
        block_i = sb("r_block_i", [P, VC], I32)
        meta = sb("r_meta", [P, HOLD, 2 * BATCH], I32)
        this = sb("r_this", [BATCHES, BATCH, 3], F32)
        prev = sb("r_prev", [BATCHES, BATCH, 3], F32)
        enter = sb("r_enter", [BATCHES, BATCH + 1], F32)
        many = sb("r_many", [BATCHES, BATCH], F32)
        through = sb("r_through", [BATCHES, 2, BATCH], F32)
        table = sb("r_table", [BATCHES, ROWTAB], F32)
        psum_cnt = ps("r_cnt_ps", [P, 512], F32)
        tp = [ps(f"r_tp{i}", [P, 4, P], F32) for i in range(2)]
        iotas, first_in, step, cnt_ps, tile_ready = (core.sem("r_" + n) for n in
                                                     ("iotas", "first_in", "step", "cnt_ps", "tile_ready"))
        rows_in, tp_done, tp_used, split = (core.sem("r_" + n) for n in ("rows_in", "tp_done", "tp_used", "split"))
        padded, ends_ready, ends_out, ends_in, begins_out, table_ready = (core.sem("r_" + n) for n in (
            "padded", "ends_ready", "ends_out", "ends_in", "begins_out", "table_ready"))
        with nc.Block() as block:
            @block.gpsimd
            def _(pool):
                pool.memset(first[:, :], 1 << 20).then_inc(padded, 1)
                pool.iota(bound_i[:, :], pattern=[[P, NB1]], base=0, channel_multiplier=0).then_inc(iotas, 1)
                pool.iota(visit_i[:, :], pattern=[[P, VC]], base=0, channel_multiplier=1).then_inc(iotas, 1)
                last_row = pool.to_reg(PAD_TILE)
                pool.wait_ge(tile_ready, 1)
                for c in range(VC):
                    pool.indirect_dma_start(rows[:, c, :], None, d["edges"],
                                            bass.IndirectOffsetOnAxis(ap=tile_i[:, c:c + 1], axis=0),
                                            bounds_check=last_row, oob_is_err=False).then_inc(rows_in, 16)

            @block.sync
            def _(sp):
                dst_first = d["edges"][:, P:P + 1]
                sp.wait_ge(padded, 1)
                sp.dma_start(first[:, 0:full].unsqueeze(2),
                             dst_first[0:full * P, :].rearrange("(p c) o -> p c o", c=full),
                             allow_slow_non_contiguous=True).then_inc(first_in, 16)
                sp.dma_start(first[0:left, full:full + 1], dst_first[full * P:TILES, :],
                             allow_slow_non_contiguous=True).then_inc(first_in, 16)
                sp.wait_ge(first_in, 32)
                sp.wait_ge(ends_ready, 1)
                visits = d["ends_table"][1:VPAD + 1, :].rearrange("(c p) k -> p c k", p=P)
                sp.dma_start(visits, ends[:, :, :]).then_inc(ends_out, 16)
                sp.dma_start(d["ends_table"][0:1, :], before[:, :]).then_inc(ends_out, 16)
                sp.dma_start(d["block_table"].rearrange("(c p) -> p c", p=P).unsqueeze(2),
                             block_i[:, :].unsqueeze(2), allow_slow_non_contiguous=True).then_inc(ends_out, 16)
                sp.dma_start(d["begins_table"].rearrange("(c p) e -> p c e", p=P), begins[:, :, :]
                             ).then_inc(begins_out, 16)
                sp.wait_ge(ends_out, 48)
                sp.dma_start(this[:, :, :], d["ends_table"][1:VISITS + 1, :].rearrange("(b v) k -> b v k", v=BATCH)
                             ).then_inc(ends_in, 16)
                sp.dma_start(prev[:, :, :], d["ends_table"][0:VISITS, :].rearrange("(b v) k -> b v k", v=BATCH)
                             ).then_inc(ends_in, 16)
                sp.dma_start(core.block_of[:, :].unsqueeze(2),
                             d["block_table"][0:VISITS].rearrange("(o g v) -> o g v", o=1, v=GV)[:, :, 0:1],
                             allow_slow_non_contiguous=True).then_inc(ends_in, 16)
                sp.wait_ge(tp_used, 2 * VC)
                sp.dma_start(d["meta_table"], meta[:, :, :].rearrange("p b k -> p (b k)")).then_inc(begins_out, 16)
                sp.wait_ge(table_ready, 1)
                sp.dma_start(d["row_table"], table[:, :]).then_inc(begins_out, 16)
                sp.wait_ge(begins_out, 48)
                sp.wait_ge(ends_in, 48)

            @block.tensor
            def _(pe):
                pe.wait_ge(step, 1)
                pe.matmul(psum_cnt[:, 0:NB1], core.ones[:, :], cnt[:, :], start=True, stop=True).then_inc(cnt_ps, 1)
                for c in range(VC):
                    pe.wait_ge(split, c + 1)
                    if c >= 2:
                        pe.wait_ge(tp_used, 2 * (c - 1))
                    pe.transpose(tp[c % 2][:, 0, :], src_f[:, c, :], core.ident[:, :])
                    pe.transpose(tp[c % 2][:, 1, :], loc_f[:, c, :], core.ident[:, :]).then_inc(tp_done, 1)

            @block.scalar
            def _(act):
                for c in range(VC):
                    act.wait_ge(tp_done, c + 1)
                    batches = meta[:, c * P // BATCH:(c + 1) * P // BATCH, :]
                    act.copy(batches[:, :, 0:BATCH], tp[c % 2][:, 0, :].rearrange("p (b v) -> p b v", v=BATCH)
                             ).then_inc(tp_used, 1)
                    act.copy(batches[:, :, BATCH:].bitcast(F32),
                             tp[c % 2][:, 1, :].rearrange("p (b v) -> p b v", v=BATCH)).then_inc(tp_used, 1)

            @block.vector
            def _(dve):
                done = [0]
                chain = core.sem("r_chain")

                def then(ins):
                    done[0] += 1
                    ins.then_inc(chain, 1)
                    dve.wait_ge(chain, done[0])

                dve.wait_ge(iotas, 2)
                dve.wait_ge(first_in, 32)
                dve.tensor_copy(bound[:, :], bound_i[:, :])
                dve.tensor_copy(visit[:, :], visit_i[:, :])
                dve.memset(one[:, :], 1.0)
                then(dve.tensor_copy(firstf[:, :], first[:, :]))
                then(dve.tensor_tensor(below[:, :, :], firstf[:, :].unsqueeze(1).to_broadcast([P, NB1, full + 1]),
                                       bound[:, :].unsqueeze(2).to_broadcast([P, NB1, full + 1]), ALU.is_lt))
                dve.tensor_reduce(cnt[:, :], below[:, :, :], X, ALU.add).then_inc(step, 1)
                dve.wait_ge(cnt_ps, 1)
                then(dve.tensor_scalar(T[:, :], psum_cnt[:, 0:NB1], -1.0, 0.0, ALU.add, ALU.max))
                then(dve.tensor_tensor(size[:, :], T[:, 1:NB1], T[:, 0:BLOCKS], ALU.subtract))
                then(dve.tensor_scalar(size_i[:, :], size[:, :], float(GV), None, ALU.add))
                then(dve.tensor_scalar(size_q[:, :], size_i[:, :], 2, None, ALU.arith_shift_right))
                then(dve.tensor_copy(size[:, :], size_q[:, :]))
                then(dve.tensor_tensor_scan(gend[:, :], one[:, :], size[:, :], 0.0, ALU.mult, ALU.add))
                then(dve.tensor_tensor(v0[:, :], gend[:, :], size[:, :], ALU.subtract))
                then(dve.tensor_scalar(v0[:, :], v0[:, :], float(GV), None, ALU.mult))
                then(dve.tensor_tensor(rel[:, :], T[:, 0:BLOCKS], v0[:, :], ALU.subtract))
                dve.memset(steps[:, 0, 0:1], 0.0)
                dve.memset(steps[:, 0, 1:BLOCKS], 1.0)
                dve.tensor_copy(steps[:, 1, 0:1], rel[:, 0:1])
                dve.tensor_tensor(steps[:, 1, 1:BLOCKS], rel[:, 1:BLOCKS], rel[:, 0:BLOCKS - 1], ALU.subtract)
                dve.tensor_copy(steps[:, 2, 0:1], T[:, 1:2])
                dve.tensor_tensor(steps[:, 2, 1:BLOCKS], T[:, 2:NB1], T[:, 1:BLOCKS], ALU.subtract)
                then(dve.tensor_tensor(ge[:, :, :], visit[:, :].unsqueeze(2).to_broadcast([P, VC, BLOCKS]),
                                       v0[:, :].unsqueeze(1).to_broadcast([P, VC, BLOCKS]), ALU.is_ge))
                for n, out in enumerate((vb, vt, vend)):
                    then(dve.tensor_tensor(tmp[:, :, :], ge[:, :, :],
                                           steps[:, n, :].unsqueeze(1).to_broadcast([P, VC, BLOCKS]), ALU.mult))
                    then(dve.tensor_reduce(out[:, :], tmp[:, :, :], X, ALU.add))
                then(dve.tensor_tensor(vt[:, :], vt[:, :], visit[:, :], ALU.add))
                then(dve.tensor_tensor(ok[:, :], vt[:, :], vend[:, :], ALU.is_le))
                then(dve.tensor_scalar(vt[:, :], vt[:, :], -float(PAD_TILE), None, ALU.add))
                then(dve.tensor_tensor(vt[:, :], vt[:, :], ok[:, :], ALU.mult))
                then(dve.tensor_copy(block_i[:, :], vb[:, :]))
                dve.tensor_scalar(vb[:, :], vb[:, :], float(P), None, ALU.mult)
                dve.tensor_scalar(tile_i[:, :], vt[:, :], float(PAD_TILE), None, ALU.add).then_inc(tile_ready, 1)
                dve.wait_ge(tile_ready, 1)
                dve.wait_ge(rows_in, 16 * VC)
                dve.tensor_copy(src_f[:, :, :], rows[:, :, 0:P])
                then(dve.tensor_copy(dst_f[:, :, :], rows[:, :, P:2 * P]))
                for c in range(VC):
                    dve.tensor_scalar(loc_f[:, c, :], dst_f[:, c, :], vb[:, c:c + 1], None,
                                      ALU.subtract).then_inc(split, 1)
                dve.wait_ge(split, VC)
                dve.tensor_scalar(dst_f[:, :, :], dst_f[:, :, :], 1.0, None, ALU.add)
                dve.tensor_scalar(below_end[:, :, :], loc_f[:, :, :], float(P), None, ALU.is_lt)
                then(dve.tensor_scalar(inside[:, :, :], loc_f[:, :, :], 0.0, None, ALU.is_ge))
                then(dve.tensor_tensor(inside[:, :, :], inside[:, :, :], below_end[:, :, :], ALU.mult))
                then(dve.tensor_tensor(dst_f[:, :, :], dst_f[:, :, :], inside[:, :, :], ALU.mult))
                then(dve.tensor_scalar(dst_f[:, :, :], dst_f[:, :, :], -1.0, None, ALU.add))
                dve.tensor_copy(ends[:, :, 0:1], dst_f[:, :, 0:1])
                dve.tensor_copy(ends[:, :, 1:2], dst_f[:, :, P - 1:P])
                dve.tensor_copy(ends[:, :, 2:3], loc_f[:, :, 0:1])
                dve.memset(before[:, :], -2.0)
                dve.memset(begins[:, :, 0:1], -BIG)
                dve.memset(begins[:, :, P:P + 1], -BIG)
                then(dve.tensor_tensor(begins[:, :, 1:P], dst_f[:, :, 1:P], dst_f[:, :, 0:P - 1], ALU.not_equal))
                dve.tensor_scalar(begins[:, :, 1:P], begins[:, :, 1:P], -BIG, None, ALU.mult).then_inc(ends_ready, 1)
                dve.wait_ge(ends_in, 48)
                span = HEADS * (BATCH + 1)
                dve.memset(table[:, :], 0.0)
                dve.memset(enter[:, BATCH:], 0.0)
                dve.tensor_tensor(enter[:, 0:BATCH], this[:, :, 0], prev[:, :, 1], ALU.not_equal)
                then(dve.tensor_tensor(many[:, :], this[:, :, 0], this[:, :, 1], ALU.not_equal))
                dve.tensor_scalar(table[:, 2 * span + 2 * BATCH:2 * span + 2 * BATCH + 1], enter[:, 0:1], -1.0, 1.0,
                                  ALU.mult, ALU.add)
                then(dve.tensor_copy(table[:, 2 * span + 2 * BATCH + 1:], this[:, 0, 2:3]))
                then(dve.tensor_scalar(enter[:, :], enter[:, :], -BIG, None, ALU.mult))
                then(dve.tensor_scalar(many[:, :], many[:, :], -BIG, None, ALU.mult))
                dve.tensor_copy(table[:, 2 * span:2 * span + BATCH], enter[:, 0:BATCH])
                dve.tensor_copy(table[:, 2 * span + BATCH:2 * span + 2 * BATCH], enter[:, 1:BATCH + 1])
                dve.tensor_tensor(through[:, 0, :], enter[:, 0:BATCH], many[:, :], ALU.min)
                then(dve.tensor_tensor(through[:, 1, :], enter[:, 1:BATCH + 1], many[:, :], ALU.min))
                for way in range(2):
                    part = table[:, way * span:(way + 1) * span].rearrange("b (h v) -> b h v", h=HEADS)
                    edge = 0 if way == 0 else BATCH
                    dve.memset(part[:, :, edge:edge + 1], -BIG)
                    ins = dve.tensor_copy(part[:, :, 1 - way:BATCH + 1 - way],
                                          through[:, way, :].unsqueeze(1).to_broadcast([BATCHES, HEADS, BATCH]))
                ins.then_inc(table_ready, 1)


def need(eng, sem, count):
    if not isinstance(count, int) or count > 0:
        eng.wait_ge(sem, count)


def batches(eng, body):
    loops = (BATCHES - 4) // 2

    def peeled(B):
        body(lambda k, off=0: k * B + off, B // 2, B % 2, B)

    for B in (0, 1):
        peeled(B)
    with eng.Fori(0, loops) as i:
        for c in range(2):
            body(lambda k, off=0: i * (2 * k) + ((2 + c) * k + off), i + 1, c, None)
    for B in range(2 + 2 * loops, BATCHES + 2):
        peeled(B)


def has(B, n, off):
    return B is None or 0 <= STEPS * B + n + off < STEPS * BATCHES


def phase_attention(nc, core, d):
    GROUP_STEPS = GV // 2
    SPAN = HEADS * (BATCH + 1)
    with ExitStack() as st:
        sb, ps = tensors(nc, st)
        kv_ring = sb("a_kv_ring", [P, 2 * RING_STEPS, 2 * D], F32)
        meta = sb("a_meta", [P, 2, 2 * BATCH], I32)
        begins = sb("a_begins", [P, 2, P + 1], F32)
        rows = sb("a_rows", [1, ROWTAB], F32)
        local = sb("a_local", [P, 2, BATCH], F32)
        onehot = sb("a_onehot", [P, 2, 2, P], BF16)
        onehotT = sb("a_onehotT", [P, 2, 2, P], BF16)
        onehot32 = sb("a_onehot32", [P, 2, 2, P], F32)
        prod = sb("a_prod", [P, 2, 2 * D], F32)
        att = sb("a_att", [P, 2, BATCH * HEADS], F32)
        scratch = sb("a_scratch", [P, 2 * SPAN], F32)
        fwd, diff = scratch[:, 0:P], scratch[:, P:2 * P]
        segmax = sb("a_segmax", [P, P], F32)
        ends = sb("a_ends", [1, 2, SPAN], F32)
        chain = scratch[0:1, :].rearrange("o (w k) -> o w k", w=2)
        carry = sb("a_carry", [1, 2, P], F32)
        drop = sb("a_drop", [1, 2, HEADS], F32)

        tp = [ps(f"a_tp{i}", [P, 8, P], BF16) for i in range(2)]
        q_edge = [ps(f"a_q_edge{i}", [P, 2 * D], F32) for i in range(2)]
        acc_ps = ps("a_acc", [P, 512], F32)
        turn = ps("a_turn", [P, 512], F32)
        small = ps("a_small", [P, 512], F32)
        p_ps = ps("a_p", [P, 512], F32)
        FIRST, CARRY, SCALES = 128, 256, 272

        row_in = [core.sem(f"a_row_in{i}") for i in range(RING_STEPS)]
        meta_in = [core.sem(f"a_meta_in{i}") for i in range(2)]
        begins_in = [core.sem(f"a_begins_in{i}") for i in range(2)]
        local_in = [core.sem(f"a_local_in{i}") for i in range(2)]
        rows_in = core.sem("a_rows_in")
        onehot_done, tp_done, onehotT_done, q_edge_done, prod_done, att_done, onehot32_done, pv_done, mm_done = (
            core.sem("a_" + n) for n in ("onehot", "tp", "onehotT", "q_edge", "prod", "att", "onehot32", "pv", "mm"))
        acc_done = core.sem("a_acc_done")
        turned, segmax_done, ends_done, carry_done, carried, diff_done, diff_turned, p_done, p_col_done = (
            core.sem("a_" + n) for n in ("turned", "segmax", "ends", "carry", "carried", "diff", "diff_turned", "p",
                                         "p_col"))
        own, scaled = core.sem("a_own"), core.sem("a_scaled")
        OWN = 6

        with nc.Block() as block:
            @block.sync
            def _(sp):
                def batch(at, rounds, c, B):
                    if has(B, 0, 0):
                        need(sp, prod_done, at(STEPS, -STEPS))
                        sp.dma_start(meta[:, c, :], d["meta_table"][:, bass.ds(at(2 * BATCH), 2 * BATCH)]
                                     ).then_inc(meta_in[c], 16)
                    if has(B, 0, -STEPS):
                        need(sp, carry_done, at(1, -1))
                        sp.dma_start(rows[:, :], d["row_table"][bass.ds(at(1, -1), 1), :]).then_inc(rows_in, 16)
                    if has(B, 0, 0):
                        need(sp, diff_done, at(1, -1))
                        sp.dma_start(begins[:, c, :], d["begins_table"][bass.ds(at(BATCH), BATCH), :].unsqueeze(1)
                                     .to_broadcast([BATCH, HEADS, P + 1])).then_inc(begins_in[c], 16)
                    if has(B, 0, -STEPS):
                        need(sp, onehot32_done, at(STEPS, -2 * STEPS))
                        sp.dma_start(local[:, 1 - c, :], d["meta_table"][:, bass.ds(at(2 * BATCH, -BATCH), BATCH)]
                                     .bitcast(F32)).then_inc(local_in[1 - c], 16)

                batches(sp, batch)

            @block.gpsimd
            def _(pool):
                last_row = pool.to_reg(ROWS - 1)

                def batch(at, rounds, c, B):
                    if not has(B, 0, 0):
                        return
                    need(pool, meta_in[c], 16 * (rounds + 1))
                    for n in range(STEPS):
                        slot = c * STEPS + n
                        need(pool, mm_done, at(STEPS, n - RING_STEPS + 1))
                        wait_here(pool, core)
                        for u in range(2):
                            pool.indirect_dma_start(
                                kv_ring[:, 2 * slot + u, :], None, d["kv_table"],
                                bass.IndirectOffsetOnAxis(ap=meta[:, c, 2 * n + u:2 * n + u + 1], axis=0),
                                bounds_check=last_row, oob_is_err=False).then_inc(row_in[slot], 16)

                batches(pool, batch)

            @block.vector
            def _(dve):
                def one_hots(at, rounds, c, n, B, ahead):
                    if not has(B, n, ahead):
                        return
                    if n + ahead >= STEPS:
                        rounds, c = (rounds + 1 if c else rounds), 1 - c
                    need(dve, meta_in[c], 16 * (rounds + 1))
                    need(dve, tp_done, at(STEPS, n + ahead - 1))
                    m = (n + ahead) % STEPS
                    receiver = meta[:, c, BATCH + 2 * m:BATCH + 2 * m + 2].bitcast(F32)
                    for u in range(2):
                        ins = dve.tensor_scalar(onehot[:, m % 2, u, :], core.iota_bf[:, :],
                                                receiver[:, u:u + 1], None, ALU.is_equal)
                    ins.then_inc(onehot_done, 1)

                def product(at, rounds, c, n, B):
                    if not has(B, n, 0):
                        return
                    h, slot = n % 2, c * STEPS + n
                    need(dve, att_done, at(STEPS, n - 1))
                    need(dve, row_in[slot], 32 * (rounds + 1))
                    need(dve, q_edge_done, at(STEPS, n + 1))
                    dve.tensor_tensor(prod[:, h, :].rearrange("p (u k) -> p u k", u=2),
                                      q_edge[h][:, :].rearrange("p (u k) -> p u k", u=2),
                                      kv_ring[:, 2 * slot:2 * slot + 2, 0:D], ALU.mult).then_inc(prod_done, 1)

                def score(at, c, n, B):
                    if not has(B, n, -1):
                        return
                    m = (n - 1) % STEPS
                    cc = c if n else 1 - c
                    need(dve, prod_done, at(STEPS, n))
                    dve.tensor_reduce(att[:, cc, m * 2 * HEADS:(m + 1) * 2 * HEADS],
                                      prod[:, m % 2, :].rearrange("p (g k) -> p g k", k=DH), X,
                                      ALU.add).then_inc(att_done, 1)

                def in_visit_scans(pen, source, own_count):
                    dve.tensor_tensor_scan(fwd[:, :], pen[:, 0:P], source, -BIG, ALU.add, ALU.max).then_inc(own, 1)
                    dve.wait_ge(own, own_count)
                    return dve.tensor_tensor_scan(segmax[:, ::-1], pen[:, 1:P + 1][:, ::-1], fwd[:, ::-1], -BIG,
                                                  ALU.add, ALU.max)

                def maxima(at, rounds, c, n, B):
                    if n not in (1, 2, 3) or not has(B, 0, -STEPS):
                        return
                    rounds, c = (rounds if c else (rounds - 1)), 1 - c
                    pen, row = begins[:, c, :], rows
                    owned = lambda k: at(OWN, k - OWN)
                    if n == 1:
                        need(dve, turned, at(1))
                        need(dve, begins_in[c], 16 * (rounds + 1))
                        in_visit_scans(pen, turn[:, 0:P], owned(1)).then_inc(segmax_done, 1)
                    elif n == 2:
                        need(dve, ends_done, at(1))
                        need(dve, rows_in, at(16))
                        run = ends[:, 0, :].rearrange("o (h v) -> o h v", h=HEADS)
                        back = ends[:, 1, :].rearrange("o (h v) -> o h v", h=HEADS)
                        dve.tensor_copy(run[:, :, 1:BATCH + 1], small[0:1, 0:P].rearrange("o (v h) -> o h v", h=HEADS))
                        dve.tensor_copy(back[:, :, 0:BATCH], small[0:1, FIRST:FIRST + P]
                                        .rearrange("o (v h) -> o h v", h=HEADS)).then_inc(own, 1)
                        dve.tensor_scalar(att[0:1, c, :], core.iota_bf[0:1, :], row[:, ROWTAB - 1:ROWTAB], None,
                                          ALU.is_equal)
                        dve.wait_ge(own, owned(2))
                        dve.tensor_tensor_scan(chain[:, 0, :], row[:, 0:SPAN], ends[:, 0, :], -BIG, ALU.add, ALU.max)
                        dve.tensor_tensor_scan(chain[:, 1, :][:, ::-1], row[:, SPAN:2 * SPAN][:, ::-1],
                                               ends[:, 1, :][:, ::-1], -BIG, ALU.add, ALU.max).then_inc(own, 1)
                        dve.wait_ge(own, owned(3))
                        by_head = chain[:, :, :].rearrange("o w (h v) -> o w v h", h=HEADS)
                        for way, first in ((0, 0), (1, 1)):
                            enter = row[:, 2 * SPAN + way * BATCH:2 * SPAN + (way + 1) * BATCH]
                            dve.tensor_tensor(carry[:, way, :].rearrange("o (v h) -> o v h", h=HEADS),
                                              by_head[:, way, first:first + BATCH, :],
                                              enter.unsqueeze(2).to_broadcast([1, BATCH, HEADS]), ALU.add)
                        dve.tensor_tensor(drop[:, 0, :], run[:, :, 0], by_head[:, 1, 0, :],
                                          ALU.subtract).then_inc(own, 1)
                        dve.wait_ge(own, owned(4))
                        dve.tensor_copy(run[:, :, 0], by_head[:, 0, BATCH, :])
                        dve.tensor_scalar(drop[:, 1, :], drop[:, 0, :], 0.0, row[:, ROWTAB - 2:ROWTAB - 1], ALU.min,
                                          ALU.mult).then_inc(carry_done, 1)
                    else:
                        need(dve, carried, at(1))
                        for way, e in ((0, 0), (1, P - 1)):
                            col = small[:, CARRY + way:CARRY + way + 1]
                            ins = dve.tensor_tensor(segmax[:, e:e + 1], col, segmax[:, e:e + 1], ALU.max)
                        ins.then_inc(own, 1)
                        dve.wait_ge(own, owned(5))
                        in_visit_scans(pen, segmax[:, :], owned(6)).then_inc(diff_scans, 1)
                        need(dve, diff_scans, at(1))
                        dve.tensor_tensor(diff[:, :], turn[:, 0:P], segmax[:, :], ALU.subtract).then_inc(diff_done, 1)

                diff_scans = core.sem("a_diff_scans")

                def load_block(at, n):
                    return dve.value_load(core.block_of[0:1, bass.ds(at(STEPS // 2, n // 2 - (LAG + 2) // 2), 1)],
                                          min_val=0, max_val=BLOCKS - 1)

                def add_group(at, n, B):
                    if n == 5 and has(B, n, -LAG):
                        blk = dve.value_load(core.block_of[0:1, bass.ds(at(STEPS // 2, -STEPS // 2), 1)],
                                             min_val=0, max_val=BLOCKS - 1)
                        need(dve, acc_done, at(STEPS // 2, -STEPS // 2))
                        need(dve, p_done, at(1))
                        wait_here(dve, core)
                        a = core.acc[:, bass.ds(blk * W, W)]
                        f = p_ps[:, P:P + HEADS]
                        sums, total = a[:, HEADS:W].rearrange("p (h k) -> p h k", h=HEADS), a[:, 0:HEADS]
                        dve.tensor_tensor(total, f, total, ALU.mult)
                        dve.tensor_tensor(sums, f.unsqueeze(2).to_broadcast([P, HEADS, DH]), sums,
                                          ALU.mult).then_inc(scaled, 1)
                    if n % 2 == 0 and has(B, n, -LAG - 1):
                        blk = load_block(at, n)
                        need(dve, mm_done, at(STEPS, n - LAG))
                        need(dve, acc_done, at(STEPS // 2, n // 2 - (LAG + 2) // 2))
                        need(dve, scaled, at(1) if n == 6 else at(1, -1))
                        wait_here(dve, core)
                        a = core.acc[:, bass.ds(blk * W, W)]
                        dve.tensor_tensor(a, acc_ps[:, 0:W], a, ALU.add).then_inc(acc_done, 1)

                def weigh(at, c, n, B):
                    if not has(B, n, -LAG):
                        return
                    slot = (c * STEPS + n - LAG) % RING_STEPS
                    m = slot % STEPS
                    need(dve, p_done, at(1) if n >= 4 else at(1, -1))
                    v = kv_ring[:, 2 * slot:2 * slot + 2, D:2 * D].rearrange("p u (g k) -> p u g k", k=DH)
                    p = p_ps[:, m * 2 * HEADS:(m + 1) * 2 * HEADS].rearrange("p (u g) -> p u g", u=2)
                    dve.tensor_tensor(v, p.unsqueeze(3).to_broadcast([P, 2, HEADS, DH]), v,
                                      ALU.mult).then_inc(pv_done, 1)

                def batch(at, rounds, c, B):
                    for n in range(STEPS):
                        maxima(at, rounds, c, n, B)
                        one_hots(at, rounds, c, n, B, 2)
                        product(at, rounds, c, n, B)
                        score(at, c, n, B)
                        weigh(at, c, n, B)
                        add_group(at, n, B)

                dve.memset(ends[:, :, :], -BIG)
                for n in range(2):
                    one_hots(lambda k, off=0: off, 0, 0, n, 0, 0)
                batches(dve, batch)

            @block.tensor
            def _(pe):
                def turn_one_hots(at, c, n, B, ahead):
                    if not has(B, n, ahead):
                        return
                    s = n + ahead
                    need(pe, onehot_done, at(STEPS, s + 1))
                    need(pe, onehotT_done, at(STEPS, s - 1))
                    for u in range(2):
                        mm = pe.transpose(tp[s % 2][:, u, :], onehot[:, s % 2, u, :], core.ident_bf[:, :])
                    mm.then_inc(tp_done, 1)

                def expand_queries(at, c, n, B, ahead):
                    if not has(B, n, ahead):
                        return
                    s = n + ahead
                    blk = pe.value_load(core.block_of[0:1, bass.ds(at(STEPS // 2, s // GROUP_STEPS), 1)],
                                        min_val=0, max_val=BLOCKS - 1)
                    need(pe, onehotT_done, at(STEPS, s + 1))
                    need(pe, prod_done, at(STEPS, s - 1))
                    for u in range(2):
                        for part in range(3):
                            mm = pe.matmul(q_edge[s % 2][:, u * D:(u + 1) * D], onehotT[:, s % 2, u, :],
                                           core.q_parts[:, bass.ds((blk * 3 + part) * D, D)],
                                           start=(part == 0), stop=(part == 2))
                    mm.then_inc(q_edge_done, 1)

                def sum_values(at, c, n, B):
                    if not has(B, n, -LAG - 1):
                        return
                    r = n - LAG - 1
                    slot = (c * STEPS + r) % RING_STEPS
                    need(pe, pv_done, at(STEPS, r + 1))
                    need(pe, onehot32_done, at(STEPS, r + 1))
                    need(pe, p_col_done, at(1) if n >= 5 else at(1, -1))
                    if r % 2 == 0:
                        need(pe, acc_done, at(STEPS // 2, r // 2))
                    for u in range(2):
                        mm = pe.matmul(acc_ps[:, 0:W], onehot32[:, r % 2, u, :],
                                       kv_ring[:, 2 * slot + u, D - HEADS:2 * D],
                                       start=(r % 2 == 0 and u == 0), stop=(r % 2 == 1 and u == 1))
                    mm.then_inc(mm_done, 1)

                def maxima(at, c, n, B):
                    if not has(B, 0, -STEPS):
                        return
                    if n == 0:
                        need(pe, att_done, at(STEPS))
                        need(pe, p_col_done, at(1, -1))
                        pe.transpose(turn[:, 0:P], att[:, 1 - c, :], core.ident[:, :]).then_inc(turned, 1)
                    elif n == 1:
                        need(pe, segmax_done, at(1))
                        pe.transpose(small[0:1, 0:P], segmax[:, P - 1:P], core.ident[:, :])
                        pe.transpose(small[0:1, FIRST:FIRST + P], segmax[:, 0:1], core.ident[:, :]
                                     ).then_inc(ends_done, 1)
                    elif n == 2:
                        need(pe, carry_done, at(1))
                        wait_here(pe, core)
                        for way in range(2):
                            pe.transpose(small[:, CARRY + way:CARRY + way + 1], carry[0:1, way, :],
                                         core.ident[0:1, 0:1])
                        pe.matmul(small[:, SCALES:SCALES + HEADS], att[0:1, 1 - c, :], drop[0:1, 1, :], start=True,
                                  stop=True).then_inc(carried, 1)
                    elif n == 3:
                        need(pe, diff_done, at(1))
                        pe.transpose(turn[:, 0:P], diff[:, :], core.ident[:, :]).then_inc(diff_turned, 1)

                def batch(at, rounds, c, B):
                    for n in range(STEPS):
                        sum_values(at, c, n, B)
                        expand_queries(at, c, n, B, 1)
                        maxima(at, c, n, B)
                        turn_one_hots(at, c, n, B, 2)

                start = lambda k, off=0: off
                for n in range(2):
                    turn_one_hots(start, 0, n, 0, 0)
                expand_queries(start, 0, 0, 0, 0)
                batches(pe, batch)

            @block.scalar
            def _(act):
                apart = core.sem("a_apart")

                def copy_turned(at, n, B, ahead):
                    if not has(B, n, ahead):
                        return
                    s = n + ahead
                    need(act, tp_done, at(STEPS, s + 1))
                    need(act, q_edge_done, at(STEPS, s - 1))
                    act.copy(onehotT[:, s % 2, :, :], tp[s % 2][:, 0:2, :]).then_inc(onehotT_done, 1)

                def wide_one_hots(at, rounds, c, n, B):
                    if not has(B, n, -LAG):
                        return
                    r = n - LAG
                    slot = (c * STEPS + r) % RING_STEPS
                    c, m = slot // STEPS, slot % STEPS
                    need(act, mm_done, at(STEPS, r - 1))
                    need(act, local_in[c], 16 * (rounds if n >= 4 and c or n < 4 else rounds + 1))
                    for u in range(2):
                        ins = act.activation(onehot32[:, r % 2, u, :], core.iota_bf[:, :], ACT.Abs, scale=-1.0,
                                             bias=local[:, c, 2 * m + u:2 * m + u + 1])
                    ins.then_inc(apart, 1)
                    need(act, apart, at(STEPS, r + 1))
                    act.activation(onehot32[:, r % 2, :, :], onehot32[:, r % 2, :, :], ACT.Relu, scale=-1.0,
                                   bias=core.ones[:, 0:1]).then_inc(onehot32_done, 1)

                def exponentials(at, c, n, B):
                    if n != 3 or not has(B, 0, -STEPS):
                        return
                    need(act, diff_turned, at(1))
                    need(act, pv_done, at(STEPS, -STEPS))
                    need(act, scaled, at(1, -1))
                    act.activation(p_ps[:, 0:P], turn[:, 0:P], ACT.Exp, scale=SCALE)
                    act.activation(p_ps[:, P:P + HEADS], small[:, SCALES:SCALES + HEADS], ACT.Exp, scale=SCALE
                                   ).then_inc(p_done, 1)
                    lo = (1 - c) * BATCH
                    act.activation(kv_ring[:, lo:lo + BATCH, D - HEADS:D],
                                   turn[:, 0:P].rearrange("p (v h) -> p v h", h=HEADS), ACT.Exp, scale=SCALE
                                   ).then_inc(p_col_done, 1)

                def batch(at, rounds, c, B):
                    for n in range(STEPS):
                        wide_one_hots(at, rounds, c, n, B)
                        copy_turned(at, n, B, 2)
                        exponentials(at, c, n, B)

                for n in range(2):
                    copy_turned(lambda k, off=0: off, n, 0, 0)
                batches(act, batch)


def phase_node(nc, core, d):
    with ExitStack() as st:
        sb, ps = tensors(nc, st)
        inv_l = sb("n_inv_l", [P, 2, SB, HEADS], F32)
        x_t = core.tail[:, 0:SB * D].rearrange("p (j k) -> p j k", j=SB)
        ln = core.tail[:, SB * D:3 * SB * D].rearrange("p (r j k) -> p r j k", r=2, j=SB)
        o = ln[:, 1, :, :]
        oT = sb("n_oT", [P, SB, KC, P], F32)
        xnT = oT
        stats = sb("n_stats", [P, 2, SB, 6], F32)
        mv = sb("n_mv", [P, 2, SB, 2], F32)
        std = sb("n_std", [P, 2, SB], F32)
        rstd = sb("n_rstd", [P, 2, SB], F32)
        b_ff = sb("n_b_ff", [P, D], F32)
        wr = sb("n_wr", [P, KC, EXPERTS], F32)
        br = sb("n_br", [P, EXPERTS], F32)
        wffT = sb("n_wffT", [P, KC, D], F32)
        gamma = sb("n_gamma", [P, KC], F32)
        beta = sb("n_beta", [P, KC], F32)
        o_tp = [ps(f"n_o_tp{i}", [P, KC, 256], F32) for i in range(2)]
        yp = [ps(f"n_yp{i}", [P, 512], F32) for i in range(2)]
        z_tp = [ps(f"n_z_tp{i}", [P, KC, 256], F32) for i in range(2)]
        lp = [ps(f"n_lp{i}", [P, 512], F32) for i in range(2)]
        x_in = [core.sem(f"n_x_in{j}") for j in range(SB)]
        par_in = core.sem("n_par_in")
        names = ("lmax", "inv_l", "xb", "o", "o_tp", "oT", "yp", "y1", "stats", "mv", "std", "rstd", "ln",
                 "z_tp", "xnT", "keep", "lp", "logits")
        s = {n: core.sem("n_s_" + n) for n in names}

        def free_slot(eng, sem, n, j):
            eng.wait_ge(sem, n if j == 0 else n - 1)

        def y1_at(n):
            return core.acc[:, bass.ds(n * W + HEADS, D)]

        with nc.Block() as block:
            @block.sync
            def _(sp):
                sp.dma_start(b_ff[:, :], d["b_ff"].partition_broadcast(P)).then_inc(par_in, 16)
                sp.dma_start(br[:, :], d["br"].partition_broadcast(P)).then_inc(par_in, 16)
                sp.dma_start(wffT[:, :, :], d["wff_table"]).then_inc(par_in, 16)
                sp.dma_start(wr[:, :, :], d["Wr"].rearrange("(k p) e -> p k e", p=P)).then_inc(par_in, 16)
                for k in range(KC):
                    for tile, name in ((gamma, "gamma"), (beta, "beta")):
                        sp.dma_start(tile[:, k:k + 1], d[name][k * P:(k + 1) * P].rearrange("(p a) -> p a", a=1)
                                     ).then_inc(par_in, 16)
                with sp.Fori(0, ST) as t:
                    for j in range(SB):
                        sp.wait_ge(s["y1"], t * SB)
                        sp.dma_start(x_t[:, j, :], d["x"][bass.ds((t * SB + j) * P, P), :]).then_inc(x_in[j], 16)
                sp.dma_start(core.w1[:, :, :, :], d["W1"].rearrange("e (k p) h -> p e k h", p=P)
                             ).then_inc(core.w_in, 16)
                sp.dma_start(core.w2[:, :, :, :], d["W2"].rearrange("e (c p) o -> p e c o", p=P)
                             ).then_inc(core.w_in, 16)
                sp.dma_start(core.b2[:, :], d["b2"]).then_inc(core.w_in, 16)
                sp.dma_start(core.b1_rows[:, :], d["b1"].rearrange("e (c p) -> (e c) p", p=P)).then_inc(core.w_in, 16)
                sp.wait_ge(core.w_in, 64)

            @block.gpsimd
            def _(pool):
                pool.wait_ge(par_in, 16 * (4 + 2 * KC))
                with pool.Fori(0, ST) as t:
                    for j in range(SB):
                        n = t * SB + j
                        pool.wait_ge(s["inv_l"], t + 1)
                        pool.wait_ge(s["z_tp"], t * SB)
                        pool.tensor_tensor(
                            o[:, j, :].rearrange("p (h k) -> p h k", k=DH),
                            y1_at(n).rearrange("p (h k) -> p h k", k=DH),
                            inv_l[:, 1, j, :].unsqueeze(2).to_broadcast([P, HEADS, DH]), ALU.mult).then_inc(s["o"], 1)
                    for j in range(SB):
                        pool.wait_ge(x_in[j], 16 * (t + 1))
                        pool.tensor_tensor(x_t[:, j, :], x_t[:, j, :], b_ff[:, :], ALU.add).then_inc(s["xb"], 1)
                    for j in range(SB):
                        n = t * SB + j
                        pool.wait_ge(s["xnT"], n + 1)
                        pool.tensor_copy(core.xnT[:, :, bass.ds(n * P, P)], xnT[:, j, :, :]).then_inc(s["keep"], 1)

            @block.vector
            def _(dve):
                dve.wait_ge(par_in, 16 * (4 + 2 * KC))
                with dve.Fori(0, ST) as t:
                    sums = core.acc[:, bass.ds(t * SB * W, SB * W)].rearrange("p (j w) -> p j w", w=W)[:, :, 0:HEADS]
                    dve.wait_ge(s["o"], t * SB)
                    dve.tensor_scalar(inv_l[:, 0, :, :], sums, 1e-30, None, ALU.max).then_inc(s["lmax"], 1)
                    dve.wait_ge(s["lmax"], t + 1)
                    dve.reciprocal(inv_l[:, 1, :, :], inv_l[:, 0, :, :]).then_inc(s["inv_l"], 1)
                    for j in range(SB):
                        n = t * SB + j
                        dve.wait_ge(s["yp"], n + 1)
                        dve.wait_ge(s["xb"], n + 1)
                        dve.wait_ge(s["o"], n + 1)
                        dve.tensor_tensor(y1_at(n), yp[j % 2][:, 0:D], x_t[:, j, :], ALU.add).then_inc(s["y1"], 1)
                    for r in range(2):
                        for j in range(SB):
                            n = t * SB + j
                            if r == 0:
                                dve.wait_ge(s["y1"], n + 1)
                            else:
                                dve.wait_ge(s["ln"], 2 * t * SB + j + 1)
                            wait_here(dve, core)
                            dve.bn_stats(stats[:, r, j, :], ln[:, 0, j, :] if r else y1_at(n)).then_inc(s["stats"], 1)
                        for j in range(SB):
                            dve.wait_ge(s["stats"], (2 * t + r) * SB + j + 1)
                            wait_here(dve, core)
                            dve.bn_aggr(mv[:, r, j, :], stats[:, r, j, :]).then_inc(s["mv"], 1)
                        for j in range(SB):
                            dve.wait_ge(s["std"], (2 * t + r) * SB + j + 1)
                            dve.reciprocal(rstd[:, r, j:j + 1], std[:, r, j:j + 1]).then_inc(s["rstd"], 1)
                        for j in range(SB):
                            n = t * SB + j
                            dve.wait_ge(s["rstd"], (2 * t + r) * SB + j + 1)
                            if r == 1:
                                dve.wait_ge(s["z_tp"], t * SB)
                            dve.tensor_scalar(ln[:, r, j, :], ln[:, 0, j, :] if r else y1_at(n),
                                              mv[:, r, j, 0:1], rstd[:, r, j:j + 1], ALU.subtract,
                                              ALU.mult).then_inc(s["ln"], 1)
                    for j in range(SB):
                        n = t * SB + j
                        dve.wait_ge(s["lp"], n + 1)
                        dve.tensor_tensor(core.logits[:, bass.ds(n, 1), :].rearrange("p a e -> p (a e)"),
                                          lp[j % 2][:, 0:EXPERTS], br[:, :], ALU.add).then_inc(s["logits"], 1)

            @block.scalar
            def _(act):
                act.wait_ge(par_in, 16 * (4 + 2 * KC))
                with act.Fori(0, ST) as t:
                    for j in range(SB):
                        n = t * SB + j
                        act.wait_ge(s["o_tp"], n + 1)
                        act.wait_ge(s["keep"], t * SB)
                        act.wait_ge(s["lp"], t * SB)
                        act.copy(oT[:, j, :, :], o_tp[j % 2][:, :, 0:P]).then_inc(s["oT"], 1)
                    for r in range(2):
                        for j in range(SB):
                            act.wait_ge(s["mv"], (2 * t + r) * SB + j + 1)
                            act.activation(std[:, r, j:j + 1], mv[:, r, j, 1:2], ACT.Sqrt,
                                           bias=core.eps[:, :]).then_inc(s["std"], 1)
                    for j in range(SB):
                        n = t * SB + j
                        act.wait_ge(s["z_tp"], n + 1)
                        act.wait_ge(s["yp"], (t + 1) * SB)
                        for k in range(KC):
                            ins = act.activation(xnT[:, j, k, :], z_tp[j % 2][:, k, 0:P], ACT.Identity,
                                                 scale=gamma[:, k:k + 1], bias=beta[:, k:k + 1])
                        ins.then_inc(s["xnT"], 1)

            @block.tensor
            def _(pe):
                pe.wait_ge(par_in, 16 * (4 + 2 * KC))
                with pe.Fori(0, ST) as t:
                    for j in range(SB):
                        n = t * SB + j
                        pe.wait_ge(s["o"], n + 1)
                        free_slot(pe, s["oT"], n, j)
                        for k in range(KC):
                            mm = pe.transpose(o_tp[j % 2][:, k, 0:P], o[:, j, k * P:(k + 1) * P], core.ident[:, :])
                        mm.then_inc(s["o_tp"], 1)
                    for j in range(SB):
                        n = t * SB + j
                        pe.wait_ge(s["oT"], n + 1)
                        free_slot(pe, s["y1"], n, j)
                        for k in range(KC):
                            mm = pe.matmul(yp[j % 2][:, 0:D], oT[:, j, k, :], wffT[:, k, :], start=(k == 0),
                                           stop=(k == KC - 1))
                        mm.then_inc(s["yp"], 1)
                    for j in range(SB):
                        n = t * SB + j
                        pe.wait_ge(s["ln"], (2 * t + 1) * SB + j + 1)
                        free_slot(pe, s["xnT"], n, j)
                        for k in range(KC):
                            mm = pe.transpose(z_tp[j % 2][:, k, 0:P], ln[:, 1, j, k * P:(k + 1) * P],
                                              core.ident[:, :])
                        mm.then_inc(s["z_tp"], 1)
                    for j in range(SB):
                        n = t * SB + j
                        pe.wait_ge(s["xnT"], n + 1)
                        free_slot(pe, s["logits"], n, j)
                        for k in range(KC):
                            mm = pe.matmul(lp[j % 2][:, 0:EXPERTS], xnT[:, j, k, :], wr[:, k, :], start=(k == 0),
                                           stop=(k == KC - 1))
                        mm.then_inc(s["lp"], 1)


def phase_gate(nc, core, d):
    with ExitStack() as st:
        sb, ps = tensors(nc, st)
        iota = sb("g_iota", [P, EXPERTS], I32)
        rank = sb("g_rank", [P, EXPERTS], F32)
        key = sb("g_key", [P, BLOCKS, EXPERTS], F32)
        left = sb("g_left", [P, BLOCKS, EXPERTS], F32)
        mask = sb("g_mask", [P, 2, BLOCKS, EXPERTS], F32)
        top = sb("g_top", [P, 2, BLOCKS], F32)
        best = sb("g_best", [P, BLOCKS], F32)
        diff = sb("g_diff", [P, BLOCKS], F32)
        e2 = sb("g_e2", [P, BLOCKS], F32)
        part = sb("g_part", [P, 2, BLOCKS], F32)
        w_now = sb("g_w_now", [P, SB, EXPERTS], F32)
        wT = sb("g_wT", [EXPERTS, SB, P], F32)
        tp = [ps(f"g_tp{i}", [P, 512], F32) for i in range(2)]
        bp = [ps(f"g_bp{i}", [P, 512], F32) for i in range(2)]
        b1_tp = ps("g_b1_tp", [P, 512], F32)
        iota_done, chain, diff_done, e2_done, w_now_done, tp_done, wT_done, bp_done, y_done, b1_done = (
            core.sem("g_" + n) for n in ("iota", "chain", "diff", "e2", "w_now", "tp", "wT", "bp", "y", "b1"))

        def over_experts(a):
            return a.unsqueeze(2).to_broadcast([P, BLOCKS, EXPERTS])

        with nc.Block() as block:
            @block.gpsimd
            def _(pool):
                pool.iota(iota[:, :], pattern=[[-1, EXPERTS]], base=EXPERTS, channel_multiplier=0
                          ).then_inc(iota_done, 1)

            @block.scalar
            def _(act):
                act.wait_ge(b1_done, 1)
                act.copy(core.b1[:, :], b1_tp[:, 0:EXPERTS * HC])
                act.wait_ge(diff_done, 1)
                act.activation(e2[:, :], diff[:, :], ACT.Exp).then_inc(e2_done, 1)
                with act.Fori(0, ST) as t:
                    for j in range(SB):
                        n = t * SB + j
                        act.wait_ge(tp_done, n + 1)
                        act.wait_ge(bp_done, t * SB)
                        act.copy(wT[:, j, :], tp[j % 2][0:EXPERTS, 0:P]).then_inc(wT_done, 1)

            @block.tensor
            def _(pe):
                pe.transpose(b1_tp[:, 0:EXPERTS * HC], core.b1_rows[:, :],
                             core.ident[0:EXPERTS * HC, 0:EXPERTS * HC]).then_inc(b1_done, 1)
                with pe.Fori(0, ST) as t:
                    for j in range(SB):
                        n = t * SB + j
                        pe.wait_ge(w_now_done, t + 1)
                        pe.wait_ge(wT_done, n if j == 0 else n - 1)
                        pe.transpose(tp[j % 2][0:EXPERTS, 0:P], w_now[:, j, :], core.ident[:, :]
                                     ).then_inc(tp_done, 1)
                    for j in range(SB):
                        n = t * SB + j
                        pe.wait_ge(wT_done, n + 1)
                        pe.wait_ge(y_done, n if j == 0 else n - 1)
                        pe.matmul(bp[j % 2][:, 0:D], wT[:, j, :], core.b2[:, :], start=True, stop=True
                                  ).then_inc(bp_done, 1)

            @block.vector
            def _(dve):
                done = [0]

                def then(ins):
                    done[0] += 1
                    ins.then_inc(chain, 1)
                    dve.wait_ge(chain, done[0])

                dve.wait_ge(iota_done, 1)
                then(dve.tensor_copy(rank[:, :], iota[:, :]))
                for r in range(2):
                    source = left if r else core.logits
                    then(dve.tensor_reduce(top[:, r, :], source[:, :, :], X, ALU.max))
                    then(dve.tensor_tensor(key[:, :, :], source[:, :, :], over_experts(top[:, r, :]), ALU.is_equal))
                    then(dve.tensor_tensor(key[:, :, :], key[:, :, :],
                                           rank[:, :].unsqueeze(1).to_broadcast([P, BLOCKS, EXPERTS]), ALU.mult))
                    then(dve.tensor_reduce(best[:, :], key[:, :, :], X, ALU.max))
                    then(dve.tensor_tensor(mask[:, r, :, :], key[:, :, :], over_experts(best[:, :]), ALU.is_equal))
                    if r == 0:
                        then(dve.scalar_tensor_tensor(out=left[:, :, :], in0=mask[:, 0, :, :], scalar=-BIG,
                                                      in1=core.logits[:, :, :], op0=ALU.mult, op1=ALU.add))
                dve.tensor_tensor(diff[:, :], top[:, 1, :], top[:, 0, :], ALU.subtract).then_inc(diff_done, 1)
                dve.wait_ge(e2_done, 1)
                then(dve.tensor_scalar(best[:, :], e2[:, :], 1.0, None, ALU.add))
                then(dve.reciprocal(part[:, 0, :], best[:, :]))
                then(dve.tensor_tensor(part[:, 1, :], e2[:, :], part[:, 0, :], ALU.mult))
                for r in range(2):
                    then(dve.tensor_tensor(mask[:, r, :, :], mask[:, r, :, :], over_experts(part[:, r, :]),
                                           ALU.mult))
                then(dve.tensor_tensor(core.gate[:, :, :], mask[:, 0, :, :], mask[:, 1, :, :], ALU.add))
                with dve.Fori(0, ST) as t:
                    dve.wait_ge(tp_done, t * SB)
                    dve.tensor_copy(w_now[:, :, :], core.gate[:, bass.ds(t * SB, SB), :]).then_inc(w_now_done, 1)
                    for j in range(SB):
                        n = t * SB + j
                        dve.wait_ge(bp_done, n + 1)
                        y = core.acc[:, bass.ds(n * W + HEADS, D)]
                        dve.tensor_tensor(y, bp[j % 2][:, 0:D], y, ALU.add).then_inc(y_done, 1)


def phase_experts(nc, core, d):
    HALF = SB * P // 2
    assert HALF <= 512 and (EXPERTS * SB) % 4 == 0
    with ExitStack() as st:
        sb, ps = tensors(nc, st)
        hT = [sb("e_hT", [P, HC, SB * P], F32),
              core.tail[:, 0:HC * SB * P].rearrange("p (c n) -> p c n", c=HC)]
        hp = [ps(f"e_hp{i}", [P, 2, 512], F32) for i in range(2)]
        yp = [ps(f"e_yp{i}", [P, 512], F32) for i in range(4)]
        hp_done, gelu_done, yp_done, y_done, out_done = (core.sem("e_" + n) for n in
                                                         ("hp", "gelu", "yp", "y", "out"))
        with nc.Block() as block:
            @block.tensor
            def _(pe):
                pe.sem_inc(yp_done, 2 * SB)

                def up(t, e):
                    for c in range(HC):
                        m = (t * EXPERTS + e) * HC + c
                        pe.wait_ge(gelu_done, m + 1)
                        for half in range(2):
                            for k in range(KC):
                                mm = pe.matmul(hp[c % 2][:, half, 0:HALF], core.w1[:, e, k, c * P:(c + 1) * P],
                                               core.xnT[:, k, bass.ds(t * SB * P + half * HALF, HALF)],
                                               start=(k == 0), stop=(k == KC - 1))
                        mm.then_inc(hp_done, 1)

                def down(t, e):
                    pe.wait_ge(gelu_done, (t * EXPERTS + e + 1) * HC + 2)
                    for j in range(SB):
                        r = (t * EXPERTS + e) * SB + j
                        slot = (e * SB + j) % 4
                        pe.wait_ge(y_done, r + 1)
                        for c in range(HC):
                            mm = pe.matmul(yp[slot][:, 0:D], hT[e % 2][:, c, j * P:(j + 1) * P],
                                           core.w2[:, e, c, :], start=(c == 0), stop=(c == HC - 1))
                        mm.then_inc(yp_done, 1)

                with pe.Fori(0, ST) as t:
                    up(t, 0)
                    for e in range(EXPERTS):
                        if e + 1 < EXPERTS:
                            up(t, e + 1)
                        down(t, e)

            @block.scalar
            def _(act):
                act.sem_inc(gelu_done, 2)
                with act.Fori(0, ST) as t:
                    for e in range(EXPERTS):
                        for c in range(HC):
                            m = (t * EXPERTS + e) * HC + c
                            act.wait_ge(hp_done, m + 1)
                            if c == 0:
                                act.wait_ge(yp_done, (t * EXPERTS + e + 1) * SB)
                            act.activation(hT[e % 2][:, c, :].rearrange("p (a n) -> p a n", a=2),
                                           hp[c % 2][:, :, 0:HALF], ACT.Gelu,
                                           bias=core.b1[:, e * HC + c:e * HC + c + 1]).then_inc(gelu_done, 1)

            @block.vector
            def _(dve):
                dve.sem_inc(y_done, 4)
                with dve.Fori(0, ST) as t:
                    for e in range(EXPERTS):
                        for j in range(SB):
                            n, r = t * SB + j, (t * EXPERTS + e) * SB + j
                            dve.wait_ge(yp_done, r + 1 + 2 * SB)
                            if e:
                                dve.wait_ge(y_done, r - SB + 1 + 4)
                            y = core.acc[:, bass.ds(n * W + HEADS, D)]
                            gate = core.gate[:, bass.ds(n, 1), e]
                            dve.scalar_tensor_tensor(out=y, in0=yp[(e * SB + j) % 4][:, 0:D], scalar=gate, in1=y,
                                                     op0=ALU.mult, op1=ALU.add).then_inc(y_done, 1)

            @block.sync
            def _(sp):
                with sp.Fori(0, ST) as t:
                    sp.wait_ge(y_done, (t + 1) * EXPERTS * SB + 4)
                    sp.dma_start(d["out"][bass.ds(t * SB * P, SB * P), :].rearrange("(j p) c -> p j c", p=P),
                                 core.acc[:, bass.ds(t * SB * W, SB * W)].rearrange("p (j w) -> p j w", w=W)[:, :, HEADS:W]
                                 ).then_inc(out_done, 16)
                sp.wait_ge(out_done, 16 * ST)


def build(nc, d):
    with ExitStack() as st:
        core = Core(nc, st)
        sb, ps = tensors(nc, st)
        core.ident = sb("ident", [P, P], F32)
        core.ident_bf = sb("ident_bf", [P, P], BF16)
        core.iota_bf = sb("iota_bf", [P, P], BF16)
        core.ones = sb("ones", [P, P], F32)
        core.eps = sb("eps", [P, 1], F32)
        core.w_in = core.sem("w_in")
        core.waited = core.sem("waited")
        core.acc = sb("acc", [P, BLOCKS * W], F32)
        with ExitStack() as edge_life:
            sbe, _ = tensors(nc, edge_life)
            core.q_parts = sbe("q_parts", [P, BLOCKS * 3 * D], BF16)
            core.block_of = sbe("block_of", [1, GROUPS], I32)
            with ExitStack() as w_life:
                sbw, _ = tensors(nc, w_life)
                core.wqkvT = sbw("wqkvT", [P, KC, 3 * D], F32)
                core.b_qkv = sbw("b_qkv", [P, 3 * D], F32)
                phase_constants(nc, core, d)
                phase_project(nc, core, d)
            phase_route(nc, core, d)
            phase_attention(nc, core, d)
        core.xnT = sb("xnT", [P, KC, ROWS], F32)
        core.tail = sb("tail", [P, max(3 * SB * D, HC * SB * P)], F32)
        core.gate = sb("gate", [P, BLOCKS, EXPERTS], F32)
        core.w1 = sb("w1", [P, EXPERTS, KC, HID], F32)
        core.w2 = sb("w2", [P, EXPERTS, HC, D], F32)
        core.b1 = sb("b1", [P, EXPERTS * HC], F32)
        with ExitStack() as gate_life:
            sbg, _ = tensors(nc, gate_life)
            core.logits = sbg("logits", [P, BLOCKS, EXPERTS], F32)
            core.b2 = sbg("b2", [EXPERTS, D], F32)
            core.b1_rows = sbg("b1_rows", [EXPERTS * HC, P], F32)
            phase_node(nc, core, d)
            phase_gate(nc, core, d)
        phase_experts(nc, core, d)


def dram_tables(nc, d):
    for name, shape, dt in (("kv_table", (ROWS, 2 * D), F32), ("ends_table", (VPAD + 1, 3), F32),
                            ("begins_table", (VPAD, P + 1), F32), ("row_table", (BATCHES, ROWTAB), F32),
                            ("wff_table", (P, KC, D), F32), ("block_table", (VPAD,), I32), ("meta_table", (P, HOLD * 2 * BATCH), I32)):
        d[name] = nc.dram_tensor(name, shape, dt).ap()


_WEIGHTS = {"W_qkv": "L0_gnn_W_qkv", "b_qkv": "L0_gnn_b_qkv", "W_ff": "L0_gnn_W_ff", "b_ff": "L0_gnn_b_ff",
            "gamma": "L0_ffn_gamma", "beta": "L0_ffn_beta", "Wr": "L0_ffn_Wr", "br": "L0_ffn_br",
            "W1": "L0_ffn_W1", "b1": "L0_ffn_b1", "W2": "L0_ffn_W2", "b2": "L0_ffn_b2"}


def kernel(**inputs):
    import numpy as np
    import concourse.bacc as bacc
    from concourse.bass_utils import run_bass_kernel_spmd

    x = np.zeros((ROWS, D), np.float32)
    x[:NODES] = inputs["x"]
    edges = np.zeros((2, (TILES + 1) * P), np.int32)
    edges[1] = -1
    edges[0, :EDGES] = inputs["src"]
    edges[1, :EDGES] = inputs["dst"]
    edges = np.ascontiguousarray(edges.reshape(2, TILES + 1, P).transpose(1, 0, 2)).reshape(TILES + 1, 2 * P)
    arrays = {"x": x, "edges": edges}
    for name, given in _WEIGHTS.items():
        arrays[name] = np.ascontiguousarray(inputs[given])

    nc = bacc.Bacc("TRN2", target_bir_lowering=False, num_devices=1)
    d = {name: nc.dram_tensor("in_" + name, a.shape, mybir.dt.from_np(a.dtype), kind="ExternalInput").ap()
         for name, a in arrays.items()}
    dram_tables(nc, d)
    d["out"] = nc.dram_tensor("out", (ROWS, D), F32, kind="ExternalOutput").ap()
    build(nc, d)
    got = run_bass_kernel_spmd(nc, [{"in_" + name: a for name, a in arrays.items()}], core_ids=[0])
    return got.results[0]["out"][:NODES]
```

```python
from contextlib import ExitStack

import concourse.bass as bass
from concourse import mybir

ALU = mybir.AluOpType
ACT = mybir.ActivationFunctionType
F32 = mybir.dt.float32
BF16 = mybir.dt.bfloat16
I32 = mybir.dt.int32
X = mybir.AxisListType.X

P = 128
NODES = 6250
EDGES = 200000
D = 256
HEADS = 8
DH = D // HEADS
KC = D // P
BLOCKS = -(-NODES // P)
ROWS = BLOCKS * P
TILES = -(-EDGES // P)
PAD_TILE = TILES
GV = 4
GROUPS = -(-((TILES + BLOCKS - 1 + BLOCKS * (GV - 1)) // GV) // 4) * 4
VISITS = GROUPS * GV
VC = -(-(VISITS + 8) // P)
VPAD = VC * P
BATCH = 16
BATCHES = VISITS // BATCH
STEPS = BATCH // 2
RING_STEPS = 2 * STEPS
LAG = STEPS + STEPS // 2
W = HEADS + D
HOLD = VPAD // BATCH
ROWTAB = 2 * HEADS * (BATCH + 1) + 2 * BATCH + 2
BIG = 1.0e30
SB = 7
ST = BLOCKS // SB
EXPERTS = 8
HID = 512
HC = HID // P
EPS = 1e-5
TOP = 2
PAIR = 2 * P
PAIRS = (ROWS * TOP + EXPERTS * (PAIR - 1)) // PAIR
PLACES = 2 * PAIRS
NOWHERE = 1 << 20
SCALE = float(DH) ** -0.5
assert ST * SB == BLOCKS and VISITS % (2 * BATCH) == 0 and D == HEADS * DH and PAIRS % 2 == 0


class Core:

    def __init__(self, nc, stack):
        self.nc = nc
        self.stack = stack

    def sem(self, name):
        return self.stack.enter_context(self.nc.semaphore(name))


def wait_here(eng, core):
    eng.sem_inc(core.waited, 1)


def need(eng, sem, count):
    if not isinstance(count, int) or count > 0:
        eng.wait_ge(sem, count)


def rounds(eng, first, second):
    first(0)
    first(1)
    second(0)
    with eng.Fori(0, ST - 2) as i:
        first(i + 2)
        second(i + 1)
    second(ST - 1)


def tensors(nc, stack):
    def sb(name, shape, dt):
        return stack.enter_context(nc.sbuf_tensor(name, shape, dt))

    def ps(name, shape, dt):
        return stack.enter_context(nc.psum_tensor(name, shape, dt))
    return sb, ps


def phase_constants(nc, core, d):
    with ExitStack() as st:
        sb, ps = tensors(nc, st)
        diag = sb("diag", [P, P], I32)
        iota_i = sb("iota_i", [P, P], I32)
        wq_rows = sb("wq_rows", [P, 3 * KC, D], F32)
        wf_rows = sb("wf_rows", [P, KC, D], F32)
        wffT = sb("wffT_first", [P, KC, D], F32)
        tp = ps("tp_w", [P, 4, 512], F32)
        iota_done, ident_done = core.sem("c_iota"), core.sem("c_ident")
        w_in, tp_done, tp_used, small_in = (core.sem(n) for n in ("c_w_in", "c_tp", "c_tp_used", "c_small"))
        with nc.Block() as block:
            @block.gpsimd
            def _(pool):
                pool.iota(diag[:, :], pattern=[[1, P]], base=0, channel_multiplier=-1).then_inc(iota_done, 1)
                pool.iota(iota_i[:, :], pattern=[[1, P]], base=0, channel_multiplier=0).then_inc(iota_done, 1)
                pool.memset(core.acc[:, :], 0.0)

            @block.sync
            def _(sp):
                sp.dma_start(wq_rows[:, :, :], d["W_qkv"].rearrange("(c p) k -> p c k", p=P)).then_inc(w_in, 16)
                sp.dma_start(wf_rows[:, :, :], d["W_ff"].rearrange("(c p) k -> p c k", p=P)).then_inc(w_in, 16)
                sp.dma_start(core.b_qkv[:, :], d["b_qkv"].partition_broadcast(P)).then_inc(small_in, 16)
                sp.wait_ge(small_in, 16)
                sp.wait_ge(tp_used, (3 * KC + KC) * KC)
                sp.dma_start(d["wff_table"], wffT[:, :, :]).then_inc(small_in, 16)
                sp.wait_ge(small_in, 32)

            @block.vector
            def _(dve):
                dve.wait_ge(iota_done, 2)
                dve.tensor_scalar(core.ident[:, :], diag[:, :], 0.0, None, ALU.is_equal)
                dve.tensor_scalar(core.ident_bf[:, :], diag[:, :], 0.0, None, ALU.is_equal)
                dve.tensor_copy(core.iota_bf[:, :], iota_i[:, :])
                dve.memset(core.ones[:, :], 1.0)
                dve.memset(core.eps[:, :], EPS).then_inc(ident_done, 1)

            def weight_chunks():
                for c in range(3 * KC):
                    for k in range(KC):
                        yield wq_rows[:, c, k * P:(k + 1) * P], core.wqkvT[:, k, c * P:(c + 1) * P]
                for c in range(KC):
                    for k in range(KC):
                        yield wf_rows[:, c, k * P:(k + 1) * P], wffT[:, k, c * P:(c + 1) * P]

            @block.tensor
            def _(pe):
                pe.wait_ge(ident_done, 1)
                pe.wait_ge(w_in, 32)
                for n, (src, _) in enumerate(weight_chunks()):
                    if n >= 4:
                        pe.wait_ge(tp_used, n - 3)
                    pe.transpose(tp[:, n % 4, 0:P], src, core.ident[:, :]).then_inc(tp_done, 1)

            @block.scalar
            def _(act):
                for n, (_, dst) in enumerate(weight_chunks()):
                    act.wait_ge(tp_done, n + 1)
                    act.copy(dst, tp[:, n % 4, 0:P]).then_inc(tp_used, 1)


def phase_project(nc, core, d):
    with ExitStack() as st:
        sb, ps = tensors(nc, st)
        x_t = sb("p_x_t", [P, SB, D], F32)
        stats = sb("p_stats", [P, SB, 6], F32)
        mv = sb("p_mv", [P, SB, 2], F32)
        std = sb("p_std", [P, SB], F32)
        rstd = sb("p_rstd", [P, SB], F32)
        xh = sb("p_xh", [P, SB, D], F32)
        xhT = sb("p_xhT", [P, SB, KC, P], F32)
        qkv = sb("p_qkv", [P, SB, 3 * D], F32)
        rest1 = sb("p_rest1", [P, SB, D], F32)
        rest2 = sb("p_rest2", [P, SB, D], F32)
        tp = [ps(f"p_tp{i}", [P, KC, 256], F32) for i in range(2)]
        qp = [ps(f"p_qp{i}", [P, 1024], F32) for i in range(3)]
        x_in, kv_out = core.sem("p_x_in"), core.sem("p_kv_out")
        names = ("stats", "mv", "std", "rstd", "xh", "tp", "xhT", "qkvp", "qkv", "q1", "r1", "q2", "r2", "q3")
        s = {n: core.sem("p_s_" + n) for n in names}

        with nc.Block() as block:
            @block.sync
            def _(sp):
                def first(t):
                    need(sp, s["xh"], t * SB)
                    sp.dma_start(x_t[:, :, :], d["x"][bass.ds(t * SB * P, SB * P), :]
                                 .rearrange("(j p) c -> p j c", p=P)).then_inc(x_in, 16)

                def second(t):
                    for j in range(SB):
                        n = t * SB + j
                        sp.wait_ge(s["qkv"], n + 1)
                        sp.dma_start(d["kv_table"][bass.ds(n * P, P), :], qkv[:, j, D:3 * D]).then_inc(kv_out, 16)

                rounds(sp, first, second)

                sp.wait_ge(kv_out, 16 * BLOCKS)

            @block.vector
            def _(dve):
                def first(t):
                    for j in range(SB):
                        dve.wait_ge(x_in, 16 * (t + 1))
                        dve.bn_stats(stats[:, j, :], x_t[:, j, :]).then_inc(s["stats"], 1)
                    for j in range(SB):
                        dve.wait_ge(s["stats"], t * SB + j + 1)
                        need(dve, s["std"], t)
                        wait_here(dve, core)
                        dve.bn_aggr(mv[:, j, :], stats[:, j, :]).then_inc(s["mv"], 1)
                    dve.wait_ge(s["std"], t + 1)
                    dve.reciprocal(rstd[:, :], std[:, :]).then_inc(s["rstd"], 1)
                    for j in range(SB):
                        dve.wait_ge(s["rstd"], t + 1)
                        need(dve, s["tp"], t * SB)
                        dve.tensor_scalar(xh[:, j, :], x_t[:, j, :], mv[:, j, 0:1], rstd[:, j:j + 1],
                                          ALU.subtract, ALU.mult).then_inc(s["xh"], 1)

                def second(t):
                    for j in range(SB):
                        n = t * SB + j
                        dve.wait_ge(s["qkvp"], n + 1)
                        need(dve, s["r1"], t * SB)
                        need(dve, s["q1"], t * SB)
                        need(dve, kv_out, 16 * SB * t)
                        dve.tensor_tensor(qkv[:, j, :], qp[j % 3][:, 0:3 * D], core.b_qkv[:, :],
                                          ALU.add).then_inc(s["qkv"], 1)

                rounds(dve, first, second)

            @block.scalar
            def _(act):
                def split_queries(t):
                    for part, src, source_done in ((0, None, "qkv"), (1, rest1, "r1"), (2, rest2, "r2")):
                        for j in range(SB):
                            n = t * SB + j
                            act.wait_ge(s[source_done], n + 1)
                            source = qkv[:, j, 0:D] if src is None else src[:, j, :]
                            wait_here(act, core)
                            act.copy(core.q_parts[:, bass.ds((n * 3 + part) * D, D)],
                                     source).then_inc(s[("q1", "q2", "q3")[part]], 1)

                def first(t):
                    act.wait_ge(s["mv"], (t + 1) * SB)
                    need(act, s["rstd"], t)
                    act.activation(std[:, :], mv[:, :, 1], ACT.Sqrt, bias=core.eps[:, :]).then_inc(s["std"], 1)

                def second(t):
                    for j in range(SB):
                        act.wait_ge(s["tp"], t * SB + j + 1)
                        need(act, s["qkvp"], t * SB)
                        act.copy(xhT[:, j, :, :], tp[j % 2][:, :, 0:P]).then_inc(s["xhT"], 1)
                    if not isinstance(t, int) or t > 0:
                        split_queries(t - 1)

                rounds(act, first, second)
                split_queries(ST - 1)

            @block.gpsimd
            def _(pool):
                def second(t):
                    for part in range(2):
                        for j in range(SB):
                            n = t * SB + j
                            pool.wait_ge(s[("q1", "q2")[part]], n + 1)
                            if part:
                                pool.wait_ge(s["r1"], n + 1)
                            need(pool, s[("q2", "q3")[part]], t * SB)
                            src = rest1[:, j, :] if part else qkv[:, j, 0:D]
                            dst = rest2 if part else rest1
                            pool.tensor_tensor(dst[:, j, :], src, core.q_parts[:, bass.ds((n * 3 + part) * D, D)],
                                               ALU.subtract).then_inc(s[("r1", "r2")[part]], 1)

                rounds(pool, lambda t: None, second)

            @block.tensor
            def _(pe):
                def second(t):
                    for j in range(SB):
                        n = t * SB + j
                        pe.wait_ge(s["xh"], n + 1)
                        need(pe, s["xhT"], n if j == 0 else n - 1)
                        for k in range(KC):
                            mm = pe.transpose(tp[j % 2][:, k, 0:P], xh[:, j, k * P:(k + 1) * P], core.ident[:, :])
                        mm.then_inc(s["tp"], 1)
                    for j in range(SB):
                        n = t * SB + j
                        pe.wait_ge(s["xhT"], n + 1)
                        need(pe, s["qkv"], n if j == 0 else (n - 1 if j == 1 else n - 2))
                        for lo, hi in ((0, 512), (512, 768)):
                            for k in range(KC):
                                mm = pe.matmul(qp[j % 3][:, lo:hi], xhT[:, j, k, :], core.wqkvT[:, k, lo:hi],
                                               start=(k == 0), stop=(k == KC - 1))
                        mm.then_inc(s["qkvp"], 1)

                rounds(pe, lambda t: None, second)


def phase_route(nc, core, d):
    NB1 = BLOCKS + 1
    full = TILES // P * P // P
    left = TILES - full * P
    with ExitStack() as st:
        sb, ps = tensors(nc, st)
        first = sb("r_first", [P, full + 1], I32)
        firstf = sb("r_firstf", [P, full + 1], F32)
        bound_i = sb("r_bound_i", [P, NB1], I32)
        bound = sb("r_bound", [P, NB1], F32)
        visit_i = sb("r_visit_i", [P, VC], I32)
        visit = sb("r_visit", [P, VC], F32)
        below = sb("r_below", [P, NB1, full + 1], F32)
        cnt = sb("r_cnt", [P, NB1], F32)
        T = sb("r_T", [P, NB1], F32)
        size = sb("r_size", [P, BLOCKS], F32)
        size_i = sb("r_size_i", [P, BLOCKS], I32)
        size_q = sb("r_size_q", [P, BLOCKS], I32)
        one = sb("r_one", [P, BLOCKS], F32)
        gend = sb("r_gend", [P, BLOCKS], F32)
        v0 = sb("r_v0", [P, BLOCKS], F32)
        rel = sb("r_rel", [P, BLOCKS], F32)
        steps = sb("r_steps", [P, 3, BLOCKS], F32)
        ge = sb("r_ge", [P, VC, BLOCKS], F32)
        tmp = sb("r_tmp", [P, VC, BLOCKS], F32)
        vb = sb("r_vb", [P, VC], F32)
        vt = sb("r_vt", [P, VC], F32)
        vend = sb("r_vend", [P, VC], F32)
        ok = sb("r_ok", [P, VC], F32)
        tile_i = sb("r_tile_i", [P, VC], I32)
        rows = sb("r_rows", [P, VC, 2 * P], I32)
        src_f = sb("r_src_f", [P, VC, P], F32)
        loc_f = sb("r_loc_f", [P, VC, P], F32)
        dst_f = sb("r_dst_f", [P, VC, P], F32)
        inside, below_end = rows[:, :, 0:P].bitcast(F32), rows[:, :, P:2 * P].bitcast(F32)
        begins = sb("r_begins", [P, VC, P + 1], F32)
        ends = sb("r_ends", [P, VC, 3], F32)
        before = sb("r_before", [1, 3], F32)
        block_i = sb("r_block_i", [P, VC], I32)
        meta = sb("r_meta", [P, HOLD, 2 * BATCH], I32)
        this = sb("r_this", [BATCHES, BATCH, 3], F32)
        prev = sb("r_prev", [BATCHES, BATCH, 3], F32)
        enter = sb("r_enter", [BATCHES, BATCH + 1], F32)
        many = sb("r_many", [BATCHES, BATCH], F32)
        through = sb("r_through", [BATCHES, 2, BATCH], F32)
        table = sb("r_table", [BATCHES, ROWTAB], F32)
        psum_cnt = ps("r_cnt_ps", [P, 512], F32)
        tp = [ps(f"r_tp{i}", [P, 4, P], F32) for i in range(2)]
        iotas, first_in, step, cnt_ps, tile_ready = (core.sem("r_" + n) for n in
                                                     ("iotas", "first_in", "step", "cnt_ps", "tile_ready"))
        rows_in, tp_done, tp_used, split = (core.sem("r_" + n) for n in ("rows_in", "tp_done", "tp_used", "split"))
        padded, ends_ready, ends_out, ends_in, begins_out, table_ready = (core.sem("r_" + n) for n in (
            "padded", "ends_ready", "ends_out", "ends_in", "begins_out", "table_ready"))
        with nc.Block() as block:
            @block.gpsimd
            def _(pool):
                pool.memset(first[:, :], 1 << 20).then_inc(padded, 1)
                pool.iota(bound_i[:, :], pattern=[[P, NB1]], base=0, channel_multiplier=0).then_inc(iotas, 1)
                pool.iota(visit_i[:, :], pattern=[[P, VC]], base=0, channel_multiplier=1).then_inc(iotas, 1)
                last_row = pool.to_reg(PAD_TILE)
                pool.wait_ge(tile_ready, 1)
                for c in range(VC):
                    pool.indirect_dma_start(rows[:, c, :], None, d["edges"],
                                            bass.IndirectOffsetOnAxis(ap=tile_i[:, c:c + 1], axis=0),
                                            bounds_check=last_row, oob_is_err=False).then_inc(rows_in, 16)

            @block.sync
            def _(sp):
                dst_first = d["edges"][:, P:P + 1]
                sp.wait_ge(padded, 1)
                sp.dma_start(first[:, 0:full].unsqueeze(2),
                             dst_first[0:full * P, :].rearrange("(p c) o -> p c o", c=full),
                             allow_slow_non_contiguous=True).then_inc(first_in, 16)
                sp.dma_start(first[0:left, full:full + 1], dst_first[full * P:TILES, :],
                             allow_slow_non_contiguous=True).then_inc(first_in, 16)
                sp.wait_ge(first_in, 32)
                sp.wait_ge(ends_ready, 1)
                visits = d["ends_table"][1:VPAD + 1, :].rearrange("(c p) k -> p c k", p=P)
                sp.dma_start(visits, ends[:, :, :]).then_inc(ends_out, 16)
                sp.dma_start(d["ends_table"][0:1, :], before[:, :]).then_inc(ends_out, 16)
                sp.dma_start(d["block_table"].rearrange("(c p) -> p c", p=P).unsqueeze(2),
                             block_i[:, :].unsqueeze(2), allow_slow_non_contiguous=True).then_inc(ends_out, 16)
                sp.dma_start(d["begins_table"].rearrange("(c p) e -> p c e", p=P), begins[:, :, :]
                             ).then_inc(begins_out, 16)
                sp.wait_ge(ends_out, 48)
                sp.dma_start(this[:, :, :], d["ends_table"][1:VISITS + 1, :].rearrange("(b v) k -> b v k", v=BATCH)
                             ).then_inc(ends_in, 16)
                sp.dma_start(prev[:, :, :], d["ends_table"][0:VISITS, :].rearrange("(b v) k -> b v k", v=BATCH)
                             ).then_inc(ends_in, 16)
                sp.dma_start(core.block_of[:, :].unsqueeze(2),
                             d["block_table"][0:VISITS].rearrange("(o g v) -> o g v", o=1, v=GV)[:, :, 0:1],
                             allow_slow_non_contiguous=True).then_inc(ends_in, 16)
                sp.wait_ge(tp_used, 2 * VC)
                sp.dma_start(d["meta_table"], meta[:, :, :].rearrange("p b k -> p (b k)")).then_inc(begins_out, 16)
                sp.wait_ge(table_ready, 1)
                sp.dma_start(d["row_table"], table[:, :]).then_inc(begins_out, 16)
                sp.wait_ge(begins_out, 48)
                sp.wait_ge(ends_in, 48)

            @block.tensor
            def _(pe):
                pe.wait_ge(step, 1)
                pe.matmul(psum_cnt[:, 0:NB1], core.ones[:, :], cnt[:, :], start=True, stop=True).then_inc(cnt_ps, 1)
                for c in range(VC):
                    pe.wait_ge(split, c + 1)
                    if c >= 2:
                        pe.wait_ge(tp_used, 2 * (c - 1))
                    pe.transpose(tp[c % 2][:, 0, :], src_f[:, c, :], core.ident[:, :])
                    pe.transpose(tp[c % 2][:, 1, :], loc_f[:, c, :], core.ident[:, :]).then_inc(tp_done, 1)

            @block.scalar
            def _(act):
                for c in range(VC):
                    act.wait_ge(tp_done, c + 1)
                    batches = meta[:, c * P // BATCH:(c + 1) * P // BATCH, :]
                    act.copy(batches[:, :, 0:BATCH], tp[c % 2][:, 0, :].rearrange("p (b v) -> p b v", v=BATCH)
                             ).then_inc(tp_used, 1)
                    act.copy(batches[:, :, BATCH:].bitcast(F32),
                             tp[c % 2][:, 1, :].rearrange("p (b v) -> p b v", v=BATCH)).then_inc(tp_used, 1)

            @block.vector
            def _(dve):
                done = [0]
                chain = core.sem("r_chain")

                def then(ins):
                    done[0] += 1
                    ins.then_inc(chain, 1)
                    dve.wait_ge(chain, done[0])

                dve.wait_ge(iotas, 2)
                dve.wait_ge(first_in, 32)
                dve.tensor_copy(bound[:, :], bound_i[:, :])
                dve.tensor_copy(visit[:, :], visit_i[:, :])
                dve.memset(one[:, :], 1.0)
                then(dve.tensor_copy(firstf[:, :], first[:, :]))
                then(dve.tensor_tensor(below[:, :, :], firstf[:, :].unsqueeze(1).to_broadcast([P, NB1, full + 1]),
                                       bound[:, :].unsqueeze(2).to_broadcast([P, NB1, full + 1]), ALU.is_lt))
                dve.tensor_reduce(cnt[:, :], below[:, :, :], X, ALU.add).then_inc(step, 1)
                dve.wait_ge(cnt_ps, 1)
                then(dve.tensor_scalar(T[:, :], psum_cnt[:, 0:NB1], -1.0, 0.0, ALU.add, ALU.max))
                then(dve.tensor_tensor(size[:, :], T[:, 1:NB1], T[:, 0:BLOCKS], ALU.subtract))
                then(dve.tensor_scalar(size_i[:, :], size[:, :], float(GV), None, ALU.add))
                then(dve.tensor_scalar(size_q[:, :], size_i[:, :], 2, None, ALU.arith_shift_right))
                then(dve.tensor_copy(size[:, :], size_q[:, :]))
                then(dve.tensor_tensor_scan(gend[:, :], one[:, :], size[:, :], 0.0, ALU.mult, ALU.add))
                then(dve.tensor_tensor(v0[:, :], gend[:, :], size[:, :], ALU.subtract))
                then(dve.tensor_scalar(v0[:, :], v0[:, :], float(GV), None, ALU.mult))
                then(dve.tensor_tensor(rel[:, :], T[:, 0:BLOCKS], v0[:, :], ALU.subtract))
                dve.memset(steps[:, 0, 0:1], 0.0)
                dve.memset(steps[:, 0, 1:BLOCKS], 1.0)
                dve.tensor_copy(steps[:, 1, 0:1], rel[:, 0:1])
                dve.tensor_tensor(steps[:, 1, 1:BLOCKS], rel[:, 1:BLOCKS], rel[:, 0:BLOCKS - 1], ALU.subtract)
                dve.tensor_copy(steps[:, 2, 0:1], T[:, 1:2])
                dve.tensor_tensor(steps[:, 2, 1:BLOCKS], T[:, 2:NB1], T[:, 1:BLOCKS], ALU.subtract)
                then(dve.tensor_tensor(ge[:, :, :], visit[:, :].unsqueeze(2).to_broadcast([P, VC, BLOCKS]),
                                       v0[:, :].unsqueeze(1).to_broadcast([P, VC, BLOCKS]), ALU.is_ge))
                for n, out in enumerate((vb, vt, vend)):
                    then(dve.tensor_tensor(tmp[:, :, :], ge[:, :, :],
                                           steps[:, n, :].unsqueeze(1).to_broadcast([P, VC, BLOCKS]), ALU.mult))
                    then(dve.tensor_reduce(out[:, :], tmp[:, :, :], X, ALU.add))
                then(dve.tensor_tensor(vt[:, :], vt[:, :], visit[:, :], ALU.add))
                then(dve.tensor_tensor(ok[:, :], vt[:, :], vend[:, :], ALU.is_le))
                then(dve.tensor_scalar(vt[:, :], vt[:, :], -float(PAD_TILE), None, ALU.add))
                then(dve.tensor_tensor(vt[:, :], vt[:, :], ok[:, :], ALU.mult))
                then(dve.tensor_copy(block_i[:, :], vb[:, :]))
                dve.tensor_scalar(vb[:, :], vb[:, :], float(P), None, ALU.mult)
                dve.tensor_scalar(tile_i[:, :], vt[:, :], float(PAD_TILE), None, ALU.add).then_inc(tile_ready, 1)
                dve.wait_ge(tile_ready, 1)
                dve.wait_ge(rows_in, 16 * VC)
                dve.tensor_copy(src_f[:, :, :], rows[:, :, 0:P])
                then(dve.tensor_copy(dst_f[:, :, :], rows[:, :, P:2 * P]))
                for c in range(VC):
                    dve.tensor_scalar(loc_f[:, c, :], dst_f[:, c, :], vb[:, c:c + 1], None,
                                      ALU.subtract).then_inc(split, 1)
                dve.wait_ge(split, VC)
                dve.tensor_scalar(dst_f[:, :, :], dst_f[:, :, :], 1.0, None, ALU.add)
                dve.tensor_scalar(below_end[:, :, :], loc_f[:, :, :], float(P), None, ALU.is_lt)
                then(dve.tensor_scalar(inside[:, :, :], loc_f[:, :, :], 0.0, None, ALU.is_ge))
                then(dve.tensor_tensor(inside[:, :, :], inside[:, :, :], below_end[:, :, :], ALU.mult))
                then(dve.tensor_tensor(dst_f[:, :, :], dst_f[:, :, :], inside[:, :, :], ALU.mult))
                then(dve.tensor_scalar(dst_f[:, :, :], dst_f[:, :, :], -1.0, None, ALU.add))
                dve.tensor_copy(ends[:, :, 0:1], dst_f[:, :, 0:1])
                dve.tensor_copy(ends[:, :, 1:2], dst_f[:, :, P - 1:P])
                dve.tensor_copy(ends[:, :, 2:3], loc_f[:, :, 0:1])
                dve.memset(before[:, :], -2.0)
                dve.memset(begins[:, :, 0:1], -BIG)
                dve.memset(begins[:, :, P:P + 1], -BIG)
                then(dve.tensor_tensor(begins[:, :, 1:P], dst_f[:, :, 1:P], dst_f[:, :, 0:P - 1], ALU.not_equal))
                dve.tensor_scalar(begins[:, :, 1:P], begins[:, :, 1:P], -BIG, None, ALU.mult).then_inc(ends_ready, 1)
                dve.wait_ge(ends_in, 48)
                span = HEADS * (BATCH + 1)
                dve.memset(table[:, :], 0.0)
                dve.memset(enter[:, BATCH:], 0.0)
                dve.tensor_tensor(enter[:, 0:BATCH], this[:, :, 0], prev[:, :, 1], ALU.not_equal)
                then(dve.tensor_tensor(many[:, :], this[:, :, 0], this[:, :, 1], ALU.not_equal))
                dve.tensor_scalar(table[:, 2 * span + 2 * BATCH:2 * span + 2 * BATCH + 1], enter[:, 0:1], -1.0, 1.0,
                                  ALU.mult, ALU.add)
                then(dve.tensor_copy(table[:, 2 * span + 2 * BATCH + 1:], this[:, 0, 2:3]))
                then(dve.tensor_scalar(enter[:, :], enter[:, :], -BIG, None, ALU.mult))
                then(dve.tensor_scalar(many[:, :], many[:, :], -BIG, None, ALU.mult))
                dve.tensor_copy(table[:, 2 * span:2 * span + BATCH], enter[:, 0:BATCH])
                dve.tensor_copy(table[:, 2 * span + BATCH:2 * span + 2 * BATCH], enter[:, 1:BATCH + 1])
                dve.tensor_tensor(through[:, 0, :], enter[:, 0:BATCH], many[:, :], ALU.min)
                then(dve.tensor_tensor(through[:, 1, :], enter[:, 1:BATCH + 1], many[:, :], ALU.min))
                for way in range(2):
                    part = table[:, way * span:(way + 1) * span].rearrange("b (h v) -> b h v", h=HEADS)
                    edge = 0 if way == 0 else BATCH
                    dve.memset(part[:, :, edge:edge + 1], -BIG)
                    ins = dve.tensor_copy(part[:, :, 1 - way:BATCH + 1 - way],
                                          through[:, way, :].unsqueeze(1).to_broadcast([BATCHES, HEADS, BATCH]))
                ins.then_inc(table_ready, 1)


def batches(eng, body, total, after, before=2):
    loops = (total - before - 2) // 2

    def peeled(B):
        body(lambda k, off=0: k * B + off, B // 2, B % 2, B)

    for B in range(before):
        peeled(B)
    with eng.Fori(0, loops) as i:
        for c in range(2):
            body(lambda k, off=0: i * (2 * k) + ((before + c) * k + off), i + before // 2, c, None)
    for B in range(before + 2 * loops, total + after):
        peeled(B)


def has(B, n, off):
    return B is None or 0 <= STEPS * B + n + off < STEPS * BATCHES


def phase_attention(nc, core, d):
    GROUP_STEPS = GV // 2
    SPAN = HEADS * (BATCH + 1)
    with ExitStack() as st:
        sb, ps = tensors(nc, st)
        kv_ring = sb("a_kv_ring", [P, 2 * RING_STEPS, 2 * D], F32)
        meta = sb("a_meta", [P, 2, 2 * BATCH], I32)
        begins = sb("a_begins", [P, 2, P + 1], F32)
        rows = sb("a_rows", [1, ROWTAB], F32)
        local = sb("a_local", [P, 2, BATCH], F32)
        onehot = sb("a_onehot", [P, 2, 2, P], BF16)
        onehotT = sb("a_onehotT", [P, 2, 2, P], BF16)
        onehot32 = sb("a_onehot32", [P, 2, 2, P], F32)
        prod = sb("a_prod", [P, 2, 2 * D], F32)
        att = sb("a_att", [P, 2, BATCH * HEADS], F32)
        scratch = sb("a_scratch", [P, 2 * SPAN], F32)
        fwd, diff = scratch[:, 0:P], scratch[:, P:2 * P]
        segmax = sb("a_segmax", [P, P], F32)
        ends = sb("a_ends", [1, 2, SPAN], F32)
        chain = scratch[0:1, :].rearrange("o (w k) -> o w k", w=2)
        carry = sb("a_carry", [1, 2, P], F32)
        drop = sb("a_drop", [1, 2, HEADS], F32)

        tp = [ps(f"a_tp{i}", [P, 8, P], BF16) for i in range(2)]
        q_edge = [ps(f"a_q_edge{i}", [P, 2 * D], F32) for i in range(2)]
        acc_ps = ps("a_acc", [P, 512], F32)
        turn = ps("a_turn", [P, 512], F32)
        small = ps("a_small", [P, 512], F32)
        p_ps = ps("a_p", [P, 512], F32)
        FIRST, CARRY, SCALES = 128, 256, 272

        row_in = [core.sem(f"a_row_in{i}") for i in range(RING_STEPS)]
        meta_in = [core.sem(f"a_meta_in{i}") for i in range(2)]
        begins_in = [core.sem(f"a_begins_in{i}") for i in range(2)]
        local_in = [core.sem(f"a_local_in{i}") for i in range(2)]
        rows_in = core.sem("a_rows_in")
        onehot_done, tp_done, onehotT_done, q_edge_done, prod_done, att_done, onehot32_done, pv_done, mm_done = (
            core.sem("a_" + n) for n in ("onehot", "tp", "onehotT", "q_edge", "prod", "att", "onehot32", "pv", "mm"))
        acc_done = core.sem("a_acc_done")
        turned, segmax_done, ends_done, carry_done, carried, diff_done, diff_turned, p_done, p_col_done = (
            core.sem("a_" + n) for n in ("turned", "segmax", "ends", "carry", "carried", "diff", "diff_turned", "p",
                                         "p_col"))
        own, scaled, pv_odd_done = core.sem("a_own"), core.sem("a_scaled"), core.sem("a_pv_odd")
        OWN = 6

        with nc.Block() as block:
            @block.sync
            def _(sp):
                def batch(at, rounds, c, B):
                    if has(B, 0, 0):
                        need(sp, prod_done, at(STEPS, -STEPS))
                        need(sp, onehot_done, at(STEPS, -STEPS))
                        sp.dma_start(meta[:, c, :], d["meta_table"][:, bass.ds(at(2 * BATCH), 2 * BATCH)]
                                     ).then_inc(meta_in[c], 16)
                    if has(B, 0, -STEPS):
                        need(sp, carry_done, at(1, -1))
                        sp.dma_start(rows[:, :], d["row_table"][bass.ds(at(1, -1), 1), :]).then_inc(rows_in, 16)
                    if has(B, 0, 0):
                        need(sp, diff_done, at(1, -1))
                        sp.dma_start(begins[:, c, :], d["begins_table"][bass.ds(at(BATCH), BATCH), :].unsqueeze(1)
                                     .to_broadcast([BATCH, HEADS, P + 1])).then_inc(begins_in[c], 16)
                    if has(B, 0, -STEPS):
                        need(sp, onehot32_done, at(STEPS, 1 - 2 * STEPS))
                        sp.dma_start(local[:, 1 - c, :], d["meta_table"][:, bass.ds(at(2 * BATCH, -BATCH), BATCH)]
                                     .bitcast(F32)).then_inc(local_in[1 - c], 16)

                batches(sp, batch, BATCHES, 2)

            @block.gpsimd
            def _(pool):
                last_row = pool.to_reg(ROWS - 1)

                def weigh(at, c, n, B):
                    r = n - LAG - 2
                    if r % 2 == 0 or not has(B, n, -LAG - 2):
                        return
                    need(pool, p_col_done, at(1, r // STEPS + 1))
                    visit = 2 * ((c * STEPS + r) % RING_STEPS) + 1
                    v = kv_ring[:, visit, D:2 * D].rearrange("p (g k) -> p g k", k=DH)
                    p = kv_ring[:, visit, D - HEADS:D].unsqueeze(2).to_broadcast([P, HEADS, DH])
                    pool.tensor_tensor(v, v, p, ALU.mult).then_inc(pv_odd_done, 1)

                def batch(at, rounds, c, B):
                    if has(B, 0, 0):
                        need(pool, meta_in[c], 16 * (rounds + 1))
                    for n in range(STEPS):
                        weigh(at, c, n, B)
                        if not has(B, 0, 0):
                            continue
                        slot = c * STEPS + n
                        need(pool, mm_done, at(STEPS, n - RING_STEPS + 1))
                        wait_here(pool, core)
                        for u in range(2):
                            pool.indirect_dma_start(
                                kv_ring[:, 2 * slot + u, :], None, d["kv_table"],
                                bass.IndirectOffsetOnAxis(ap=meta[:, c, 2 * n + u:2 * n + u + 1], axis=0),
                                bounds_check=last_row, oob_is_err=False).then_inc(row_in[slot], 16)

                batches(pool, batch, BATCHES, 2)

            @block.vector
            def _(dve):
                def product(at, rounds, c, n, B):
                    if not has(B, n, 0):
                        return
                    h, slot = n % 2, c * STEPS + n
                    need(dve, att_done, at(STEPS, n - 1))
                    need(dve, row_in[slot], 32 * (rounds + 1))
                    need(dve, q_edge_done, at(STEPS, n + 1))
                    dve.tensor_tensor(prod[:, h, :].rearrange("p (u k) -> p u k", u=2),
                                      q_edge[h][:, :].rearrange("p (u k) -> p u k", u=2),
                                      kv_ring[:, 2 * slot:2 * slot + 2, 0:D], ALU.mult).then_inc(prod_done, 1)

                def score(at, c, n, B):
                    if not has(B, n, -1):
                        return
                    m = (n - 1) % STEPS
                    cc = c if n else 1 - c
                    need(dve, prod_done, at(STEPS, n))
                    dve.tensor_reduce(att[:, cc, m * 2 * HEADS:(m + 1) * 2 * HEADS],
                                      prod[:, m % 2, :].rearrange("p (g k) -> p g k", k=DH), X,
                                      ALU.add).then_inc(att_done, 1)

                def in_visit_scans(pen, source, own_count):
                    dve.tensor_tensor_scan(fwd[:, :], pen[:, 0:P], source, -BIG, ALU.add, ALU.max).then_inc(own, 1)
                    dve.wait_ge(own, own_count)
                    return dve.tensor_tensor_scan(segmax[:, ::-1], pen[:, 1:P + 1][:, ::-1], fwd[:, ::-1], -BIG,
                                                  ALU.add, ALU.max)

                def maxima(at, rounds, c, n, B):
                    if n not in (1, 2, 3) or not has(B, 0, -STEPS):
                        return
                    rounds, c = (rounds if c else (rounds - 1)), 1 - c
                    pen, row = begins[:, c, :], rows
                    owned = lambda k: at(OWN, k - OWN)
                    if n == 1:
                        need(dve, turned, at(1))
                        need(dve, begins_in[c], 16 * (rounds + 1))
                        in_visit_scans(pen, turn[:, 0:P], owned(1)).then_inc(segmax_done, 1)
                    elif n == 2:
                        need(dve, ends_done, at(1))
                        need(dve, rows_in, at(16))
                        run = ends[:, 0, :].rearrange("o (h v) -> o h v", h=HEADS)
                        back = ends[:, 1, :].rearrange("o (h v) -> o h v", h=HEADS)
                        dve.tensor_copy(run[:, :, 1:BATCH + 1], small[0:1, 0:P].rearrange("o (v h) -> o h v", h=HEADS))
                        dve.tensor_copy(back[:, :, 0:BATCH], small[0:1, FIRST:FIRST + P]
                                        .rearrange("o (v h) -> o h v", h=HEADS)).then_inc(own, 1)
                        dve.tensor_scalar(att[0:1, c, :], core.iota_bf[0:1, :], row[:, ROWTAB - 1:ROWTAB], None,
                                          ALU.is_equal)
                        dve.wait_ge(own, owned(2))
                        dve.tensor_tensor_scan(chain[:, 0, :], row[:, 0:SPAN], ends[:, 0, :], -BIG, ALU.add, ALU.max)
                        dve.tensor_tensor_scan(chain[:, 1, :][:, ::-1], row[:, SPAN:2 * SPAN][:, ::-1],
                                               ends[:, 1, :][:, ::-1], -BIG, ALU.add, ALU.max).then_inc(own, 1)
                        dve.wait_ge(own, owned(3))
                        by_head = chain[:, :, :].rearrange("o w (h v) -> o w v h", h=HEADS)
                        for way, first in ((0, 0), (1, 1)):
                            enter = row[:, 2 * SPAN + way * BATCH:2 * SPAN + (way + 1) * BATCH]
                            dve.tensor_tensor(carry[:, way, :].rearrange("o (v h) -> o v h", h=HEADS),
                                              by_head[:, way, first:first + BATCH, :],
                                              enter.unsqueeze(2).to_broadcast([1, BATCH, HEADS]), ALU.add)
                        dve.tensor_tensor(drop[:, 0, :], run[:, :, 0], by_head[:, 1, 0, :],
                                          ALU.subtract).then_inc(own, 1)
                        dve.wait_ge(own, owned(4))
                        dve.tensor_copy(run[:, :, 0], by_head[:, 0, BATCH, :])
                        dve.tensor_scalar(drop[:, 1, :], drop[:, 0, :], 0.0, row[:, ROWTAB - 2:ROWTAB - 1], ALU.min,
                                          ALU.mult).then_inc(carry_done, 1)
                    else:
                        need(dve, carried, at(1))
                        for way, e in ((0, 0), (1, P - 1)):
                            col = small[:, CARRY + way:CARRY + way + 1]
                            ins = dve.tensor_tensor(segmax[:, e:e + 1], col, segmax[:, e:e + 1], ALU.max)
                        ins.then_inc(own, 1)
                        dve.wait_ge(own, owned(5))
                        in_visit_scans(pen, segmax[:, :], owned(6)).then_inc(diff_scans, 1)
                        need(dve, diff_scans, at(1))
                        dve.tensor_tensor(diff[:, :], turn[:, 0:P], segmax[:, :], ALU.subtract).then_inc(diff_done, 1)

                diff_scans = core.sem("a_diff_scans")

                def load_block(at, n):
                    return dve.value_load(core.block_of[0:1, bass.ds(at(STEPS // 2, n // 2 - (LAG + 2) // 2), 1)],
                                          min_val=0, max_val=BLOCKS - 1)

                def add_group(at, n, B):
                    if n == 5 and has(B, n, -LAG):
                        blk = dve.value_load(core.block_of[0:1, bass.ds(at(STEPS // 2, -STEPS // 2), 1)],
                                             min_val=0, max_val=BLOCKS - 1)
                        need(dve, acc_done, at(STEPS // 2, -STEPS // 2))
                        need(dve, p_done, at(1))
                        wait_here(dve, core)
                        a = core.acc[:, bass.ds(blk * W, W)]
                        f = p_ps[:, P:P + HEADS]
                        sums, total = a[:, HEADS:W].rearrange("p (h k) -> p h k", h=HEADS), a[:, 0:HEADS]
                        dve.tensor_tensor(total, f, total, ALU.mult)
                        dve.tensor_tensor(sums, f.unsqueeze(2).to_broadcast([P, HEADS, DH]), sums,
                                          ALU.mult).then_inc(scaled, 1)
                    if n % 2 == 0 and has(B, n, -LAG - 1):
                        blk = load_block(at, n)
                        need(dve, mm_done, at(STEPS, n - LAG))
                        need(dve, acc_done, at(STEPS // 2, n // 2 - (LAG + 2) // 2))
                        need(dve, scaled, at(1) if n == 6 else at(1, -1))
                        wait_here(dve, core)
                        a = core.acc[:, bass.ds(blk * W, W)]
                        dve.tensor_tensor(a, acc_ps[:, 0:W], a, ALU.add).then_inc(acc_done, 1)

                def weigh(at, c, n, B):
                    if not has(B, n, -LAG):
                        return
                    slot = (c * STEPS + n - LAG) % RING_STEPS
                    m = slot % STEPS
                    need(dve, p_done, at(1) if n >= 4 else at(1, -1))
                    v = kv_ring[:, 2 * slot:2 * slot + 2, D:2 * D].rearrange("p u (g k) -> p u g k", k=DH)
                    p = p_ps[:, m * 2 * HEADS:(m + 1) * 2 * HEADS].rearrange("p (u g) -> p u g", u=2)
                    visits = 2 if m % 2 == 0 else 1
                    dve.tensor_tensor(v[:, 0:visits], p[:, 0:visits].unsqueeze(3).to_broadcast([P, visits, HEADS, DH]),
                                      v[:, 0:visits], ALU.mult).then_inc(pv_done, 1)

                def batch(at, rounds, c, B):
                    for n in range(STEPS):
                        if n != 4:
                            weigh(at, c, n, B)
                        maxima(at, rounds, c, n, B)
                        product(at, rounds, c, n, B)
                        score(at, c, n, B)
                        if n == 4:
                            weigh(at, c, n, B)
                        add_group(at, n, B)

                dve.memset(ends[:, :, :], -BIG)
                batches(dve, batch, BATCHES, 2)

            @block.tensor
            def _(pe):
                def turn_one_hots(at, c, n, B, ahead):
                    if not has(B, n, ahead):
                        return
                    s = n + ahead
                    need(pe, onehot_done, at(STEPS, s + 1))
                    need(pe, onehotT_done, at(STEPS, s - 1))
                    for u in range(2):
                        mm = pe.transpose(tp[s % 2][:, u, :], onehot[:, s % 2, u, :], core.ident_bf[:, :])
                    mm.then_inc(tp_done, 1)

                def expand_queries(at, c, n, B, ahead):
                    if not has(B, n, ahead):
                        return
                    s = n + ahead
                    blk = pe.value_load(core.block_of[0:1, bass.ds(at(STEPS // 2, s // GROUP_STEPS), 1)],
                                        min_val=0, max_val=BLOCKS - 1)
                    need(pe, onehotT_done, at(STEPS, s + 1))
                    need(pe, prod_done, at(STEPS, s - 1))
                    for u in range(2):
                        for part in range(3):
                            mm = pe.matmul(q_edge[s % 2][:, u * D:(u + 1) * D], onehotT[:, s % 2, u, :],
                                           core.q_parts[:, bass.ds((blk * 3 + part) * D, D)],
                                           start=(part == 0), stop=(part == 2))
                    mm.then_inc(q_edge_done, 1)

                def sum_values(at, c, n, B):
                    if not has(B, n, -LAG - 1):
                        return
                    r = n - LAG - 1
                    slot = (c * STEPS + r) % RING_STEPS
                    need(pe, pv_done, at(STEPS, r + 1))
                    if r % 2 == 1:
                        need(pe, pv_odd_done, at(STEPS // 2, r // 2 + 1))
                    need(pe, onehot32_done, at(STEPS, r + 1))
                    need(pe, p_col_done, at(1) if n >= 5 else at(1, -1))
                    if r % 2 == 0:
                        need(pe, acc_done, at(STEPS // 2, r // 2))
                    for u in range(2):
                        mm = pe.matmul(acc_ps[:, 0:W], onehot32[:, r % 2, u, :],
                                       kv_ring[:, 2 * slot + u, D - HEADS:2 * D],
                                       start=(r % 2 == 0 and u == 0), stop=(r % 2 == 1 and u == 1))
                    mm.then_inc(mm_done, 1)

                def maxima(at, c, n, B):
                    if not has(B, 0, -STEPS):
                        return
                    if n == 0:
                        need(pe, att_done, at(STEPS))
                        need(pe, p_col_done, at(1, -1))
                        pe.transpose(turn[:, 0:P], att[:, 1 - c, :], core.ident[:, :]).then_inc(turned, 1)
                    elif n == 1:
                        need(pe, segmax_done, at(1))
                        pe.transpose(small[0:1, 0:P], segmax[:, P - 1:P], core.ident[:, :])
                        pe.transpose(small[0:1, FIRST:FIRST + P], segmax[:, 0:1], core.ident[:, :]
                                     ).then_inc(ends_done, 1)
                    elif n == 2:
                        need(pe, carry_done, at(1))
                        wait_here(pe, core)
                        for way in range(2):
                            pe.transpose(small[:, CARRY + way:CARRY + way + 1], carry[0:1, way, :],
                                         core.ident[0:1, 0:1])
                        pe.matmul(small[:, SCALES:SCALES + HEADS], att[0:1, 1 - c, :], drop[0:1, 1, :], start=True,
                                  stop=True).then_inc(carried, 1)
                    elif n == 3:
                        need(pe, diff_done, at(1))
                        pe.transpose(turn[:, 0:P], diff[:, :], core.ident[:, :]).then_inc(diff_turned, 1)

                def batch(at, rounds, c, B):
                    for n in range(STEPS):
                        sum_values(at, c, n, B)
                        expand_queries(at, c, n, B, 1)
                        maxima(at, c, n, B)
                        turn_one_hots(at, c, n, B, 2)

                start = lambda k, off=0: off
                for n in range(2):
                    turn_one_hots(start, 0, n, 0, 0)
                expand_queries(start, 0, 0, 0, 0)
                batches(pe, batch, BATCHES, 2)

            @block.scalar
            def _(act):
                apart, onehot_apart = core.sem("a_apart"), core.sem("a_onehot_apart")

                def copy_turned(at, n, B, ahead):
                    if not has(B, n, ahead):
                        return
                    s = n + ahead
                    need(act, tp_done, at(STEPS, s + 1))
                    need(act, q_edge_done, at(STEPS, s - 1))
                    act.copy(onehotT[:, s % 2, :, :], tp[s % 2][:, 0:2, :]).then_inc(onehotT_done, 1)

                def one_hots_apart(at, rounds, c, n, B, ahead):
                    if not has(B, n, ahead):
                        return
                    if n + ahead >= STEPS:
                        rounds, c = (rounds + 1 if c else rounds), 1 - c
                    need(act, meta_in[c], 16 * (rounds + 1))
                    need(act, tp_done, at(STEPS, n + ahead - 1))
                    m = (n + ahead) % STEPS
                    receiver = meta[:, c, BATCH + 2 * m:BATCH + 2 * m + 2].bitcast(F32)
                    for u in range(2):
                        ins = act.activation(onehot[:, m % 2, u, :], core.iota_bf[:, :], ACT.Abs, scale=-1.0,
                                             bias=receiver[:, u:u + 1])
                    ins.then_inc(onehot_apart, 1)

                def one_hots(at, n, B, ahead):
                    if not has(B, n, ahead):
                        return
                    h = (n + ahead) % 2
                    need(act, onehot_apart, at(STEPS, n + ahead + 1))
                    act.activation(onehot[:, h, :, :], onehot[:, h, :, :], ACT.Relu, scale=-1.0,
                                   bias=core.ones[:, 0:1]).then_inc(onehot_done, 1)

                def wide_one_hots_apart(at, rounds, c, n, B):
                    if not has(B, n, -LAG):
                        return
                    r = n - LAG
                    slot = (c * STEPS + r) % RING_STEPS
                    c, m = slot // STEPS, slot % STEPS
                    need(act, mm_done, at(STEPS, r - 1))
                    need(act, local_in[c], 16 * (rounds if n >= 4 and c or n < 4 else rounds + 1))
                    for u in range(2):
                        ins = act.activation(onehot32[:, r % 2, u, :], core.iota_bf[:, :], ACT.Abs, scale=-1.0,
                                             bias=local[:, c, 2 * m + u:2 * m + u + 1])
                    ins.then_inc(apart, 1)

                def wide_one_hots(at, n, B):
                    if not has(B, n, -LAG):
                        return
                    r = n - LAG
                    need(act, apart, at(STEPS, r + 1))
                    act.activation(onehot32[:, r % 2, :, :], onehot32[:, r % 2, :, :], ACT.Relu, scale=-1.0,
                                   bias=core.ones[:, 0:1]).then_inc(onehot32_done, 1)

                def exponentials(at, c, n, B):
                    if n != 3 or not has(B, 0, -STEPS):
                        return
                    need(act, diff_turned, at(1))
                    need(act, pv_done, at(STEPS, -STEPS))
                    need(act, scaled, at(1, -1))
                    act.activation(p_ps[:, 0:P], turn[:, 0:P], ACT.Exp, scale=SCALE)
                    act.activation(p_ps[:, P:P + HEADS], small[:, SCALES:SCALES + HEADS], ACT.Exp, scale=SCALE
                                   ).then_inc(p_done, 1)
                    lo = (1 - c) * BATCH
                    act.activation(kv_ring[:, lo:lo + BATCH, D - HEADS:D],
                                   turn[:, 0:P].rearrange("p (v h) -> p v h", h=HEADS), ACT.Exp, scale=SCALE
                                   ).then_inc(p_col_done, 1)

                def batch(at, rounds, c, B):
                    for n in range(STEPS):
                        one_hots_apart(at, rounds, c, n, B, 3)
                        wide_one_hots_apart(at, rounds, c, n, B)
                        one_hots(at, n, B, 3)
                        wide_one_hots(at, n, B)
                        copy_turned(at, n, B, 2)
                        exponentials(at, c, n, B)

                start = lambda k, off=0: off
                for n in range(3):
                    one_hots_apart(start, 0, 0, n, 0, 0)
                    one_hots(start, n, 0, 0)
                for n in range(2):
                    copy_turned(start, n, 0, 0)
                batches(act, batch, BATCHES, 2)


def phase_node(nc, core, d):
    with ExitStack() as st:
        sb, ps = tensors(nc, st)
        inv_l = sb("n_inv_l", [P, 2, SB, HEADS], F32)
        x_t = sb("n_x", [P, SB, D], F32)
        ln = sb("n_ln", [P, 2, SB, D], F32)
        o = sb("n_o", [P, SB, D], F32)
        oT = sb("n_oT", [P, SB, KC, P], F32)
        xnT = sb("n_xnT", [P, SB, KC, P], F32)
        stats = sb("n_stats", [P, 2, SB, 6], F32)
        mv = sb("n_mv", [P, 2, SB, 2], F32)
        std = sb("n_std", [P, 2, SB], F32)
        rstd = sb("n_rstd", [P, 2, SB], F32)
        b_ff = sb("n_b_ff", [P, D], F32)
        wr = sb("n_wr", [P, KC, EXPERTS], F32)
        br = sb("n_br", [P, EXPERTS], F32)
        wffT = sb("n_wffT", [P, KC, D], F32)
        o_tp = [ps(f"n_o_tp{i}", [P, KC, 256], F32) for i in range(2)]
        yp = [ps(f"n_yp{i}", [P, 512], F32) for i in range(2)]
        z_tp = [ps(f"n_z_tp{i}", [P, KC, 256], F32) for i in range(2)]
        lp = ps("n_lp", [P, 512], F32)
        x_in, z_out = core.sem("n_x_in"), core.sem("n_z_out")
        par_in = core.sem("n_par_in")
        names = ("lmax", "inv_l", "xb", "o", "o_tp", "oT", "yp", "y1", "stats", "mv", "std", "rstd", "ln",
                 "z_tp", "xnT", "lp", "logits")
        s = {n: core.sem("n_s_" + n) for n in names}

        def overlapped(eng, later):
            later(0, first=True)
            later(1)
            with eng.Fori(0, ST - 4) as i:
                later(i + 2)
            later(ST - 2, before_last=True)
            later(ST - 1, last=True)

        def free_slot(eng, sem, n, j):
            need(eng, sem, n if j == 0 else n - 1)

        def y1_at(n):
            return core.acc[:, bass.ds(n * W + HEADS, D)]

        with nc.Block() as block:
            @block.sync
            def _(sp):
                sp.dma_start(b_ff[:, :], d["b_ff"].partition_broadcast(P)).then_inc(par_in, 16)
                sp.dma_start(br[:, :], d["br"].partition_broadcast(P)).then_inc(par_in, 16)
                sp.dma_start(wffT[:, :, :], d["wff_table"]).then_inc(par_in, 16)
                sp.dma_start(wr[:, :, :], d["Wr"].rearrange("(k p) e -> p k e", p=P)).then_inc(par_in, 16)
                for k in range(KC):
                    for tile, name in ((core.gamma, "gamma"), (core.beta, "beta")):
                        sp.dma_start(tile[:, k:k + 1], d[name][k * P:(k + 1) * P].rearrange("(p a) -> p a", a=1)
                                     ).then_inc(par_in, 16)

                def weights():
                    sp.dma_start(core.w1[:, :, :, :], d["W1"].rearrange("e (k p) h -> p e k h", p=P)
                                 ).then_inc(core.w_in, 16)
                    sp.dma_start(core.w2[:, :, :, :], d["W2"].rearrange("e (c p) o -> p e c o", p=P)
                                 ).then_inc(core.w_in, 16)
                    sp.dma_start(core.b2[:, :], d["b2"]).then_inc(core.w_in, 16)
                    sp.dma_start(core.b1_rows[:, :], d["b1"].rearrange("e (c p) -> (e c) p", p=P)
                                 ).then_inc(core.w_in, 16)

                def first(t):
                    need(sp, s["y1"], t * SB)
                    sp.dma_start(x_t[:, :, :], d["x"][bass.ds(t * SB * P, SB * P), :]
                                 .rearrange("(j p) c -> p j c", p=P)).then_inc(x_in, 16)

                def second(t):
                    for j in range(SB):
                        n = t * SB + j
                        sp.wait_ge(s["ln"], (2 * t + 1) * SB + j + 1)
                        sp.dma_start(d["z_table"][bass.ds(n * P, P), :], ln[:, 1, j, :]).then_inc(z_out, 16)
                    if isinstance(t, int) and t == 0:
                        weights()

                rounds(sp, first, second)
                sp.wait_ge(z_out, 16 * BLOCKS)
                sp.wait_ge(core.w_in, 64)

            @block.gpsimd
            def _(pool):
                pool.wait_ge(par_in, 16 * (4 + 2 * KC))

                def first(t):
                    for j in range(SB):
                        n = t * SB + j
                        pool.wait_ge(s["inv_l"], t + 1)
                        need(pool, s["o_tp"], t * SB)
                        pool.tensor_tensor(
                            o[:, j, :].rearrange("p (h k) -> p h k", k=DH),
                            y1_at(n).rearrange("p (h k) -> p h k", k=DH),
                            inv_l[:, 1, j, :].unsqueeze(2).to_broadcast([P, HEADS, DH]), ALU.mult).then_inc(s["o"], 1)
                    for j in range(SB):
                        pool.wait_ge(x_in, 16 * (t + 1))
                        pool.tensor_tensor(x_t[:, j, :], x_t[:, j, :], b_ff[:, :], ALU.add).then_inc(s["xb"], 1)

                rounds(pool, first, lambda t: None)

            @block.vector
            def _(dve):
                dve.wait_ge(par_in, 16 * (4 + 2 * KC))


                def inverses(t):
                    sums = core.acc[:, bass.ds(t * SB * W, SB * W)].rearrange("p (j w) -> p j w", w=W)[:, :, 0:HEADS]
                    need(dve, s["o"], t * SB)
                    dve.tensor_scalar(inv_l[:, 0, :, :], sums, 1e-30, None, ALU.max).then_inc(s["lmax"], 1)
                    dve.wait_ge(s["lmax"], t + 1)
                    dve.reciprocal(inv_l[:, 1, :, :], inv_l[:, 0, :, :]).then_inc(s["inv_l"], 1)

                def outputs(t):
                    for j in range(SB):
                        n = t * SB + j
                        dve.wait_ge(s["yp"], n + 1)
                        dve.wait_ge(s["xb"], n + 1)
                        dve.wait_ge(s["o"], n + 1)
                        dve.tensor_tensor(y1_at(n), yp[j % 2][:, 0:D], x_t[:, j, :], ALU.add).then_inc(s["y1"], 1)

                def layernorm(t, r):
                    for j in range(SB):
                        n = t * SB + j
                        if r == 0:
                            dve.wait_ge(s["y1"], n + 1)
                        else:
                            dve.wait_ge(s["ln"], 2 * t * SB + j + 1)
                        wait_here(dve, core)
                        dve.bn_stats(stats[:, r, j, :], ln[:, 0, j, :] if r else y1_at(n)).then_inc(s["stats"], 1)
                    for j in range(SB):
                        dve.wait_ge(s["stats"], (2 * t + r) * SB + j + 1)
                        wait_here(dve, core)
                        dve.bn_aggr(mv[:, r, j, :], stats[:, r, j, :]).then_inc(s["mv"], 1)
                    dve.wait_ge(s["std"], 2 * t + r + 1)
                    dve.reciprocal(rstd[:, r, :], std[:, r, :]).then_inc(s["rstd"], 1)
                    dve.wait_ge(s["rstd"], 2 * t + r + 1)
                    if r == 1:
                        need(dve, s["z_tp"], t * SB)
                        need(dve, z_out, 16 * SB * t)
                    for j in range(SB):
                        wait_here(dve, core)
                        dve.tensor_scalar(ln[:, r, j, :], ln[:, 0, j, :] if r else y1_at(t * SB + j),
                                          mv[:, r, j, 0:1], rstd[:, r, j:j + 1], ALU.subtract,
                                          ALU.mult).then_inc(s["ln"], 1)

                def logits(t):
                    dve.wait_ge(s["lp"], (t + 1) * SB)
                    dve.tensor_tensor(core.logits[:, bass.ds(t * SB, SB), :],
                                      lp[:, 0:SB * EXPERTS].rearrange("p (j e) -> p j e", e=EXPERTS),
                                      br[:, :].unsqueeze(1).to_broadcast([P, SB, EXPERTS]), ALU.add
                                      ).then_inc(s["logits"], 1)

                def later(t, first=False, last=False, before_last=False):
                    layernorm(t, 0)
                    if not first:
                        logits(t - 1)
                    if not last:
                        outputs(t + 1)
                        if not before_last:
                            inverses(t + 2)
                    layernorm(t, 1)

                inverses(0)
                outputs(0)
                inverses(1)
                overlapped(dve, later)
                logits(ST - 1)

            @block.scalar
            def _(act):
                act.wait_ge(par_in, 16 * (4 + 2 * KC))

                def turned_outputs(t):
                    for j in range(SB):
                        n = t * SB + j
                        act.wait_ge(s["o_tp"], n + 1)
                        need(act, s["yp"], t * SB)
                        act.copy(oT[:, j, :, :], o_tp[j % 2][:, :, 0:P]).then_inc(s["oT"], 1)

                def roots(t, r):
                    act.wait_ge(s["mv"], (2 * t + r + 1) * SB)
                    need(act, s["rstd"], 2 * t + r - 1)
                    act.activation(std[:, r, :], mv[:, r, :, 1], ACT.Sqrt, bias=core.eps[:, :]).then_inc(s["std"], 1)

                def turned_rows(t):
                    for j in range(SB):
                        n = t * SB + j
                        act.wait_ge(s["z_tp"], n + 1)
                        need(act, s["lp"], t * SB)
                        for k in range(KC):
                            ins = act.activation(xnT[:, j, k, :], z_tp[j % 2][:, k, 0:P], ACT.Identity,
                                                 scale=core.gamma[:, k:k + 1], bias=core.beta[:, k:k + 1])
                        ins.then_inc(s["xnT"], 1)

                def later(t, first=False, last=False, before_last=False):
                    if not first:
                        turned_rows(t - 1)
                    roots(t, 0)
                    if not last:
                        turned_outputs(t + 1)
                    roots(t, 1)

                turned_outputs(0)
                overlapped(act, later)
                turned_rows(ST - 1)

            @block.tensor
            def _(pe):
                pe.wait_ge(par_in, 16 * (4 + 2 * KC))

                def project(t):
                    for j in range(SB):
                        n = t * SB + j
                        pe.wait_ge(s["o"], n + 1)
                        free_slot(pe, s["oT"], n, j)
                        for k in range(KC):
                            mm = pe.transpose(o_tp[j % 2][:, k, 0:P], o[:, j, k * P:(k + 1) * P], core.ident[:, :])
                        mm.then_inc(s["o_tp"], 1)
                    for j in range(SB):
                        n = t * SB + j
                        pe.wait_ge(s["oT"], n + 1)
                        free_slot(pe, s["y1"], n, j)
                        for k in range(KC):
                            mm = pe.matmul(yp[j % 2][:, 0:D], oT[:, j, k, :], wffT[:, k, :], start=(k == 0),
                                           stop=(k == KC - 1))
                        mm.then_inc(s["yp"], 1)

                def route(t):
                    for j in range(SB):
                        n = t * SB + j
                        pe.wait_ge(s["ln"], (2 * t + 1) * SB + j + 1)
                        free_slot(pe, s["xnT"], n, j)
                        for k in range(KC):
                            mm = pe.transpose(z_tp[j % 2][:, k, 0:P], ln[:, 1, j, k * P:(k + 1) * P],
                                              core.ident[:, :])
                        mm.then_inc(s["z_tp"], 1)
                    for j in range(SB):
                        n = t * SB + j
                        pe.wait_ge(s["xnT"], n + 1)
                        need(pe, s["logits"], t)
                        for k in range(KC):
                            mm = pe.matmul(lp[:, j * EXPERTS:(j + 1) * EXPERTS], xnT[:, j, k, :], wr[:, k, :], start=(k == 0),
                                           stop=(k == KC - 1))
                        mm.then_inc(s["lp"], 1)

                def later(t, first=False, last=False, before_last=False):
                    if not first:
                        route(t - 1)
                    if not last:
                        project(t + 1)

                project(0)
                overlapped(pe, later)
                route(ST - 1)



def phase_gate(nc, core, d):
    NE, COLS = BLOCKS * EXPERTS, SB * TOP
    with ExitStack() as st:
        sb, ps = tensors(nc, st)
        iota = sb("g_iota", [P, EXPERTS], I32)
        diag = sb("g_diag", [P, P], I32)
        node = sb("g_node", [P, BLOCKS], I32)
        before = sb("g_before", [P, P], BF16)
        ones = sb("g_ones", [P, P], BF16)
        rank = sb("g_rank", [P, EXPERTS], F32)
        key = sb("g_key", [P, BLOCKS, EXPERTS], F32)
        left = sb("g_left", [P, BLOCKS, EXPERTS], F32)
        mask = sb("g_mask", [P, 2, BLOCKS, EXPERTS], F32)
        gate = sb("g_gate", [P, BLOCKS, EXPERTS], F32)
        top = sb("g_top", [P, 2, BLOCKS], F32)
        best = sb("g_best", [P, BLOCKS], F32)
        diff = sb("g_diff", [P, BLOCKS], F32)
        e2 = sb("g_e2", [P, BLOCKS], F32)
        part = sb("g_part", [P, 2, BLOCKS], F32)
        either = sb("g_either", [P, BLOCKS, EXPERTS], BF16)
        keep = sb("g_keep", [P, EXPERTS, BLOCKS], F32)
        total = sb("g_total", [P, EXPERTS, BLOCKS], F32)
        upto = sb("g_upto", [P, EXPERTS, BLOCKS], F32)
        pos = sb("g_pos", [P, BLOCKS, EXPERTS], F32)
        count_i = sb("g_count_i", [P, 2, EXPERTS], I32)
        pairs = sb("g_pairs", [P, 3, EXPERTS], F32)
        place = sb("g_place", [P, BLOCKS, TOP], F32)
        place_i = sb("g_place_i", [P, 2, BLOCKS, TOP], I32)
        column = sb("g_column", [P, BLOCKS, TOP], F32)
        empty = sb("g_empty", [P, PLACES, 2], I32)
        place_now = sb("g_place_now", [P, COLS], I32)
        record_now = sb("g_record_now", [P, COLS, 2], I32)
        w_now = sb("g_w_now", [P, SB, EXPERTS], F32)
        wT = sb("g_wT", [EXPERTS, SB, P], F32)
        tp = [ps(f"g_tp{i}", [P, 512], F32) for i in range(2)]
        bp = [ps(f"g_bp{i}", [P, 512], F32) for i in range(2)]
        b1_tp = ps("g_b1_tp", [P, 512], F32)
        before_ps = ps("g_before_ps", [P, 512], F32)
        total_ps = ps("g_total_ps", [P, 512], F32)
        iota_done, chain, diff_done, e2_done, w_now_done, tp_done, wT_done, bp_done, y_done, b1_done = (
            core.sem("g_" + n) for n in ("iota", "chain", "diff", "e2", "w_now", "tp", "wT", "bp", "y", "b1"))
        either_done, sums_done, empty_done, out_done, place_done, staged, scattered = (
            core.sem("g_" + n) for n in ("either", "sums", "empty", "out", "place", "staged", "scattered"))

        def over_experts(a):
            return a.unsqueeze(2).to_broadcast([P, BLOCKS, EXPERTS])

        def in_rounds(eng, body):
            body(0)
            with eng.Fori(0, ST - 1) as i:
                body(i + 1)

        with nc.Block() as block:
            @block.gpsimd
            def _(pool):
                pool.iota(iota[:, :], pattern=[[-1, EXPERTS]], base=EXPERTS, channel_multiplier=0
                          ).then_inc(iota_done, 1)
                pool.iota(diag[:, :], pattern=[[1, P]], base=0, channel_multiplier=-1).then_inc(iota_done, 1)
                pool.iota(node[:, :], pattern=[[P, BLOCKS]], base=0, channel_multiplier=1).then_inc(iota_done, 1)
                last_row = pool.to_reg(P * PLACES - 1)
                pool.wait_ge(out_done, 16)
                pool.wait_ge(place_done, 1)

                def dispatch(t):
                    need(pool, scattered, 16 * COLS * t)
                    wait_here(pool, core)
                    pool.tensor_copy(place_now[:, :],
                                     core.place[:, bass.ds(t * SB, SB), :].rearrange("p b r -> p (b r)"))
                    pool.tensor_copy(record_now[:, :, :], core.record[:, bass.ds(t * SB, SB), :, :]
                                     .rearrange("p b r k -> p (b r) k")).then_inc(staged, 1)
                    pool.wait_ge(staged, t + 1)
                    wait_here(pool, core)
                    for k in range(COLS):
                        pool.indirect_dma_start(d["place_table"],
                                                bass.IndirectOffsetOnAxis(ap=place_now[:, k:k + 1], axis=0),
                                                record_now[:, k, :], None, bounds_check=last_row,
                                                oob_is_err=False).then_inc(scattered, 16)

                in_rounds(pool, dispatch)
                pool.wait_ge(scattered, 16 * COLS * ST)

            @block.sync
            def _(sp):
                sp.wait_ge(empty_done, 1)
                sp.dma_start(d["place_table"].rearrange("(p c) k -> p c k", p=P), empty[:, :, :]
                             ).then_inc(out_done, 16)
                sp.wait_ge(out_done, 16)

                def outputs(t):
                    sp.wait_ge(y_done, (t + 1) * SB)
                    sp.dma_start(d["out"][bass.ds(t * SB * P, SB * P), :].rearrange("(j p) c -> p j c", p=P),
                                 core.acc[:, bass.ds(t * SB * W, SB * W)]
                                 .rearrange("p (j w) -> p j w", w=W)[:, :, HEADS:W]).then_inc(out_done, 16)

                with sp.Fori(0, ST) as t:
                    outputs(t)
                sp.wait_ge(out_done, 16 * (ST + 1))

            @block.scalar
            def _(act):
                act.wait_ge(b1_done, 1)
                act.copy(core.b1[:, :], b1_tp[:, 0:EXPERTS * HC])
                act.wait_ge(diff_done, 1)
                act.activation(e2[:, :], diff[:, :], ACT.Exp).then_inc(e2_done, 1)

                def body(t):
                    for j in range(SB):
                        n = t * SB + j
                        act.wait_ge(tp_done, n + 1)
                        need(act, bp_done, t * SB)
                        act.copy(wT[:, j, :], tp[j % 2][0:EXPERTS, 0:P]).then_inc(wT_done, 1)

                in_rounds(act, body)

            @block.tensor
            def _(pe):
                pe.transpose(b1_tp[:, 0:EXPERTS * HC], core.b1_rows[:, :],
                             core.ident[0:EXPERTS * HC, 0:EXPERTS * HC]).then_inc(b1_done, 1)
                pe.wait_ge(either_done, 1)
                flat = either[:, :, :].rearrange("p b e -> p (b e)")
                pe.matmul(before_ps[:, 0:NE], before[:, :], flat, start=True, stop=True)
                pe.matmul(total_ps[:, 0:NE], ones[:, :], flat, start=True, stop=True).then_inc(sums_done, 1)

                def body(t):
                    for j in range(SB):
                        n = t * SB + j
                        pe.wait_ge(w_now_done, t + 1)
                        need(pe, wT_done, n if j == 0 else n - 1)
                        pe.transpose(tp[j % 2][0:EXPERTS, 0:P], w_now[:, j, :], core.ident[:, :]
                                     ).then_inc(tp_done, 1)
                    for j in range(SB):
                        n = t * SB + j
                        pe.wait_ge(wT_done, n + 1)
                        need(pe, y_done, n if j == 0 else n - 1)
                        pe.matmul(bp[j % 2][:, 0:D], wT[:, j, :], core.b2[:, :], start=True, stop=True
                                  ).then_inc(bp_done, 1)

                in_rounds(pe, body)

            @block.vector
            def _(dve):
                done = [0]

                def then(ins):
                    done[0] += 1
                    ins.then_inc(chain, 1)
                    dve.wait_ge(chain, done[0])

                dve.memset(empty[:, :, 1:2], 0)
                dve.memset(empty[:, :, 0:1], NOWHERE).then_inc(empty_done, 1)
                dve.memset(keep[:, :, 1:], 1.0)
                dve.memset(keep[:, :, 0:1], 0.0)
                dve.memset(ones[:, :], 1.0)
                dve.wait_ge(iota_done, 3)
                dve.tensor_scalar(before[:, :], diag[:, :], 0.0, None, ALU.is_gt)
                then(dve.tensor_copy(rank[:, :], iota[:, :]))
                for r in range(2):
                    source = left if r else core.logits
                    then(dve.tensor_reduce(top[:, r, :], source[:, :, :], X, ALU.max))
                    then(dve.tensor_tensor(key[:, :, :], source[:, :, :], over_experts(top[:, r, :]), ALU.is_equal))
                    then(dve.tensor_tensor(key[:, :, :], key[:, :, :],
                                           rank[:, :].unsqueeze(1).to_broadcast([P, BLOCKS, EXPERTS]), ALU.mult))
                    then(dve.tensor_reduce(best[:, :], key[:, :, :], X, ALU.max))
                    then(dve.tensor_tensor(mask[:, r, :, :], key[:, :, :], over_experts(best[:, :]), ALU.is_equal))
                    if r == 0:
                        then(dve.scalar_tensor_tensor(out=left[:, :, :], in0=mask[:, 0, :, :], scalar=-BIG,
                                                      in1=core.logits[:, :, :], op0=ALU.mult, op1=ALU.add))
                dve.tensor_tensor(diff[:, :], top[:, 1, :], top[:, 0, :], ALU.subtract).then_inc(diff_done, 1)
                dve.tensor_tensor(either[:, :, :], mask[:, 0, :, :], mask[:, 1, :, :], ALU.add
                                  ).then_inc(either_done, 1)
                dve.wait_ge(e2_done, 1)
                then(dve.tensor_scalar(best[:, :], e2[:, :], 1.0, None, ALU.add))
                then(dve.reciprocal(part[:, 0, :], best[:, :]))
                then(dve.tensor_tensor(part[:, 1, :], e2[:, :], part[:, 0, :], ALU.mult))
                dve.tensor_tensor(key[:, :, :], mask[:, 0, :, :], over_experts(part[:, 0, :]), ALU.mult)
                then(dve.tensor_tensor(left[:, :, :], mask[:, 1, :, :], over_experts(part[:, 1, :]), ALU.mult))
                then(dve.tensor_tensor(gate[:, :, :], key[:, :, :], left[:, :, :], ALU.add))
                for r in range(TOP):
                    dve.tensor_copy(core.record[:, :, r, 0], node[:, :])
                    dve.tensor_copy(core.record[:, :, r, 1].bitcast(F32), part[:, r, :])
                dve.wait_ge(sums_done, 1)
                then(dve.tensor_copy(total[:, :, :], total_ps[:, 0:NE].rearrange("p (b e) -> p e b", e=EXPERTS)))
                then(dve.tensor_tensor_scan(upto[:, :, :].rearrange("p e b -> p (e b)"),
                                            keep[:, :, :].rearrange("p e b -> p (e b)"),
                                            total[:, :, :].rearrange("p e b -> p (e b)"), 0.0, ALU.mult, ALU.add))
                then(dve.tensor_scalar(count_i[:, 0, :], upto[:, :, BLOCKS - 1], float(PAIR - 1), None, ALU.add))
                then(dve.tensor_scalar(count_i[:, 1, :], count_i[:, 0, :], PAIR.bit_length() - 1, None,
                                       ALU.arith_shift_right))
                then(dve.tensor_scalar(pairs[:, 0, :], count_i[:, 1, :], 1.0, None, ALU.max))
                then(dve.tensor_tensor_scan(pairs[:, 1, :], keep[:, 0, 1:EXPERTS + 1], pairs[:, 0, :], 0.0, ALU.mult,
                                            ALU.add))
                dve.memset(core.pair_bounds[:, 0:1], 0)
                dve.memset(core.pair_bounds[:, EXPERTS:], PAIRS)
                dve.tensor_copy(core.pair_bounds[:, 1:EXPERTS], pairs[:, 1, 0:EXPERTS - 1])
                then(dve.tensor_tensor(pairs[:, 2, :], pairs[:, 1, :], pairs[:, 0, :], ALU.subtract))
                then(dve.tensor_scalar(pairs[:, 2, :], pairs[:, 2, :], float(PAIR), None, ALU.mult))
                then(dve.tensor_tensor(upto[:, :, :], upto[:, :, :], total[:, :, :], ALU.subtract))
                then(dve.tensor_tensor(upto[:, :, :], upto[:, :, :],
                                       pairs[:, 2, :].unsqueeze(2).to_broadcast([P, EXPERTS, BLOCKS]), ALU.add))
                then(dve.tensor_tensor(pos[:, :, :], before_ps[:, 0:NE].rearrange("p (b e) -> p b e", e=EXPERTS),
                                       upto[:, :, :].rearrange("p e b -> p b e"), ALU.add))
                for r in range(TOP):
                    then(dve.tensor_tensor(key[:, :, :], mask[:, r, :, :], pos[:, :, :], ALU.mult))
                    then(dve.tensor_reduce(place[:, :, r], key[:, :, :], X, ALU.add))
                then(dve.tensor_copy(place_i[:, 0, :, :], place[:, :, :]))
                then(dve.tensor_scalar(place_i[:, 1, :, :], place_i[:, 0, :, :], P.bit_length() - 1, None,
                                       ALU.arith_shift_right))
                then(dve.tensor_scalar(column[:, :, :], place_i[:, 1, :, :], -float(P * PLACES - 1), None, ALU.mult))
                dve.scalar_tensor_tensor(out=core.place[:, :, :], in0=place[:, :, :], scalar=float(PLACES),
                                         in1=column[:, :, :], op0=ALU.mult, op1=ALU.add).then_inc(place_done, 1)

                def body(t):
                    need(dve, tp_done, t * SB)
                    dve.tensor_copy(w_now[:, :, :], gate[:, bass.ds(t * SB, SB), :]).then_inc(w_now_done, 1)
                    for j in range(SB):
                        n = t * SB + j
                        dve.wait_ge(bp_done, n + 1)
                        y = core.acc[:, bass.ds(n * W + HEADS, D)]
                        dve.tensor_tensor(y, bp[j % 2][:, 0:D], y, ALU.add).then_inc(y_done, 1)

                in_rounds(dve, body)


def phase_experts(nc, core, d):
    with ExitStack() as st:
        sb, ps = tensors(nc, st)
        places = sb("e_places", [P, PLACES, 2], I32)
        node_in = sb("e_node_in", [P, 2, 2], I32)
        node_out = sb("e_node_out", [P, 2, 2], I32)
        rows = sb("e_rows", [P, 2, D], F32)
        xnT = sb("e_xnT", [P, KC, PAIR], F32)
        hT = sb("e_hT", [P, HC, PAIR], F32)
        y = sb("e_y", [P, 2, 2, D], F32)
        tp = ps("e_tp", [P, KC, PAIR], F32)
        hp = [ps(f"e_hp{i}", [P, 512], F32) for i in range(HC)]
        yp = [ps(f"e_yp{i}", [P, 512], F32) for i in range(2)]
        places_in, rows_in, zeroed, staged_in, staged_out, tp_done, xnT_done, hp_done, gelu_done, yp_done, y_done, added = (
            core.sem("e_" + n) for n in ("places_in", "rows_in", "zeroed", "staged_in", "staged_out", "tp", "xnT", "hp",
                                         "gelu", "yp", "y", "added"))
        with nc.Block() as block:
            @block.sync
            def _(sp):
                sp.dma_start(places[:, :, :], d["place_table"].rearrange("(p c) k -> p c k", p=P)
                             ).then_inc(places_in, 16)
                sp.wait_ge(places_in, 16)

            @block.gpsimd
            def _(pool):
                last_node = pool.to_reg(ROWS - 1)
                pool.memset(rows[:, :, :], 0.0).then_inc(zeroed, 1)
                pool.wait_ge(zeroed, 1)
                pool.wait_ge(places_in, 16)

                def gather(at, B):
                    need(pool, rows_in, at(32))
                    need(pool, tp_done, at(1))
                    wait_here(pool, core)
                    first = 0 if B == PAIRS else at(2)
                    pool.tensor_copy(node_in[:, 0, :], places[:, bass.ds(first, 2), 0]).then_inc(staged_in, 1)
                    need(pool, staged_in, at(1, 1))
                    wait_here(pool, core)
                    for half in range(2):
                        pool.indirect_dma_start(rows[:, half, :], None, d["z_table"],
                                                bass.IndirectOffsetOnAxis(ap=node_in[:, 0, half:half + 1], axis=0),
                                                bounds_check=last_node, oob_is_err=False).then_inc(rows_in, 16)

                def add(at, c):
                    need(pool, added, at(32, -96))
                    wait_here(pool, core)
                    pool.tensor_copy(node_out[:, 0, :], places[:, bass.ds(at(2, -6), 2), 0]).then_inc(staged_out, 1)
                    need(pool, staged_out, at(1, -2))
                    need(pool, y_done, at(2, -2))
                    wait_here(pool, core)
                    for half in range(2):
                        pool.indirect_dma_start(d["out"],
                                                bass.IndirectOffsetOnAxis(ap=node_out[:, 0, half:half + 1], axis=0),
                                                y[:, 1 - c, half, :], None, bounds_check=last_node, oob_is_err=False,
                                                compute_op=ALU.add).then_inc(added, 16)

                def pair(at, rounds, c, B):
                    if B is None or B <= PAIRS:
                        gather(at, B)
                    if B is None or B >= 3:
                        add(at, c)

                batches(pool, pair, PAIRS, 3, before=4)
                pool.wait_ge(added, 32 * PAIRS)

            @block.vector
            def _(dve):
                dve.sem_inc(y_done, 2)
                dve.wait_ge(places_in, 16)

                def turn(at):
                    need(dve, tp_done, at(1, 2))
                    need(dve, hp_done, at(HC, HC))
                    for k in range(KC):
                        ins = dve.tensor_scalar(xnT[:, k, :], tp[:, k, :], core.gamma[:, k:k + 1],
                                                core.beta[:, k:k + 1], ALU.mult, ALU.add)
                    ins.then_inc(xnT_done, 1)

                def pair(at, rounds, c, B):
                    if B != PAIRS - 1:
                        turn(at)
                    for half in range(2):
                        need(dve, yp_done, at(2, half + 2))
                        need(dve, added, at(32, -32))
                        wait_here(dve, core)
                        weight = places[:, bass.ds(at(2, half), 1), 1].bitcast(F32)
                        dve.tensor_scalar(y[:, c, half, :], yp[half][:, 0:D], weight, None, ALU.mult
                                          ).then_inc(y_done, 1)

                turn(lambda k, off=0: -k + off)
                batches(dve, pair, PAIRS, 0)

            @block.tensor
            def _(pe):
                pe.sem_inc(yp_done, 1)

                def turn(T):
                    need(pe, rows_in, (T + 1) * 32)
                    need(pe, xnT_done, T)
                    for half in range(2):
                        for k in range(KC):
                            mm = pe.transpose(tp[:, k, half * P:(half + 1) * P], rows[:, half, k * P:(k + 1) * P],
                                              core.ident[:, :])
                    mm.then_inc(tp_done, 1)

                turn(0)
                for e in range(EXPERTS):
                    lo = pe.value_load(core.pair_bounds[0:1, e:e + 1], min_val=0, max_val=PAIRS - 1)
                    hi = pe.value_load(core.pair_bounds[0:1, e + 1:e + 2], min_val=1, max_val=PAIRS)
                    with pe.Fori(lo, hi) as T:
                        turn(T + 1)
                        pe.wait_ge(xnT_done, T + 1)
                        for c in range(HC):
                            pe.wait_ge(gelu_done, T * HC + c + 1)
                            for k in range(KC):
                                mm = pe.matmul(hp[c][:, 0:PAIR], core.w1[:, e, k, c * P:(c + 1) * P], xnT[:, k, :],
                                               start=(k == 0), stop=(k == KC - 1))
                            mm.then_inc(hp_done, 1)
                        for half in range(2):
                            pe.wait_ge(y_done, T * 2 + half + 1)
                            for c in range(HC):
                                if half == 0:
                                    pe.wait_ge(gelu_done, T * HC + c + 1 + HC)
                                mm = pe.matmul(yp[half][:, 0:D], hT[:, c, half * P:(half + 1) * P],
                                               core.w2[:, e, c, :], start=(c == 0), stop=(c == HC - 1))
                            mm.then_inc(yp_done, 1)

            @block.scalar
            def _(act):
                act.sem_inc(gelu_done, HC)
                for e in range(EXPERTS):
                    lo = act.value_load(core.pair_bounds[0:1, e:e + 1], min_val=0, max_val=PAIRS - 1)
                    hi = act.value_load(core.pair_bounds[0:1, e + 1:e + 2], min_val=1, max_val=PAIRS)
                    with act.Fori(lo, hi) as T:
                        for c in range(HC):
                            act.wait_ge(hp_done, T * HC + c + 1)
                            if c == 0:
                                act.wait_ge(yp_done, T * 2 + 1)
                            act.activation(hT[:, c, :], hp[c][:, 0:PAIR], ACT.Gelu,
                                           bias=core.b1[:, e * HC + c:e * HC + c + 1]).then_inc(gelu_done, 1)


def build(nc, d):
    with ExitStack() as st:
        core = Core(nc, st)
        sb, ps = tensors(nc, st)
        core.ident = sb("ident", [P, P], F32)
        core.ident_bf = sb("ident_bf", [P, P], BF16)
        core.iota_bf = sb("iota_bf", [P, P], BF16)
        core.ones = sb("ones", [P, P], F32)
        core.eps = sb("eps", [P, 1], F32)
        core.w_in = core.sem("w_in")
        core.waited = core.sem("waited")
        core.acc = sb("acc", [P, BLOCKS * W], F32)
        with ExitStack() as edge_life:
            sbe, _ = tensors(nc, edge_life)
            core.q_parts = sbe("q_parts", [P, BLOCKS * 3 * D], BF16)
            core.block_of = sbe("block_of", [1, GROUPS], I32)
            with ExitStack() as w_life:
                sbw, _ = tensors(nc, w_life)
                core.wqkvT = sbw("wqkvT", [P, KC, 3 * D], F32)
                core.b_qkv = sbw("b_qkv", [P, 3 * D], F32)
                phase_constants(nc, core, d)
                phase_project(nc, core, d)
            phase_route(nc, core, d)
            phase_attention(nc, core, d)
        core.w1 = sb("w1", [P, EXPERTS, KC, HID], F32)
        core.w2 = sb("w2", [P, EXPERTS, HC, D], F32)
        core.b1 = sb("b1", [P, EXPERTS * HC], F32)
        core.gamma = sb("gamma", [P, KC], F32)
        core.beta = sb("beta", [P, KC], F32)
        core.pair_bounds = sb("pair_bounds", [P, EXPERTS + 1], I32)
        with ExitStack() as gate_life:
            sbg, _ = tensors(nc, gate_life)
            core.logits = sbg("logits", [P, BLOCKS, EXPERTS], F32)
            core.b2 = sbg("b2", [EXPERTS, D], F32)
            core.b1_rows = sbg("b1_rows", [EXPERTS * HC, P], F32)
            core.record = sbg("record", [P, BLOCKS, TOP, 2], I32)
            core.place = sbg("place", [P, BLOCKS, TOP], I32)
            phase_node(nc, core, d)
            phase_gate(nc, core, d)
        phase_experts(nc, core, d)


def dram_tables(nc, d):
    for name, shape, dt in (("kv_table", (ROWS, 2 * D), F32), ("z_table", (ROWS, D), F32),
                            ("place_table", (P * PLACES, 2), I32), ("ends_table", (VPAD + 1, 3), F32),
                            ("begins_table", (VPAD, P + 1), F32), ("row_table", (BATCHES, ROWTAB), F32),
                            ("wff_table", (P, KC, D), F32), ("block_table", (VPAD,), I32), ("meta_table", (P, HOLD * 2 * BATCH), I32)):
        d[name] = nc.dram_tensor(name, shape, dt).ap()


_WEIGHTS = {"W_qkv": "L0_gnn_W_qkv", "b_qkv": "L0_gnn_b_qkv", "W_ff": "L0_gnn_W_ff", "b_ff": "L0_gnn_b_ff",
            "gamma": "L0_ffn_gamma", "beta": "L0_ffn_beta", "Wr": "L0_ffn_Wr", "br": "L0_ffn_br",
            "W1": "L0_ffn_W1", "b1": "L0_ffn_b1", "W2": "L0_ffn_W2", "b2": "L0_ffn_b2"}


def kernel(**inputs):
    import numpy as np
    import concourse.bacc as bacc
    from concourse.bass_utils import run_bass_kernel_spmd

    x = np.zeros((ROWS, D), np.float32)
    x[:NODES] = inputs["x"]
    edges = np.zeros((2, (TILES + 1) * P), np.int32)
    edges[1] = -1
    edges[0, :EDGES] = inputs["src"]
    edges[1, :EDGES] = inputs["dst"]
    edges = np.ascontiguousarray(edges.reshape(2, TILES + 1, P).transpose(1, 0, 2)).reshape(TILES + 1, 2 * P)
    arrays = {"x": x, "edges": edges}
    for name, given in _WEIGHTS.items():
        arrays[name] = np.ascontiguousarray(inputs[given])

    nc = bacc.Bacc("TRN2", target_bir_lowering=False, num_devices=1)
    d = {name: nc.dram_tensor("in_" + name, a.shape, mybir.dt.from_np(a.dtype), kind="ExternalInput").ap()
         for name, a in arrays.items()}
    dram_tables(nc, d)
    d["out"] = nc.dram_tensor("out", (ROWS, D), F32, kind="ExternalOutput").ap()
    build(nc, d)
    got = run_bass_kernel_spmd(nc, [{"in_" + name: a for name, a in arrays.items()}], core_ids=[0])
    return got.results[0]["out"][:NODES]
```
